# Optimizing a Trainium2 kernel written in Bass

```python
import numpy as np
import jax
import jax.numpy as jnp

def _softmax(x, axis=-1):
    return jax.nn.softmax(x, axis=axis)

def _gelu(x):
    return jax.nn.gelu(x, approximate=True)

def _silu(x):
    return jax.nn.silu(x)

def _sigmoid(x):
    return jax.nn.sigmoid(x)

def _layernorm(x, axis=-1, eps=1e-05):
    m = jnp.mean(x, axis=axis, keepdims=True)
    v = jnp.var(x, axis=axis, keepdims=True)
    return (x - m) / jnp.sqrt(v + eps)

def _scatter_add(tgt, idx, src, axis=0):
    return tgt.at[idx].add(src)

def _segment_sum(src, seg, n):
    return jax.ops.segment_sum(src, seg, n)
kernel_name = 'mk_gnn_preln_d4_gnn_r16_9fbf82'

def setup_inputs(seed: int=0):
    np.random.seed(seed)
    _w = jnp.asarray

    def _rec_inputs():
        import jax
        import jax.numpy as jnp
        _gk = jax.random.key(seed)
        x = -8.776e-05 + 1 * jax.random.normal(jax.random.fold_in(_gk, 1), (625, 512), jnp.float32)
        src = jax.random.randint(jax.random.fold_in(_gk, 2), (20000,), 0, 625, jnp.int32)
        dst = jnp.minimum((625 * jax.random.uniform(jax.random.fold_in(_gk, 3), (20000,)) ** 2.0).astype(jnp.int32), 9999)
        _o = jnp.argsort(dst, stable=True)
        src = src[_o]
        dst = dst[_o]
        edge_attr_3 = 0.000669165 + 0.999965 * jax.random.normal(jax.random.fold_in(_gk, 11), (20000, 3), jnp.float32)
        edge_attr_64 = 0.000279952 + 1.00013 * jax.random.normal(jax.random.fold_in(_gk, 12), (20000, 64), jnp.float32)
        node_vec1 = jax.random.uniform(jax.random.fold_in(_gk, 14), (625, 1), jnp.float32, 0.0, 0.999957)
        return (x, src, dst, edge_attr_3, edge_attr_64, node_vec1)
    x, src, dst, edge_attr_3, edge_attr_64, node_vec1 = _rec_inputs()

    def _L0_gnn_setup():
        import jax, jax.numpy as jnp
        import numpy as np
        N_NODES = 625
        key = jax.random.key(seed)
        k1, k2, k3, k4, k5 = jax.random.split(key, 5)
        x = jax.random.normal(k1, (N_NODES, 512), dtype=jnp.float32)
        edge_index = jax.random.randint(k2, (2, 10000), 0, N_NODES, dtype=jnp.int64)
        W_l = jax.random.normal(k3, (512, 512), dtype=jnp.float32) * 0.04
        b_l = jax.random.normal(k4, (512,), dtype=jnp.float32) * 0.04
        W_r = jax.random.normal(k5, (512, 512), dtype=jnp.float32) * 0.04
        return {'x': x, 'edge_index': edge_index, 'W_l': W_l, 'b_l': b_l, 'W_r': W_r}
    _L0_gnn_all = _L0_gnn_setup()
    _L0_gnn_in = {k: v for k, v in _L0_gnn_all.items() if k in ('W_l', 'b_l', 'W_r')}
    del _L0_gnn_all

    def _L1_gnn_setup():
        import jax, jax.numpy as jnp
        import numpy as np
        N_NODES = 40962
        LATENT_DIM = 512
        N_EDGES = 40962
        NUM_BLOCKS = 4
        NUM_HEADS = 4
        NUM_FREQ = 32
        BASE_PERIOD = 16
        NOISE_EMB_DIM = 16
        EPS = 1e-05

        def _cond_layer_norm(x, cond, sw, sb, bw, bb):
            mu = jnp.mean(x, axis=-1, keepdims=True)
            var = jnp.var(x, axis=-1, keepdims=True)
            xn = (x - mu) * jax.lax.rsqrt(var + EPS)
            scale = cond @ sw + sb
            bias = cond @ bw + bb
            return xn * (1.0 + scale) + bias

        def _sparse_attention(x, src, dst, wq, bq, wk, bk, wv, bv, wo, bo):
            N, D = x.shape
            H, Dh = (NUM_HEADS, D // NUM_HEADS)
            q = (x @ wq + bq).reshape(N, H, Dh) * Dh ** (-0.5)
            k = (x @ wk + bk).reshape(N, H, Dh)
            v = (x @ wv + bv).reshape(N, H, Dh)
            scores = jnp.einsum('ehd,ehd->eh', q[src], k[dst])
            smax = jax.ops.segment_max(scores, src, num_segments=N)
            ex = jnp.exp(scores - smax[src])
            denom = jax.ops.segment_sum(ex, src, num_segments=N)
            attn = ex / denom[src]
            out = jax.ops.segment_sum(attn[:, :, None] * v[dst], src, num_segments=N)
            return out.reshape(N, D) @ wo + bo

        def _forward(x, edge_index, noise_levels, f_w1, f_b1, f_w2, f_b2, s1_w, s1_b, b1_w, b1_b, wq, bq, wk, bk, wv, bv, wo, bo, s2_w, s2_b, b2_w, b2_b, m_w1, m_b1, m_w2, m_b2):
            src, dst = (edge_index[0], edge_index[1])
            freqs = jnp.arange(1, NUM_FREQ + 1, dtype=x.dtype) * (2.0 * np.pi / BASE_PERIOD)
            ph = noise_levels * freqs
            emb = jnp.concatenate([jnp.sin(ph), jnp.cos(ph)], axis=-1)
            cond = jax.nn.silu(emb @ f_w1 + f_b1) @ f_w2 + f_b2
            for i in range(NUM_BLOCKS):
                y = _cond_layer_norm(x, cond, s1_w[i], s1_b[i], b1_w[i], b1_b[i])
                y = _sparse_attention(y, src, dst, wq[i], bq[i], wk[i], bk[i], wv[i], bv[i], wo[i], bo[i])
                x = x + y
                y = _cond_layer_norm(x, cond, s2_w[i], s2_b[i], b2_w[i], b2_b[i])
                y = jax.nn.relu(y @ m_w1[i] + m_b1[i]) @ m_w2[i] + m_b2[i]
                x = x + y
            return x
        key = jax.random.key(seed)
        ks = jax.random.split(key, 20)

        def w(k, shape, s=0.02):
            return jax.random.normal(k, shape, dtype=jnp.float32) * s
        D, B, C = (LATENT_DIM, NUM_BLOCKS, NOISE_EMB_DIM)
        z = lambda *s: jnp.zeros(s, jnp.float32)
        return {'latent_mesh_nodes': jax.random.normal(ks[0], (N_NODES, D), dtype=jnp.float32), 'edge_index': jax.random.randint(ks[1], (2, N_EDGES), 0, N_NODES, dtype=jnp.int32), 'noise_levels': jax.random.uniform(ks[2], (N_NODES, 1), dtype=jnp.float32), 'f_w1': w(ks[3], (2 * NUM_FREQ, C)), 'f_b1': z(C), 'f_w2': w(ks[4], (C, C)), 'f_b2': z(C), 's1_w': w(ks[5], (B, C, D)), 's1_b': z(B, D), 'b1_w': w(ks[6], (B, C, D)), 'b1_b': z(B, D), 'wq': w(ks[7], (B, D, D)), 'bq': z(B, D), 'wk': w(ks[8], (B, D, D)), 'bk': z(B, D), 'wv': w(ks[9], (B, D, D)), 'bv': z(B, D), 'wo': w(ks[10], (B, D, D)), 'bo': z(B, D), 's2_w': w(ks[11], (B, C, D)), 's2_b': z(B, D), 'b2_w': w(ks[12], (B, C, D)), 'b2_b': z(B, D), 'm_w1': w(ks[13], (B, D, D)), 'm_b1': z(B, D), 'm_w2': w(ks[14], (B, D, D)), 'm_b2': z(B, D)}
    _L1_gnn_all = _L1_gnn_setup()
    _L1_gnn_in = {k: v for k, v in _L1_gnn_all.items() if k in ('f_w1', 'f_b1', 'f_w2', 'f_b2', 's1_w', 's1_b', 'b1_w', 'b1_b', 'wq', 'bq', 'wk', 'bk', 'wv', 'bv', 'wo', 'bo', 's2_w', 's2_b', 'b2_w', 'b2_b', 'm_w1', 'm_b1', 'm_w2', 'm_b2')}
    del _L1_gnn_all

    def _L2_gnn_setup():
        import jax, jax.numpy as jnp
        import numpy as np
        N = 3125
        E = 50000
        D_IN = 512
        D_OUT = 512
        EDGE_DIM = 3
        key = jax.random.key(seed)
        k = jax.random.split(key, 6)
        x = jax.random.normal(k[0], (N, D_IN), dtype=jnp.float32)
        edge_index = jax.random.randint(k[1], (2, E), 0, N, dtype=jnp.int64)
        edge_attr = jax.random.normal(k[2], (E, EDGE_DIM), dtype=jnp.float32)
        lim1 = (6.0 / (D_IN + D_OUT)) ** 0.5
        lin_w = jax.random.uniform(k[3], (D_OUT, D_IN), minval=-lim1, maxval=lim1, dtype=jnp.float32)
        lin_b = jnp.zeros((D_OUT,), dtype=jnp.float32)
        lim2 = (6.0 / (EDGE_DIM + 1)) ** 0.5
        conf_w = jax.random.uniform(k[4], (1, EDGE_DIM), minval=-lim2, maxval=lim2, dtype=jnp.float32)
        conf_b = jnp.zeros((1,), dtype=jnp.float32)
        return {'x': x, 'edge_index': edge_index, 'edge_attr': edge_attr, 'lin_w': lin_w, 'lin_b': lin_b, 'conf_w': conf_w, 'conf_b': conf_b}
    _L2_gnn_all = _L2_gnn_setup()
    _L2_gnn_in = {k: v for k, v in _L2_gnn_all.items() if k in ('lin_w', 'lin_b', 'conf_w', 'conf_b')}
    del _L2_gnn_all

    def _L3_gnn_setup():
        import jax, jax.numpy as jnp
        import numpy as np
        N_NODES = 1250
        N_EDGES = 20000
        HIDDEN = 512
        EDGE_DIM = 64
        LN_EPS = 1e-05

        def mish(x):
            return x * jnp.tanh(jax.nn.softplus(x))
        key = jax.random.key(seed)
        ks = jax.random.split(key, 8)
        s = lambda fan_in: 1.0 / np.sqrt(fan_in)
        return {'x': jax.random.normal(ks[0], (N_NODES, HIDDEN), dtype=jnp.float32), 'edge_index': jax.random.randint(ks[1], (2, N_EDGES), 0, N_NODES, dtype=jnp.int64), 'edge_attr': jax.random.normal(ks[2], (N_EDGES, EDGE_DIM), dtype=jnp.float32), 'W1': jax.random.normal(ks[3], (2 * HIDDEN + EDGE_DIM, HIDDEN), dtype=jnp.float32) * s(2 * HIDDEN + EDGE_DIM), 'b1': jnp.zeros((HIDDEN,), dtype=jnp.float32), 'W2': jax.random.normal(ks[4], (HIDDEN, HIDDEN), dtype=jnp.float32) * s(HIDDEN), 'b2': jnp.zeros((HIDDEN,), dtype=jnp.float32), 'W3': jax.random.normal(ks[5], (2 * HIDDEN, HIDDEN), dtype=jnp.float32) * s(2 * HIDDEN), 'b3': jnp.zeros((HIDDEN,), dtype=jnp.float32), 'W4': jax.random.normal(ks[6], (HIDDEN, HIDDEN), dtype=jnp.float32) * s(HIDDEN), 'b4': jnp.zeros((HIDDEN,), dtype=jnp.float32), 'gamma': jnp.ones((HIDDEN,), dtype=jnp.float32), 'beta': jnp.zeros((HIDDEN,), dtype=jnp.float32)}
    _L3_gnn_all = _L3_gnn_setup()
    _L3_gnn_in = {k: v for k, v in _L3_gnn_all.items() if k in ('W1', 'b1', 'W2', 'b2', 'W3', 'b3', 'W4', 'b4', 'gamma', 'beta')}
    del _L3_gnn_all
    return {'x': x, 'src': src, 'dst': dst, 'edge_attr_3': edge_attr_3, 'edge_attr_64': edge_attr_64, 'node_vec1': node_vec1, 'L0_gnn_W_l': _L0_gnn_in['W_l'], 'L0_gnn_b_l': _L0_gnn_in['b_l'], 'L0_gnn_W_r': _L0_gnn_in['W_r'], 'L1_gnn_f_w1': _L1_gnn_in['f_w1'], 'L1_gnn_f_b1': _L1_gnn_in['f_b1'], 'L1_gnn_f_w2': _L1_gnn_in['f_w2'], 'L1_gnn_f_b2': _L1_gnn_in['f_b2'], 'L1_gnn_s1_w': _L1_gnn_in['s1_w'], 'L1_gnn_s1_b': _L1_gnn_in['s1_b'], 'L1_gnn_b1_w': _L1_gnn_in['b1_w'], 'L1_gnn_b1_b': _L1_gnn_in['b1_b'], 'L1_gnn_wq': _L1_gnn_in['wq'], 'L1_gnn_bq': _L1_gnn_in['bq'], 'L1_gnn_wk': _L1_gnn_in['wk'], 'L1_gnn_bk': _L1_gnn_in['bk'], 'L1_gnn_wv': _L1_gnn_in['wv'], 'L1_gnn_bv': _L1_gnn_in['bv'], 'L1_gnn_wo': _L1_gnn_in['wo'], 'L1_gnn_bo': _L1_gnn_in['bo'], 'L1_gnn_s2_w': _L1_gnn_in['s2_w'], 'L1_gnn_s2_b': _L1_gnn_in['s2_b'], 'L1_gnn_b2_w': _L1_gnn_in['b2_w'], 'L1_gnn_b2_b': _L1_gnn_in['b2_b'], 'L1_gnn_m_w1': _L1_gnn_in['m_w1'], 'L1_gnn_m_b1': _L1_gnn_in['m_b1'], 'L1_gnn_m_w2': _L1_gnn_in['m_w2'], 'L1_gnn_m_b2': _L1_gnn_in['m_b2'], 'L2_gnn_lin_w': _L2_gnn_in['lin_w'], 'L2_gnn_lin_b': _L2_gnn_in['lin_b'], 'L2_gnn_conf_w': _L2_gnn_in['conf_w'], 'L2_gnn_conf_b': _L2_gnn_in['conf_b'], 'L3_gnn_W1': _L3_gnn_in['W1'], 'L3_gnn_b1': _L3_gnn_in['b1'], 'L3_gnn_W2': _L3_gnn_in['W2'], 'L3_gnn_b2': _L3_gnn_in['b2'], 'L3_gnn_W3': _L3_gnn_in['W3'], 'L3_gnn_b3': _L3_gnn_in['b3'], 'L3_gnn_W4': _L3_gnn_in['W4'], 'L3_gnn_b4': _L3_gnn_in['b4'], 'L3_gnn_gamma': _L3_gnn_in['gamma'], 'L3_gnn_beta': _L3_gnn_in['beta']}

def reference(x, src, dst, edge_attr_3, edge_attr_64, node_vec1, L0_gnn_W_l, L0_gnn_b_l, L0_gnn_W_r, L1_gnn_f_w1, L1_gnn_f_b1, L1_gnn_f_w2, L1_gnn_f_b2, L1_gnn_s1_w, L1_gnn_s1_b, L1_gnn_b1_w, L1_gnn_b1_b, L1_gnn_wq, L1_gnn_bq, L1_gnn_wk, L1_gnn_bk, L1_gnn_wv, L1_gnn_bv, L1_gnn_wo, L1_gnn_bo, L1_gnn_s2_w, L1_gnn_s2_b, L1_gnn_b2_w, L1_gnn_b2_b, L1_gnn_m_w1, L1_gnn_m_b1, L1_gnn_m_w2, L1_gnn_m_b2, L2_gnn_lin_w, L2_gnn_lin_b, L2_gnn_conf_w, L2_gnn_conf_b, L3_gnn_W1, L3_gnn_b1, L3_gnn_W2, L3_gnn_b2, L3_gnn_W3, L3_gnn_b3, L3_gnn_W4, L3_gnn_b4, L3_gnn_gamma, L3_gnn_beta):
    import jax
    import jax.numpy as jnp

    def _L0_gnn_ref(x, edge_index, W_l, b_l, W_r):
        import jax, jax.numpy as jnp
        import numpy as np
        N_NODES = 625
        src, dst = (edge_index[0], edge_index[1])
        n = x.shape[0]
        summed = jax.ops.segment_sum(x[src], dst, num_segments=n)
        deg = jax.ops.segment_sum(jnp.ones_like(src, dtype=x.dtype), dst, num_segments=n)
        agg = summed / jnp.maximum(deg, 1.0)[:, None]
        out = agg @ W_l.T + b_l + x @ W_r.T
        out = jax.nn.relu(out)
        return out

    def _L1_gnn_ref(latent_mesh_nodes, edge_index, noise_levels, f_w1, f_b1, f_w2, f_b2, s1_w, s1_b, b1_w, b1_b, wq, bq, wk, bk, wv, bv, wo, bo, s2_w, s2_b, b2_w, b2_b, m_w1, m_b1, m_w2, m_b2):
        import jax, jax.numpy as jnp
        import numpy as np
        N_NODES = 40962
        LATENT_DIM = 512
        N_EDGES = 40962
        NUM_BLOCKS = 4
        NUM_HEADS = 4
        NUM_FREQ = 32
        BASE_PERIOD = 16
        NOISE_EMB_DIM = 16
        EPS = 1e-05

        def _cond_layer_norm(x, cond, sw, sb, bw, bb):
            mu = jnp.mean(x, axis=-1, keepdims=True)
            var = jnp.var(x, axis=-1, keepdims=True)
            xn = (x - mu) * jax.lax.rsqrt(var + EPS)
            scale = cond @ sw + sb
            bias = cond @ bw + bb
            return xn * (1.0 + scale) + bias

        def _sparse_attention(x, src, dst, wq, bq, wk, bk, wv, bv, wo, bo):
            N, D = x.shape
            H, Dh = (NUM_HEADS, D // NUM_HEADS)
            q = (x @ wq + bq).reshape(N, H, Dh) * Dh ** (-0.5)
            k = (x @ wk + bk).reshape(N, H, Dh)
            v = (x @ wv + bv).reshape(N, H, Dh)
            scores = jnp.einsum('ehd,ehd->eh', q[src], k[dst])
            smax = jax.ops.segment_max(scores, src, num_segments=N)
            ex = jnp.exp(scores - smax[src])
            denom = jax.ops.segment_sum(ex, src, num_segments=N)
            attn = ex / denom[src]
            out = jax.ops.segment_sum(attn[:, :, None] * v[dst], src, num_segments=N)
            return out.reshape(N, D) @ wo + bo

        def _forward(x, edge_index, noise_levels, f_w1, f_b1, f_w2, f_b2, s1_w, s1_b, b1_w, b1_b, wq, bq, wk, bk, wv, bv, wo, bo, s2_w, s2_b, b2_w, b2_b, m_w1, m_b1, m_w2, m_b2):
            src, dst = (edge_index[0], edge_index[1])
            freqs = jnp.arange(1, NUM_FREQ + 1, dtype=x.dtype) * (2.0 * np.pi / BASE_PERIOD)
            ph = noise_levels * freqs
            emb = jnp.concatenate([jnp.sin(ph), jnp.cos(ph)], axis=-1)
            cond = jax.nn.silu(emb @ f_w1 + f_b1) @ f_w2 + f_b2
            for i in range(NUM_BLOCKS):
                y = _cond_layer_norm(x, cond, s1_w[i], s1_b[i], b1_w[i], b1_b[i])
                y = _sparse_attention(y, src, dst, wq[i], bq[i], wk[i], bk[i], wv[i], bv[i], wo[i], bo[i])
                x = x + y
                y = _cond_layer_norm(x, cond, s2_w[i], s2_b[i], b2_w[i], b2_b[i])
                y = jax.nn.relu(y @ m_w1[i] + m_b1[i]) @ m_w2[i] + m_b2[i]
                x = x + y
            return x
        return _forward(latent_mesh_nodes, edge_index, noise_levels, f_w1, f_b1, f_w2, f_b2, s1_w, s1_b, b1_w, b1_b, wq, bq, wk, bk, wv, bv, wo, bo, s2_w, s2_b, b2_w, b2_b, m_w1, m_b1, m_w2, m_b2)

    def _L2_gnn_ref(x, edge_index, edge_attr, lin_w, lin_b, conf_w, conf_b):
        import jax, jax.numpy as jnp
        import numpy as np
        N = 3125
        E = 50000
        D_IN = 512
        D_OUT = 512
        EDGE_DIM = 3
        row, col = (edge_index[0], edge_index[1])
        edge_weight = jax.nn.sigmoid(edge_attr @ conf_w.T + conf_b)[:, 0]
        deg = jnp.zeros((x.shape[0],), dtype=x.dtype).at[row].add(1.0)
        deg_safe = jnp.where(deg > 0, deg, 1.0)
        deg_inv_sqrt = jnp.where(deg > 0, jax.lax.rsqrt(deg_safe), 0.0)
        norm = deg_inv_sqrt[row] * deg_inv_sqrt[col] * edge_weight
        norm = jnp.where(jnp.isnan(norm), 0.0, norm)
        out = jnp.zeros_like(x).at[col].add(x[row] * norm[:, None])
        return out @ lin_w.T + lin_b

    def _L3_gnn_ref(x, edge_index, edge_attr, W1, b1, W2, b2, W3, b3, W4, b4, gamma, beta):
        import jax, jax.numpy as jnp
        import numpy as np
        N_NODES = 1250
        N_EDGES = 20000
        HIDDEN = 512
        EDGE_DIM = 64
        LN_EPS = 1e-05

        def mish(x):
            return x * jnp.tanh(jax.nn.softplus(x))
        src, dst = (edge_index[0], edge_index[1])
        edge_feat = jnp.concatenate([x[src], x[dst], edge_attr], axis=-1)
        h = mish(edge_feat @ W1 + b1)
        messages = mish(h @ W2 + b2)
        agg = jax.ops.segment_sum(messages, dst, num_segments=x.shape[0])
        u = mish(jnp.concatenate([x, agg], axis=-1) @ W3 + b3)
        out = u @ W4 + b4
        y = x + out
        mu = jnp.mean(y, axis=-1, keepdims=True)
        var = jnp.mean(jnp.square(y - mu), axis=-1, keepdims=True)
        return (y - mu) * jax.lax.rsqrt(var + LN_EPS) * gamma + beta
    edge_index = jnp.stack([src, dst])
    h = jnp.maximum(_layernorm(x, axis=-1), 0.0)
    x = x + _L0_gnn_ref(h, edge_index, L0_gnn_W_l, L0_gnn_b_l, L0_gnn_W_r)
    h = jnp.maximum(_layernorm(x, axis=-1), 0.0)
    x = x + _L1_gnn_ref(h, edge_index, node_vec1, L1_gnn_f_w1, L1_gnn_f_b1, L1_gnn_f_w2, L1_gnn_f_b2, L1_gnn_s1_w, L1_gnn_s1_b, L1_gnn_b1_w, L1_gnn_b1_b, L1_gnn_wq, L1_gnn_bq, L1_gnn_wk, L1_gnn_bk, L1_gnn_wv, L1_gnn_bv, L1_gnn_wo, L1_gnn_bo, L1_gnn_s2_w, L1_gnn_s2_b, L1_gnn_b2_w, L1_gnn_b2_b, L1_gnn_m_w1, L1_gnn_m_b1, L1_gnn_m_w2, L1_gnn_m_b2)
    h = jnp.maximum(_layernorm(x, axis=-1), 0.0)
    x = x + _L2_gnn_ref(h, edge_index, edge_attr_3, L2_gnn_lin_w, L2_gnn_lin_b, L2_gnn_conf_w, L2_gnn_conf_b)
    h = jnp.maximum(_layernorm(x, axis=-1), 0.0)
    x = x + _L3_gnn_ref(h, edge_index, edge_attr_64, L3_gnn_W1, L3_gnn_b1, L3_gnn_W2, L3_gnn_b2, L3_gnn_W3, L3_gnn_b3, L3_gnn_W4, L3_gnn_b4, L3_gnn_gamma, L3_gnn_beta)
    return x

_drawn_inputs = setup_inputs


def setup_inputs(seed=0):
    import zlib

    import numpy as np

    out = dict(_drawn_inputs(seed))
    spreads = {'L1_gnn_f_b1': (0.0, 0.8),
     'L1_gnn_f_b2': (0.0, 0.8),
     'L1_gnn_s1_b': (0.0, 0.755),
     'L1_gnn_b1_b': (0.0, 0.339),
     'L1_gnn_bq': (0.0, 0.8),
     'L1_gnn_bk': (0.0, 0.8),
     'L1_gnn_bv': (0.0, 0.1),
     'L1_gnn_bo': (0.0, 0.1),
     'L1_gnn_s2_b': (0.0, 0.515),
     'L1_gnn_b2_b': (0.0, 0.516),
     'L1_gnn_m_b1': (0.0, 0.1),
     'L1_gnn_m_b2': (0.0, 0.1),
     'L2_gnn_lin_b': (0.0, 0.1),
     'L3_gnn_b1': (0.0, 0.1),
     'L3_gnn_b2': (0.0, 0.1),
     'L3_gnn_b3': (0.0, 0.8),
     'L3_gnn_b4': (0.0, 0.621),
     'L3_gnn_gamma': (1.0, 0.2),
     'L3_gnn_beta': (0.0, 0.1)}
    factors = {'edge_attr_3': 3.093,
     'node_vec1': 8.0,
     'L1_gnn_f_w1': 8.0,
     'L1_gnn_f_w2': 8.0,
     'L1_gnn_s1_w': 8.0,
     'L1_gnn_b1_w': 8.0,
     'L1_gnn_wq': 7.842,
     'L1_gnn_wk': 7.64,
     'L1_gnn_s2_w': 8.0,
     'L1_gnn_b2_w': 8.0,
     'L2_gnn_conf_w': 2.961}
    for name, (base, spread) in spreads.items():
        noise = np.random.default_rng([zlib.crc32(name.encode()), seed]).standard_normal(out[name].shape)
        drawn = base * np.exp(spread * noise) if base else spread * noise
        out[name] = jnp.asarray(drawn.astype(out[name].dtype))
    for name, factor in factors.items():
        out[name] = (out[name] * factor).astype(out[name].dtype)
    return out
```

```python
from contextlib import ExitStack

import concourse.bass as bass
from concourse import mybir

F32, BF16, I32 = mybir.dt.float32, mybir.dt.bfloat16, mybir.dt.int32
F16 = mybir.dt.float16
ALU, ACT, AX = mybir.AluOpType, mybir.ActivationFunctionType, mybir.AxisListType

P = 128
NODES, D, EDGES = 625, 512, 20000
NT = -(-NODES // P)
NP = NT * P
HALF = NP // 2
KF = D // P
HEADS, DH = 4, 128
BLOCKS = 4
EMB, COND = 64, 16
CROWS = 33
TPG = 4
GROUP = TPG * P
GROUPS = -(-EDGES // GROUP)
TILES = GROUPS * TPG
WIN = 64
WIDE = NP + WIN
MAXSWEEPS = NP // WIN
EATTR = 64
EPS = 1e-5
NONE = -1.0e30
LOG_AND_EXP = "natural_log_exp_and_others"
CAP = 20.0


class Kernel:

    def __init__(self, dram):
        self.dram = dram


class Product:
    def __init__(self, n, by, c, before, bank):
        self.n, self.by, self.c, self.before, self.bank = n, by, c, before, bank


class Count:

    def __init__(self, eng, sem, start=0, it=None, per=0):
        self.eng, self.sem, self.n, self.it, self.per = eng, sem, start, it, per

    def at(self, n=None):
        n = self.n if n is None else n
        return n if self.it is None else self.it * self.per + n

    def __call__(self, ins):
        ins.then_inc(self.sem, 1)
        self.n += 1
        return self.n

    def wait(self, n=None):
        self.eng.wait_ge(self.sem, self.at(n))


class Plan:

    def __init__(self, product_ready, taken, rings):
        self.ready, self.taken, self.rings = product_ready, taken, rings
        self.at, self.used, self.count = {}, {r: [] for r in rings}, {e: 0 for e in taken}
        self.total = 0

    def add(self, key, by, ring="one"):
        self.total += 1
        self.count[by] += 1
        slots = self.rings[ring]
        used = self.used[ring]
        before = used[-len(slots)] if len(used) >= len(slots) else None
        used.append(key)
        self.at[key] = Product(n=self.total, by=by, c=self.count[by], before=before,
                                       bank=slots[(len(used) - 1) % len(slots)])

    def open(self, pe, key, it=None):
        g = self.at[key]
        if g.before is not None:
            self.need(pe, g.before, it)
        return g.bank

    def need(self, eng, key, it=None):
        g = self.at[key]
        eng.wait_ge(self.taken[g.by], g.c if it is None else it * self.count[g.by] + g.c)

    def made(self, ins):
        ins.then_inc(self.ready, 1)

    def take(self, eng, key, it=None):
        g = self.at[key]
        eng.wait_ge(self.ready, g.n if it is None else it * self.total + g.n)
        return g.bank

    def took(self, key, ins):
        ins.then_inc(self.taken[self.at[key].by], 1)


def scope(ctx, nc, tag):
    return (lambda name, shape, dt=F32: ctx.enter_context(nc.sbuf_tensor(f"{tag}_{name}", shape, dt)),
            lambda name, shape: ctx.enter_context(nc.psum_tensor(f"{tag}_{name}", shape, F32)),
            lambda name: ctx.enter_context(nc.semaphore(f"{tag}_{name}")))


def settle(k, eng):
    eng.sem_inc(k.settled, 1)


def cols(ap, n):
    return ap.rearrange("p (a b) -> p a b", b=n)


def edge_windows_and_matrices(nc, k):
    ctx = ExitStack()
    with ctx:
        sb, pb, sem = scope(ctx, nc, "mat")
        sums = sb("sums", [P, NT, 4, WIDE])
        src_i, dst_i = sb("src_i", [P, TILES], I32), sb("dst_i", [P, TILES], I32)
        src_f = sb("src_f", [P, TILES])
        rows_i, rows_f = sb("rows_i", [GROUPS, GROUP], I32), sb("rows_f", [GROUPS, GROUP])
        lo_span = sb("lo_span", [GROUPS, 3])
        wtab = sb("wtab", [1, (MAXSWEEPS + 1) * GROUPS])
        span1 = sb("span1", [1, 2])
        iota_i = sb("iota_i", [P, WIDE], I32)
        attr3, confb = sb("attr3", [P, TILES, 3]), sb("confb", [P, 4])
        wz, wr = sb("wz", [P, TILES]), sb("wr", [P, TILES])
        wb = sb("wb", [P, 3, TILES], BF16)
        wf = sb("wf", [P, 3, TILES])
        group_src = [sb(f"group_src{a}", [P, TPG]) for a in range(2)]
        from_onehot = [sb(f"from_onehot{a}", [P, TPG, NP], BF16) for a in range(2)]
        to_onehot = [sb(f"to_onehot{a}", [P, TPG, 4, WIN], BF16) for a in range(2)]
        iota16 = sb("iota16", [P, WIDE], F16)
        ps = [pb(f"sum_ps{i}", [P, 4, WIN]) for i in range(NT)]
        ps_row = pb("row_ps", [1, 2, GROUPS])
        ps_deg = pb("deg_ps", [P, NT])

        loaded_rows, loaded_dst, loaded_src = sem("loaded_rows"), sem("loaded_dst"), sem("loaded_src")
        loaded_attr, loaded_conf, loaded_x = sem("loaded_attr"), sem("loaded_conf"), sem("loaded_x")
        iota_made, ident_zero, ident_made, sums_zero = sem("iota_made"), sem("ident_zero"), sem("ident_made"), sem("sums_zero")
        vec, spans_ready, rows_ready, windows_known = sem("vec"), sem("spans_ready"), sem("rows_ready"), sem("windows_known")
        z_ready, exp_ready, act_ready = sem("z_ready"), sem("exp_ready"), sem("act_ready")
        iota_ready, src_copied = sem("iota_ready"), sem("src_copied")
        from_ready, to_ready, tile_ready, tile_free = (
            sem("from_ready"), sem("to_ready"), sem("tile_ready"), sem("tile_free"))
        counts_ready, degree_ready, logs_ready = sem("counts_ready"), sem("degree_ready"), sem("logs_ready")

        def sweeps(eng):
            eng.wait_ge(windows_known, 2)
            return eng.value_load(k.sweeps[0:1, 0:1], min_val=0, max_val=MAXSWEEPS - 1)

        with nc.Block() as block:
            @block.sync
            def _(sp):
                sp.dma_start(rows_i[:, :], k.dram["dst_rows"]).then_inc(loaded_rows, 16)
                sp.dma_start(dst_i[:, :], k.dram["dst_mark"]).then_inc(loaded_dst, 16)
                sp.dma_start(src_i[:, :], k.dram["src_tiles"]).then_inc(loaded_src, 16)
                sp.dma_start(attr3[:, :, :], k.dram["attr3_tiles"].rearrange("p (t c) -> p t c", c=3)).then_inc(loaded_attr, 16)
                sp.dma_start(confb[:, :], k.dram["conf_rows"]).then_inc(loaded_conf, 16)
                sp.dma_start(k.x[:, :, :], k.dram["x_in"].rearrange("(i p) d -> p i d", p=P)).then_inc(loaded_x, 16)
                sp.wait_ge(loaded_x, 16)

            @block.gpsimd
            def _(pool):
                pool.iota(iota_i[:, :], pattern=[[1, WIDE]], base=0, channel_multiplier=0).then_inc(iota_made, 1)
                pool.memset(k.ident[:, :], 0.0).then_inc(ident_zero, 1)
                pool.wait_ge(ident_zero, 1)
                pool.affine_select(out=k.ident[:, :], in_=k.ident[:, :], compare_op=ALU.not_equal, fill=1.0,
                                   base=0, pattern=[[-1, P]], channel_multiplier=1).then_inc(ident_made, 1)
                for i in range(NT):
                    pool.memset(sums[:, i, :, :], 0.0).then_inc(sums_zero, 1)
                n = sweeps(pool)
                pool.wait_ge(iota_ready, 2)
                with pool.Fori(0, n * (GROUPS // 2) + GROUPS // 2) as t:
                    for a in range(2):
                        g = (t * 2 + a) % GROUPS
                        pool.wait_ge(tile_ready, t * (2 * NT) + NT * (a + 1))
                        settle(k, pool)
                        pool.tensor_copy(group_src[a][:, :], src_f[:, bass.ds(g * TPG, TPG)]).then_inc(src_copied, 1)
                        pool.wait_ge(src_copied, t * 2 + (a + 1))
                        settle(k, pool)
                        for j in range(TPG):
                            pool.tensor_scalar(from_onehot[a][:, j, :], iota16[:, 0:NP], group_src[a][:, j:j + 1],
                                               None, ALU.is_equal).then_inc(from_ready, 1)

            @block.scalar
            def _(act):
                act.preload_act_table_set(LOG_AND_EXP)
                act.wait_ge(z_ready, 1)
                act.activation(wz[:, :], wz[:, :], ACT.Exp, scale=-1.0).then_inc(exp_ready, 1)
                act.wait_ge(counts_ready, NT + 1)
                for i in range(NT):
                    act.activation(k.logc[:, i, :], k.logc[:, i, :], ACT.Ln).then_inc(logs_ready, 1)
                act.activation(k.dis[:, :], k.dis[:, :], ACT.Ln).then_inc(act_ready, 1)
                act.wait_ge(act_ready, 1)
                act.activation(k.dis[:, :], k.dis[:, :], ACT.Exp, scale=-0.5).then_inc(logs_ready, 1)

            @block.tensor
            def _(pe):
                pe.wait_ge(ident_made, 1)
                pe.wait_ge(spans_ready, 1)
                pe.matmul(ps_row[:, 0, :], lo_span[:, 0:1], k.ident[0:GROUPS, 0:GROUPS], start=True, stop=True)
                pe.matmul(ps_row[:, 1, :], lo_span[:, 2:3], k.ident[0:GROUPS, 0:GROUPS], start=True,
                          stop=True).then_inc(rows_ready, 1)
                n = sweeps(pe)
                pe.sem_inc(tile_ready, 2 * NT)
                pe.sem_inc(tile_free, NT)
                with pe.Fori(0, n * (GROUPS // 2) + GROUPS // 2) as t:
                    for a in range(2):
                        pe.wait_ge(from_ready, t * (2 * TPG) + TPG * (a + 1))
                        pe.wait_ge(to_ready, t * (8 * TPG) + 4 * TPG * (a + 1))
                        for i in range(NT):
                            pe.wait_ge(tile_free, t * (2 * NT) + (NT * a + i + 1))
                            for j in range(TPG):
                                mm = pe.matmul(ps[i][:, :, :].rearrange("p a b -> p (a b)"),
                                               from_onehot[a][:, j, i * P:(i + 1) * P],
                                               to_onehot[a][:, j, :, :].rearrange("p a b -> p (a b)"),
                                               start=(j == 0), stop=(j == TPG - 1))
                            mm.then_inc(tile_ready, 1)
                pe.wait_ge(counts_ready, NT + 1)
                for j in range(NT):
                    for i in range(NT):
                        mm = pe.matmul(ps_deg[:, j:j + 1], k.C[:, i, j * P:(j + 1) * P], k.ones[:, 0:1],
                                       start=(i == 0), stop=(i == NT - 1))
                mm.then_inc(degree_ready, 1)

            @block.vector
            def _(dve):
                own = Count(dve, vec)

                def step(ins):
                    own(ins)
                    own.wait()

                own(dve.memset(k.ones[:, :], 1.0))
                own(dve.memset(wtab[:, :], 0.0))
                dve.wait_ge(loaded_rows, 16)
                step(dve.tensor_copy(rows_f[:, :], rows_i[:, :]))
                own(dve.tensor_reduce(lo_span[:, 0:1], rows_f[:, :], AX.X, ALU.min))
                step(dve.tensor_reduce(lo_span[:, 1:2], rows_f[:, :], AX.X, ALU.max))
                dve.tensor_tensor(lo_span[:, 2:3], lo_span[:, 1:2], lo_span[:, 0:1], ALU.subtract).then_inc(spans_ready, 1)
                dve.wait_ge(iota_made, 1)
                dve.tensor_copy(iota16[:, :], iota_i[:, :]).then_inc(iota_ready, 1)
                dve.wait_ge(loaded_src, 16)
                dve.tensor_copy(src_f[:, :], src_i[:, :]).then_inc(iota_ready, 1)
                dve.wait_ge(loaded_dst, 16)
                step(dve.tensor_copy(k.dst_f[:, :], dst_i[:, :]))
                dve.wait_ge(rows_ready, 1)
                for w in range(MAXSWEEPS):
                    own(dve.tensor_scalar(wtab[:, w * GROUPS:(w + 1) * GROUPS], ps_row[:, 0, :], float(WIN * w),
                                          float(NP), ALU.add, ALU.min))
                own(dve.tensor_reduce(span1[:, 0:1], ps_row[:, 1, :], AX.X, ALU.max))
                step(dve.memset(span1[:, 1:2], 0.0))
                for w in range(1, MAXSWEEPS):
                    step(dve.scalar_tensor_tensor(span1[:, 1:2], span1[:, 0:1], float(WIN * w), span1[:, 1:2],
                                                  ALU.is_ge, ALU.add))
                dve.tensor_copy(k.starts[:, :], wtab[:, :]).then_inc(windows_known, 1)
                dve.tensor_copy(k.sweeps[:, :], span1[:, 1:2]).then_inc(windows_known, 1)
                dve.wait_ge(loaded_attr, 16)
                dve.wait_ge(loaded_conf, 16)
                step(dve.tensor_scalar(wz[:, :], attr3[:, :, 0], confb[:, 0:1], confb[:, 3:4], ALU.mult, ALU.add))
                step(dve.scalar_tensor_tensor(wz[:, :], attr3[:, :, 1], confb[:, 1:2], wz[:, :], ALU.mult, ALU.add))
                dve.scalar_tensor_tensor(wz[:, :], attr3[:, :, 2], confb[:, 2:3], wz[:, :],
                                         ALU.mult, ALU.add).then_inc(z_ready, 1)
                dve.wait_ge(exp_ready, 1)
                step(dve.tensor_scalar(wz[:, :], wz[:, :], 1.0, None, ALU.add))
                step(dve.reciprocal(wr[:, :], wz[:, :]))
                step(dve.tensor_scalar(wr[:, :], wr[:, :], 0.0, None, ALU.max))
                for n in range(3):
                    step(dve.tensor_copy(wb[:, n, :], wr[:, :]))
                    step(dve.tensor_copy(wf[:, n, :], wb[:, n, :]))
                    if n < 2:
                        step(dve.tensor_tensor(wr[:, :], wr[:, :], wf[:, n, :], ALU.subtract))

                def start_of(u):
                    return dve.value_load(k.starts[0:1, bass.ds(u, 1)], min_val=0, max_val=NP)

                def compare(u, a, start):
                    g = u % GROUPS
                    for j in range(TPG):
                        col = bass.ds(g * TPG + j, 1)
                        dve.tensor_scalar(to_onehot[a][:, j, 0, :], iota16[:, bass.ds(start, WIN)], k.dst_f[:, col],
                                          None, ALU.is_equal).then_inc(to_ready, 1)
                        for n in range(3):
                            dve.tensor_scalar(to_onehot[a][:, j, n + 1, :], iota16[:, bass.ds(start, WIN)],
                                              k.dst_f[:, col], wf[:, n, col], ALU.is_equal, ALU.mult).then_inc(to_ready, 1)

                n = sweeps(dve)
                dve.wait_ge(sums_zero, NT)
                dve.wait_ge(iota_ready, 2)
                compare(0, 0, start_of(0))
                with dve.Fori(0, n * (GROUPS // 2) + GROUPS // 2) as t:
                    for a in range(2):
                        u = t * 2 + a
                        dve.wait_ge(tile_ready, u * NT + 2 * NT)
                        compare(u + 1, 1 - a, start_of(u + 1))
                        start = start_of(u)
                        dve.wait_ge(tile_free, u * NT + NT)
                        for i in range(NT):
                            dve.wait_ge(tile_ready, u * NT + (i + 1 + 2 * NT))
                            into = sums[:, i, :, bass.ds(start, WIN)]
                            dve.tensor_tensor(into, into, ps[i][:, :, :], ALU.add).then_inc(tile_free, 1)
                dve.wait_ge(tile_free, n * (GROUPS * NT) + (GROUPS + 1) * NT)
                done = Count(dve, counts_ready)
                for i in range(NT):
                    done(dve.tensor_copy(k.C[:, i, :], sums[:, i, 0, 0:NP]))
                    own(dve.tensor_tensor(k.W[:, i, :], sums[:, i, 1, 0:NP], sums[:, i, 2, 0:NP], ALU.add))
                done.wait()
                step(dve.tensor_reduce(k.has[:, :], k.C[:, :, :], AX.X, ALU.add))
                step(dve.tensor_scalar(k.dis[:, :], k.has[:, :], 1.0, None, ALU.max))
                step(dve.tensor_scalar(k.has[:, :], k.has[:, :], 1.0, None, ALU.min))
                for i in range(NT):
                    own(dve.tensor_tensor(k.W[:, i, :], k.W[:, i, :], sums[:, i, 3, 0:NP], ALU.add))
                    own(dve.tensor_scalar(k.logc[:, i, :], k.C[:, i, :], 1.0, None, ALU.max))
                own.wait()
                done(dve.memset(sums[:, 0, 0, 0:1], 0.0))
                dve.wait_ge(logs_ready, NT + 1)
                own(dve.tensor_tensor(k.dis[:, :], k.dis[:, :], k.has[:, :], ALU.mult))
                for i in range(NT):
                    none = sums[:, i, 0, 0:NP]
                    step(dve.tensor_scalar(none, k.C[:, i, :], 0.0, NONE, ALU.is_equal, ALU.mult))
                    own(dve.tensor_tensor(k.logc[:, i, :], k.logc[:, i, :], none, ALU.add))
                dve.wait_ge(degree_ready, 1)
                step(dve.tensor_scalar(k.rdeg[:, :], ps_deg[:, :], 1.0, None, ALU.max))
                step(dve.reciprocal(k.rdeg[:, :], k.rdeg[:, :]))



def layernorm_relu(nc, k, x, h, st, mv, var_ready, rstd_ready, h_ready, own, dve):
    for i in range(NT):
        own(dve.bn_stats(st[:, i, :], x[:, i, :]))
    own.wait()
    for i in range(NT):
        own(dve.bn_aggr(mv[:, i, :], st[:, i, :]))
    own.wait()
    dve.tensor_scalar(k.rstd[:, :], mv[:, :, 1], EPS, None, ALU.add).then_inc(var_ready, 1)
    dve.wait_ge(rstd_ready, 1)
    for i in range(NT):
        own(dve.tensor_scalar(h[:, i, :], x[:, i, :], mv[:, i, 0:1], k.rstd[:, i:i + 1], ALU.subtract, ALU.mult))
    own.wait()
    for i in range(NT):
        dve.tensor_scalar(h[:, i, :], h[:, i, :], 0.0, None, ALU.max).then_inc(h_ready, 1)


def inverse_root(act, k, own, rstd_ready):
    own(act.activation(k.rstd[:, :], k.rstd[:, :], ACT.Ln))
    own.wait()
    act.activation(k.rstd[:, :], k.rstd[:, :], ACT.Exp, scale=-0.5).then_inc(rstd_ready, 1)


def turn(pe, bank, src, ident):
    for m in range(KF):
        mm = pe.transpose(bank[:, m * P:(m + 1) * P], src[:, m * P:(m + 1) * P], ident)
    return mm


def chain(pe, out, pairs):
    last = len(pairs) - 1
    for n, (a, b) in enumerate(pairs):
        mm = pe.matmul(out, a, b, start=(n == 0), stop=(n == last))
    return mm


def sage_layer(nc, k):
    ctx = ExitStack()
    with ctx:
        sb, pb, sem = scope(ctx, nc, "sage")
        wl, wr = sb("wl", [P, KF, D]), sb("wr_", [P, KF, D])
        bl = sb("bl", [P, D])
        h, hT, aggT = sb("h", [P, NT, D]), sb("hT", [P, KF, NP]), sb("aggT0", [P, KF, NP])
        own_part = sb("own_part", [P, NT, D])
        st, mv = sb("st", [P, NT, 6]), sb("mv", [P, NT, 2])
        ps = [pb(f"p{i}", [P, D]) for i in range(8)]
        loaded_wl, loaded_wr, loaded_bl = sem("loaded_wl"), sem("loaded_wr"), sem("loaded_bl")
        vec, sca, var_ready, rstd_ready, h_ready = (sem(n) for n in ("vec", "sca", "var_ready", "rstd_ready", "h_ready"))
        plan = Plan(sem("product_ready"), {"vec": sem("taken_vec"), "sca": sem("taken_sca")}, {"one": ps})
        for i in range(NT):
            plan.add(("hT", i), "sca")
        for m in range(KF):
            for f in range(2):
                plan.add(("agg", m, f), "vec")
        for i in range(NT):
            plan.add(("left", i), "sca")
            plan.add(("right", i), "vec")

        with nc.Block() as block:
            @block.sync
            def _(sp):
                sp.dma_start(wl[:, :, :], k.dram["w_l"].rearrange("(c p) n -> p c n", p=P)).then_inc(loaded_wl, 16)
                sp.dma_start(wr[:, :, :], k.dram["w_r"].rearrange("(c p) n -> p c n", p=P)).then_inc(loaded_wr, 16)
                sp.dma_start(bl[:, :], k.dram["b_l"][None, :].to_broadcast([P, D])).then_inc(loaded_bl, 16)

            @block.tensor
            def _(pe):
                for i in range(NT):
                    bank = plan.open(pe, ("hT", i))
                    pe.wait_ge(h_ready, i + 1)
                    plan.made(turn(pe, bank, h[:, i, :], k.ident[:, :]))
                for m in range(KF):
                    for f in range(2):
                        bank = plan.open(pe, ("agg", m, f))
                        plan.made(chain(pe, bank[:, 0:HALF], [(h[:, i, m * P:(m + 1) * P],
                                  k.C[:, i, f * HALF:(f + 1) * HALF]) for i in range(NT)]))
                pe.wait_ge(loaded_wl, 16)
                pe.wait_ge(loaded_wr, 16)
                for i in range(NT):
                    for key, wts, src, before in (("left", wl, aggT, ("agg", KF - 1, 1)), ("right", wr, hT, ("hT", NT - 1))):
                        bank = plan.open(pe, (key, i))
                        if i == 0:
                            plan.need(pe, before)
                        plan.made(chain(pe, bank[:, :], [(src[:, c, i * P:(i + 1) * P], wts[:, c, :]) for c in range(KF)]))

            @block.scalar
            def _(act):
                act.preload_act_table_set(LOG_AND_EXP)
                own = Count(act, sca)
                act.wait_ge(var_ready, 1)
                inverse_root(act, k, own, rstd_ready)
                for i in range(NT):
                    bank = plan.take(act, ("hT", i))
                    plan.took(("hT", i), act.activation(hT[:, :, i * P:(i + 1) * P], cols(bank[:, :], P), ACT.Copy))
                for i in range(NT):
                    bank = plan.take(act, ("left", i))
                    plan.took(("left", i), act.activation(own_part[:, i, :], bank[:, :], ACT.Copy,
                                                          scale=k.rdeg[:, i:i + 1]))

            @block.vector
            def _(dve):
                own = Count(dve, vec)
                layernorm_relu(nc, k, k.x, h, st, mv, var_ready, rstd_ready, h_ready, own, dve)
                for m in range(KF):
                    for f in range(2):
                        bank = plan.take(dve, ("agg", m, f))
                        plan.took(("agg", m, f), dve.tensor_copy(aggT[:, m, f * HALF:(f + 1) * HALF], bank[:, 0:HALF]))
                dve.wait_ge(loaded_bl, 16)
                for i in range(NT):
                    plan.need(dve, ("left", i))
                    own(dve.tensor_tensor(own_part[:, i, :], own_part[:, i, :], bl[:, :], ALU.add))
                    own.wait()
                    bank = plan.take(dve, ("right", i))
                    plan.took(("right", i), dve.tensor_tensor(own_part[:, i, :], own_part[:, i, :], bank[:, :], ALU.add))
                    plan.need(dve, ("right", i))
                    own(dve.scalar_tensor_tensor(k.x[:, i, :], own_part[:, i, :], 0.0, k.x[:, i, :], ALU.max, ALU.add))


TWO_PI_PARTS = (6.28125, 0.0019353071795864769 - 3.0199159819567e-07, 3.0199159819567e-07)
ROUND = 1.5 * 2.0 ** 23


def condition(nc, k):
    ctx = ExitStack()
    with ctx:
        sb, pb, sem = scope(ctx, nc, "cond")
        noise, ph, turns = sb("noise", [EMB, NP]), sb("ph", [EMB, NP]), sb("turns", [EMB, NP])
        emb = sb("emb", [EMB, NP])
        consts = sb("consts", [EMB, 3])
        f1, f2, fb = sb("f1", [EMB, COND]), sb("f2", [COND, COND]), sb("fb", [COND, 2])
        z, e = sb("z", [COND, NP]), sb("e", [COND, NP])
        ps = [pb(f"cp{i}", [COND, HALF]) for i in range(4)]
        loaded_noise, loaded_w = sem("loaded_noise"), sem("loaded_w")
        loaded = [sem(f"loaded_{n}") for n in range(4)]
        vec, angle_ready, emb_ready, hidden_ready, z_ready, e_ready, silu_ready, out_ready = (
            sem(n) for n in ("vec", "angle_ready", "emb_ready", "hidden_ready", "z_ready", "e_ready", "silu_ready", "out_ready"))
        with nc.Block() as block:
            @block.sync
            def _(sp):
                sp.dma_start(noise[:, :], k.dram["noise_rows"]).then_inc(loaded_noise, 16)
                for s, dst, src in zip(loaded, (consts, f1, f2, fb), (k.dram["angle_consts"], k.dram["f_w1"], k.dram["f_w2"], k.dram["f_b"])):
                    sp.dma_start(dst[:, :], src).then_inc(s, 16)

            @block.vector
            def _(dve):
                own = Count(dve, vec)

                def step(ins):
                    own(ins)
                    own.wait()

                step(dve.memset(k.condT[:, :], 0.0))
                own(dve.memset(k.condT[32:33, :], 1.0))
                dve.wait_ge(loaded_noise, 16)
                dve.wait_ge(loaded[0], 16)
                step(dve.tensor_scalar(ph[:, :], noise[:, :], consts[:, 0:1], None, ALU.mult))
                step(dve.tensor_scalar(turns[:, :], ph[:, :], 0.15915494309189535, consts[:, 1:2], ALU.mult, ALU.add))
                step(dve.tensor_scalar(turns[:, :], turns[:, :], ROUND, None, ALU.add))
                step(dve.tensor_scalar(turns[:, :], turns[:, :], ROUND, None, ALU.subtract))
                for part in TWO_PI_PARTS:
                    step(dve.scalar_tensor_tensor(ph[:, :], turns[:, :], -part, ph[:, :], ALU.mult, ALU.add))
                step(dve.tensor_scalar(ph[:, :], ph[:, :], consts[:, 2:3], None, ALU.add))
                dve.tensor_scalar(ph[:, :], ph[:, :], 3.1415925, -3.1415925, ALU.min, ALU.max).then_inc(angle_ready, 1)
                dve.wait_ge(loaded[3], 16)
                for f in range(2):
                    dve.wait_ge(hidden_ready, f + 1)
                    dve.tensor_scalar(z[:, f * HALF:(f + 1) * HALF], ps[f][:, :], fb[:, 0:1], None,
                                      ALU.add).then_inc(z_ready, 1)
                dve.wait_ge(z_ready, 2)
                dve.wait_ge(e_ready, 1)
                step(dve.tensor_scalar(e[:, :], e[:, :], 1.0, None, ALU.add))
                step(dve.reciprocal(e[:, :], e[:, :]))
                dve.tensor_tensor(z[:, :], z[:, :], e[:, :], ALU.mult).then_inc(silu_ready, 1)
                for f in range(2):
                    dve.wait_ge(out_ready, f + 1)
                    own(dve.tensor_scalar(k.condT[0:COND, f * HALF:(f + 1) * HALF], ps[2 + f][:, :], fb[:, 1:2], None,
                                          ALU.add))

            @block.scalar
            def _(act):
                act.wait_ge(angle_ready, 1)
                act.activation(emb[:, :], ph[:, :], ACT.Sin).then_inc(emb_ready, 1)
                act.preload_act_table_set(LOG_AND_EXP)
                act.wait_ge(z_ready, 2)
                act.activation(e[:, :], z[:, :], ACT.Exp, scale=-1.0).then_inc(e_ready, 1)

            @block.tensor
            def _(pe):
                pe.wait_ge(emb_ready, 1)
                pe.wait_ge(loaded[1], 16)
                for f in range(2):
                    pe.matmul(ps[f][:, :], f1[:, :], emb[:, f * HALF:(f + 1) * HALF], start=True,
                              stop=True).then_inc(hidden_ready, 1)
                pe.wait_ge(silu_ready, 1)
                pe.wait_ge(loaded[2], 16)
                for f in range(2):
                    pe.matmul(ps[2 + f][:, :], f2[:, :], z[:, f * HALF:(f + 1) * HALF], start=True,
                              stop=True).then_inc(out_ready, 1)


def transformer_layer(nc, k):
    ctx = ExitStack()
    with ctx:
        sb, pb, sem = scope(ctx, nc, "tr")
        names = ("wq", "wk", "wv", "wo", "m1", "m2")
        w = {n: sb("w_" + n, [P, KF, D]) for n in names}
        cw = sb("cw", [CROWS, 4, D])
        rows = {n: sb("row_" + n, [P, D]) for n in ("bv", "bo", "mb2")}
        cb = sb("cb", [P, BLOCKS, 3, KF])
        r, y = sb("r", [P, NT, D]), sb("y", [P, NT, D])
        yT, qT, kT, v = sb("yT", [P, KF, NP]), sb("qT", [P, KF, NP]), sb("kT", [P, KF, NP]), sb("v", [P, NT, D])
        scores, probs = sb("scores", [P, 3, NP]), sb("probs", [P, 3, NP])
        probsT = [sb("probsT", [P, NT, NP]), k.C]
        hidT = qT
        oT = yT
        nmax, den = sb("nmax", [P, HEADS * NT]), sb("den", [P, HEADS * NT])
        st, mv = sb("st", [P, NT, 6]), sb("mv", [P, NT, 2])
        one = [pb(f"one{i}", [P, D]) for i in range(2)]
        two = [pb(f"two{i}", [P, 2, D]) for i in range(3)]
        loaded = {n: sem("loaded_" + n) for n in names + ("cw", "bv", "bo", "mb2", "cb")}
        vec, sca, var_ready, rstd_ready, h_ready, exp_ready, probs_ready, read1, bias_added, block_done = (
            sem(n) for n in ("vec", "sca", "var_ready", "rstd_ready", "h_ready", "exp_ready", "probs_ready",
                             "read1", "bias_added", "block_done"))
        cb_scaled = sem("cb_scaled")
        plan = Plan(sem("product_ready"), {"vec": sem("taken_vec"), "sca": sem("taken_sca")}, {"one": one, "two": two})
        N = HEADS * NT

        def norm_products(s):
            for i in range(NT):
                plan.add(("scale", s, i), "vec")
                plan.add(("shift", s, i), "vec")
            for i in range(NT):
                plan.add(("yT", s, i), "sca")

        norm_products(0)
        for name, by in (("q", "sca"), ("k", "vec")):
            for m in range(KF):
                for f in range(2):
                    plan.add((name, m, f), by)
        for i in range(NT):
            plan.add(("v", i), "vec")
        for n in range(N + 4):
            if n < N:
                plan.add(("S", n), "vec", "two")
            if 2 <= n < N + 2:
                plan.add(("T", n - 2), "sca", "two")
            if n >= 8 and (n - 8) % NT == 0:
                for f in range(2):
                    plan.add(("o", (n - 8) // NT, f), "sca")
        for i in range(NT):
            plan.add(("wo", i), "vec")
        norm_products(1)
        for m in range(KF):
            for f in range(2):
                plan.add(("m1", m, f), "sca")
        for i in range(NT):
            plan.add(("m2", i), "vec")

        with nc.Block() as block:
            @block.sync
            def _(sp):
                def load(name, b):
                    if name == "cw":
                        dst, src = cw[:, :, :], k.dram["cond_w"][bass.ds(b, 1)].rearrange("o p a n -> p (o a) n")
                    elif name in rows:
                        dst = rows[name][:, :]
                        src = row_biases[name][bass.ds(b, 1), :].to_broadcast([P, D])
                    else:
                        dst = w[name][:, :, :]
                        src = mats[name].rearrange("b (c p) n -> b p c n", p=P)[bass.ds(b, 1)].rearrange("o p c n -> p (o c) n")
                    sp.dma_start(dst, src).then_inc(loaded[name], 16)

                mats = {"wq": k.dram["wq"], "wk": k.dram["wk"], "wv": k.dram["wv"], "wo": k.dram["wo"], "m1": k.dram["m1"], "m2": k.dram["m2"]}
                row_biases = {"bv": k.dram["bv"], "bo": k.dram["bo"], "mb2": k.dram["mb2"]}
                sp.dma_start(cb[:, :, :, :], k.dram["col_biases"].rearrange("p (b n c) -> p b n c", n=3, c=KF)).then_inc(loaded["cb"], 16)
                for name in ("cw", "wq", "wk", "wv", "bv", "bo", "wo", "m1", "m2", "mb2"):
                    load(name, 0)
                with sp.Fori(0, BLOCKS - 1) as b:
                    for name, key in (("wq", ("q", KF - 1, 1)), ("wk", ("k", KF - 1, 1)), ("wv", ("v", NT - 1)),
                                      ("bv", None), ("bo", None), ("wo", ("wo", NT - 1)), ("cw", ("shift", 1, NT - 1)),
                                      ("m1", ("m1", KF - 1, 1)), ("m2", ("m2", NT - 1)), ("mb2", None)):
                        if key:
                            plan.take(sp, key, b)
                        elif name == "bv":
                            plan.need(sp, ("v", NT - 1), b)
                        elif name == "bo":
                            sp.wait_ge(bias_added, b * 2 * NT + NT)
                        else:
                            sp.wait_ge(bias_added, b * 2 * NT + 2 * NT)
                        load(name, b + 1)

            @block.gpsimd
            def _(pool):
                with pool.Fori(0, BLOCKS) as b:
                    for s, name in enumerate(("bo", "mb2")):
                        pool.wait_ge(loaded[name], b * 16 + 16)
                        for i in range(NT):
                            pool.wait_ge(read1, b * (2 * NT) + (s * NT + i + 1))
                            pool.tensor_tensor(r[:, i, :], r[:, i, :], rows[name][:, :], ALU.add).then_inc(bias_added, 1)

            @block.tensor
            def _(pe):
                def norm(s, b):
                    if s == 0:
                        pe.wait_ge(loaded["cw"], b * 16 + 16)
                    for i in range(NT):
                        for key, c in (("scale", 0), ("shift", 1)):
                            bank = plan.open(pe, (key, s, i), b)
                            plan.made(pe.matmul(bank[:, :], k.condT[:, i * P:(i + 1) * P], cw[:, 2 * s + c, :],
                                                start=True, stop=True))
                    for i in range(NT):
                        bank = plan.open(pe, ("yT", s, i), b)
                        plan.need(pe, ("shift", s, i), b)
                        plan.made(turn(pe, bank, y[:, i, :], k.ident[:, :]))

                def by_feature(name, wts, src, b):
                    for m in range(KF):
                        for f in range(2):
                            bank = plan.open(pe, (name, m, f), b)
                            plan.made(chain(pe, bank[:, 0:HALF], [(wts[:, c, m * P:(m + 1) * P],
                                      src[:, c, f * HALF:(f + 1) * HALF]) for c in range(KF)]))

                def by_node(name, wts, src, b):
                    for i in range(NT):
                        bank = plan.open(pe, (name, i), b)
                        plan.made(chain(pe, bank[:, :], [(src[:, c, i * P:(i + 1) * P], wts[:, c, :]) for c in range(KF)]))

                pe.sem_inc(block_done, 1)
                with pe.Fori(0, BLOCKS) as b:
                    pe.wait_ge(block_done, b + 1)
                    norm(0, b)
                    plan.need(pe, ("yT", 0, NT - 1), b)
                    pe.wait_ge(loaded["wq"], b * 16 + 16)
                    by_feature("q", w["wq"], yT, b)
                    pe.wait_ge(loaded["wk"], b * 16 + 16)
                    by_feature("k", w["wk"], yT, b)
                    pe.wait_ge(loaded["wv"], b * 16 + 16)
                    by_node("v", w["wv"], yT, b)
                    for n in range(N + 4):
                        if n < N:
                            h, i = divmod(n, NT)
                            bank = plan.open(pe, ("S", n), b)
                            if i == 0:
                                plan.need(pe, ("q", h, 1), b)
                                plan.need(pe, ("k", h, 1), b)
                            for f in range(2):
                                mm = pe.matmul(bank[:, f, 0:HALF], qT[:, h, i * P:(i + 1) * P],
                                               kT[:, h, f * HALF:(f + 1) * HALF], start=True, stop=True)
                            plan.made(mm)
                        if 2 <= n < N + 2:
                            bank = plan.open(pe, ("T", n - 2), b)
                            pe.wait_ge(probs_ready, b * N + (n - 1))
                            flat = bank[:, :, :].rearrange("p a b -> p (a b)")
                            for j in range(NT):
                                mm = pe.transpose(flat[:, j * P:(j + 1) * P], probs[:, (n - 2) % 3, j * P:(j + 1) * P],
                                                  k.ident[:, :])
                            plan.made(mm)
                        if n >= 8 and (n - 8) % NT == 0:
                            h = (n - 8) // NT
                            plan.need(pe, ("T", h * NT + NT - 1), b)
                            if h == 0:
                                plan.need(pe, ("v", NT - 1), b)
                            for f in range(2):
                                bank = plan.open(pe, ("o", h, f), b)
                                plan.made(chain(pe, bank[:, 0:HALF], [(v[:, j, h * DH:(h + 1) * DH],
                                          probsT[h % 2][:, j, f * HALF:(f + 1) * HALF]) for j in range(NT)]))
                    plan.need(pe, ("o", HEADS - 1, 1), b)
                    pe.wait_ge(loaded["wo"], b * 16 + 16)
                    by_node("wo", w["wo"], oT, b)
                    norm(1, b)
                    plan.need(pe, ("yT", 1, NT - 1), b)
                    pe.wait_ge(loaded["m1"], b * 16 + 16)
                    by_feature("m1", w["m1"], yT, b)
                    plan.need(pe, ("m1", KF - 1, 1), b)
                    pe.wait_ge(loaded["m2"], b * 16 + 16)
                    by_node("m2", w["m2"], hidT, b)

            @block.scalar
            def _(act):
                act.preload_act_table_set(LOG_AND_EXP)
                first = Count(act, sca)
                act.wait_ge(var_ready, 1)
                inverse_root(act, k, first, rstd_ready)
                act.wait_ge(cb_scaled, 1)

                with act.Fori(0, BLOCKS) as b:
                    own = Count(act, sca, 1, b, 2)

                    def norm(s):
                        act.wait_ge(var_ready, b * 2 + (s + 2))
                        inverse_root(act, k, own, rstd_ready)
                        for i in range(NT):
                            bank = plan.take(act, ("yT", s, i), b)
                            plan.took(("yT", s, i), act.activation(yT[:, :, i * P:(i + 1) * P], cols(bank[:, :], P), ACT.Copy))

                    def bias_of(which, m):
                        return cb[:, bass.ds(b, 1), which, m]

                    norm(0)
                    for m in range(KF):
                        for f in range(2):
                            bank = plan.take(act, ("q", m, f), b)
                            settle(k, act)
                            plan.took(("q", m, f), act.activation(qT[:, m, f * HALF:(f + 1) * HALF], bank[:, 0:HALF],
                                                                  ACT.Identity, bias=bias_of(0, m), scale=DH ** -0.5))
                    for n in range(N + 4):
                        if n < N:
                            plan.need(act, ("S", n), b)
                            act.activation(probs[:, n % 3, :], scores[:, n % 3, :], ACT.Exp, bias=nmax[:, n:n + 1],
                                           scale=-1.0, accum_out=den[:, n:n + 1]).then_inc(exp_ready, 1)
                        if 2 <= n < N + 2:
                            h, i = divmod(n - 2, NT)
                            bank = plan.take(act, ("T", n - 2), b)
                            flat = bank[:, :, :].rearrange("p a b -> p (a b)")
                            plan.took(("T", n - 2), act.activation(probsT[h % 2][:, :, i * P:(i + 1) * P],
                                                                   cols(flat[:, 0:NP], P), ACT.Copy))
                        if n >= 8 and (n - 8) % NT == 0:
                            h = (n - 8) // NT
                            for f in range(2):
                                bank = plan.take(act, ("o", h, f), b)
                                plan.took(("o", h, f), act.activation(oT[:, h, f * HALF:(f + 1) * HALF],
                                                                      bank[:, 0:HALF], ACT.Copy))
                    norm(1)
                    for m in range(KF):
                        for f in range(2):
                            bank = plan.take(act, ("m1", m, f), b)
                            settle(k, act)
                            plan.took(("m1", m, f), act.activation(hidT[:, m, f * HALF:(f + 1) * HALF], bank[:, 0:HALF],
                                                                   ACT.Relu, bias=bias_of(2, m)))

            @block.vector
            def _(dve):
                first = Count(dve, vec)
                layernorm_relu(nc, k, k.x, r, st, mv, var_ready, rstd_ready, h_ready, first, dve)
                dve.wait_ge(loaded["cb"], 16)
                dve.tensor_scalar(cb[:, :, 0, :], cb[:, :, 0, :], DH ** -0.5, None, ALU.mult).then_inc(cb_scaled, 1)
                dve.wait_ge(cb_scaled, 1)
                dve.wait_ge(h_ready, NT)

                with dve.Fori(0, BLOCKS) as b:
                    own = Count(dve, vec, first.n, b, 4 * NT + N)

                    def norm(s):
                        for i in range(NT):
                            own(dve.bn_stats(st[:, i, :], r[:, i, :]))
                        own.wait()
                        settle(k, dve)
                        for i in range(NT):
                            own(dve.bn_aggr(mv[:, i, :], st[:, i, :]))
                        own.wait()
                        dve.tensor_scalar(k.rstd[:, :], mv[:, :, 1], EPS, None, ALU.add).then_inc(var_ready, 1)
                        dve.wait_ge(rstd_ready, b * 2 + (s + 2))
                        for i in range(NT):
                            dve.tensor_scalar(y[:, i, :], r[:, i, :], mv[:, i, 0:1], k.rstd[:, i:i + 1],
                                              ALU.subtract, ALU.mult).then_inc(read1, 1)
                        dve.wait_ge(read1, b * (2 * NT) + (s + 1) * NT)
                        for i in range(NT):
                            bank = plan.take(dve, ("scale", s, i), b)
                            plan.took(("scale", s, i), dve.scalar_tensor_tensor(y[:, i, :], bank[:, :], 1.0, y[:, i, :],
                                                                                ALU.add, ALU.mult))
                            bank = plan.take(dve, ("shift", s, i), b)
                            plan.need(dve, ("scale", s, i), b)
                            plan.took(("shift", s, i), dve.tensor_tensor(y[:, i, :], y[:, i, :], bank[:, :], ALU.add))

                    def residual(name, s):
                        for i in range(NT):
                            dve.wait_ge(bias_added, b * (2 * NT) + (s * NT + i + 1))
                            bank = plan.take(dve, (name, i), b)
                            plan.took((name, i), dve.tensor_tensor(r[:, i, :], r[:, i, :], bank[:, :], ALU.add))
                        plan.need(dve, (name, NT - 1), b)

                    norm(0)
                    for m in range(KF):
                        for f in range(2):
                            bank = plan.take(dve, ("k", m, f), b)
                            plan.took(("k", m, f), dve.tensor_scalar(kT[:, m, f * HALF:(f + 1) * HALF], bank[:, 0:HALF],
                                                                     cb[:, bass.ds(b, 1), 1, m], None, ALU.add))
                    dve.wait_ge(loaded["bv"], b * 16 + 16)
                    for i in range(NT):
                        bank = plan.take(dve, ("v", i), b)
                        plan.took(("v", i), dve.tensor_tensor(v[:, i, :], bank[:, :], rows["bv"][:, :], ALU.add))
                    for n in range(N + 1):
                        if n < N:
                            i = n % NT
                            bank = plan.take(dve, ("S", n), b)
                            settle(k, dve)
                            ins = dve.tensor_tensor_reduce(out=cols(scores[:, n % 3, :], HALF), in0=bank[:, :, 0:HALF],
                                                           in1=cols(k.logc[:, i, :], HALF), scale=-1.0, scalar=3.0e38,
                                                           op0=ALU.add, op1=ALU.min, accum_out=nmax[:, n:n + 1])
                            plan.took(("S", n), ins)
                        if n >= 1:
                            m = n - 1
                            dve.wait_ge(exp_ready, b * N + (m + 1))
                            own(dve.reciprocal(den[:, m:m + 1], den[:, m:m + 1]))
                            own.wait()
                            dve.tensor_scalar(probs[:, m % 3, :], probs[:, m % 3, :], den[:, m:m + 1],
                                              k.has[:, m % NT:m % NT + 1], ALU.mult, ALU.mult).then_inc(probs_ready, 1)
                    residual("wo", 0)
                    norm(1)
                    residual("m2", 1)
                    dve.sem_inc(block_done, 1)
                for i in range(NT):
                    dve.tensor_tensor(k.x[:, i, :], k.x[:, i, :], r[:, i, :], ALU.add).then_inc(h_ready, 1)


def gcn_layer(nc, k):
    ctx = ExitStack()
    with ctx:
        sb, pb, sem = scope(ctx, nc, "gcn")
        wt, lb = sb("wt", [P, KF, D]), sb("lb", [P, D])
        h, aggT = sb("h", [P, NT, D]), sb("aggT", [P, KF, NP])
        st, mv = sb("st", [P, NT, 6]), sb("mv", [P, NT, 2])
        ps = [pb(f"p{i}", [P, D]) for i in range(8)]
        loaded_wt, loaded_lb = sem("loaded_wt"), sem("loaded_lb")
        vec, sca, var_ready, rstd_ready, h_ready, scaled = (
            sem(n) for n in ("vec", "sca", "var_ready", "rstd_ready", "h_ready", "scaled"))
        plan = Plan(sem("product_ready"), {"vec": sem("taken_vec"), "sca": sem("taken_sca")}, {"one": ps})
        for m in range(KF):
            for f in range(2):
                plan.add(("agg", m, f), "sca")
        for i in range(NT):
            plan.add(("lin", i), "vec")

        with nc.Block() as block:
            @block.sync
            def _(sp):
                sp.dma_start(wt[:, :, :], k.dram["lin_w"].rearrange("(c p) n -> p c n", p=P)).then_inc(loaded_wt, 16)
                sp.dma_start(lb[:, :], k.dram["lin_b"][None, :].to_broadcast([P, D])).then_inc(loaded_lb, 16)

            @block.scalar
            def _(act):
                act.preload_act_table_set(LOG_AND_EXP)
                own = Count(act, sca)
                act.wait_ge(var_ready, 1)
                inverse_root(act, k, own, rstd_ready)
                for m in range(KF):
                    for f in range(2):
                        bank = plan.take(act, ("agg", m, f))
                        plan.took(("agg", m, f), act.activation(aggT[:, m, f * HALF:(f + 1) * HALF], bank[:, 0:HALF], ACT.Copy))

            @block.tensor
            def _(pe):
                pe.wait_ge(scaled, NT)
                for m in range(KF):
                    for f in range(2):
                        bank = plan.open(pe, ("agg", m, f))
                        plan.made(chain(pe, bank[:, 0:HALF], [(h[:, i, m * P:(m + 1) * P],
                                  k.W[:, i, f * HALF:(f + 1) * HALF]) for i in range(NT)]))
                pe.wait_ge(loaded_wt, 16)
                for i in range(NT):
                    bank = plan.open(pe, ("lin", i))
                    if i == 0:
                        plan.need(pe, ("agg", KF - 1, 1))
                    plan.made(chain(pe, bank[:, :], [(aggT[:, c, i * P:(i + 1) * P], wt[:, c, :]) for c in range(KF)]))

            @block.vector
            def _(dve):
                own = Count(dve, vec)
                layernorm_relu(nc, k, k.x, h, st, mv, var_ready, rstd_ready, h_ready, own, dve)
                dve.wait_ge(h_ready, NT)
                for i in range(NT):
                    dve.tensor_scalar(h[:, i, :], h[:, i, :], k.dis[:, i:i + 1], None, ALU.mult).then_inc(scaled, 1)
                dve.wait_ge(loaded_lb, 16)
                for i in range(NT):
                    own(dve.tensor_tensor(k.x[:, i, :], k.x[:, i, :], lb[:, :], ALU.add))
                own.wait()
                for i in range(NT):
                    bank = plan.take(dve, ("lin", i))
                    plan.took(("lin", i), dve.scalar_tensor_tensor(k.x[:, i, :], bank[:, :], k.dis[:, i:i + 1],
                                                                   k.x[:, i, :], ALU.mult, ALU.add))


class Mish:

    def __init__(self, z, e, n, out):
        self.z, self.e, self.n, self.out = z, e, n, out

    def cap(self, dve):
        return dve.tensor_scalar(self.e, self.z, CAP, None, ALU.min)

    def exp(self, act):
        return act.activation(self.e, self.e, ACT.Exp)

    def square(self, dve):
        return dve.scalar_tensor_tensor(self.n, self.e, 2.0, self.e, ALU.add, ALU.mult)

    def log(self, act):
        return act.activation(self.n, self.n, ACT.Ln, bias=1.0, scale=0.5)

    def quotient(self, act):
        return act.activation(self.n, self.n, ACT.Exp, scale=-1.0)

    def product(self, dve):
        return dve.scalar_tensor_tensor(self.out, self.n, 1.0, self.z, ALU.subtract, ALU.mult, reverse0=True)


def edge_layer_tables(nc, k):
    ctx = ExitStack()
    with ctx:
        sb, pb, sem = scope(ctx, nc, "tab")
        ws, wd, b1 = sb("ws", [P, KF, D]), sb("wd", [P, KF, D]), sb("b1", [P, D])
        tables = {"src": sb("ts", [P, NT, D]), "dst": sb("td", [P, NT, D])}
        st, mv = sb("st", [P, NT, 6]), sb("mv", [P, NT, 2])
        ps = [pb(f"p{i}", [P, D]) for i in range(8)]
        loaded = {n: sem("loaded_" + n) for n in ("src", "dst", "b1")}
        stored = {n: sem("stored_" + n) for n in ("src", "dst")}
        vec, sca, var_ready, rstd_ready, h_ready = (
            sem(n) for n in ("vec", "sca", "var_ready", "rstd_ready", "h_ready"))
        plan = Plan(sem("product_ready"), {"vec": sem("taken_vec"), "sca": sem("taken_sca")}, {"one": ps})
        for i in range(NT):
            plan.add(("hT", i), "sca")
        for name in ("src", "dst"):
            for i in range(NT):
                plan.add((name, i), "vec")

        with nc.Block() as block:
            @block.sync
            def _(sp):
                w1 = k.dram["w1"][0:2 * D, :].rearrange("(c p) n -> p c n", p=P)
                sp.dma_start(ws[:, :, :], w1[:, 0:KF, :]).then_inc(loaded["src"], 16)
                sp.dma_start(wd[:, :, :], w1[:, KF:2 * KF, :]).then_inc(loaded["dst"], 16)
                sp.dma_start(b1[:, :], k.dram["b1"][None, :].to_broadcast([P, D])).then_inc(loaded["b1"], 16)
                for name, out in (("src", k.src_table), ("dst", k.dst_table)):
                    plan.need(sp, (name, NT - 1))
                    sp.dma_start(out.rearrange("(i p) d -> p i d", p=P), tables[name][:, :, :]).then_inc(stored[name], 16)
                sp.wait_ge(stored["src"], 16)
                sp.wait_ge(stored["dst"], 16)

            @block.scalar
            def _(act):
                act.preload_act_table_set(LOG_AND_EXP)
                own = Count(act, sca)
                act.wait_ge(var_ready, 1)
                inverse_root(act, k, own, rstd_ready)
                for i in range(NT):
                    bank = plan.take(act, ("hT", i))
                    plan.took(("hT", i), act.activation(k.hT[:, :, i * P:(i + 1) * P], cols(bank[:, :], P), ACT.Copy))

            @block.tensor
            def _(pe):
                for i in range(NT):
                    bank = plan.open(pe, ("hT", i))
                    pe.wait_ge(h_ready, i + 1)
                    plan.made(turn(pe, bank, k.h[:, i, :], k.ident[:, :]))
                for name, w in (("src", ws), ("dst", wd)):
                    pe.wait_ge(loaded[name], 16)
                    for i in range(NT):
                        bank = plan.open(pe, (name, i))
                        plan.need(pe, ("hT", i))
                        plan.made(chain(pe, bank[:, :], [(k.hT[:, c, i * P:(i + 1) * P], w[:, c, :]) for c in range(KF)]))

            @block.vector
            def _(dve):
                own = Count(dve, vec)
                layernorm_relu(nc, k, k.x, k.h, st, mv, var_ready, rstd_ready, h_ready, own, dve)
                dve.wait_ge(loaded["b1"], 16)
                for name in ("src", "dst"):
                    for i in range(NT):
                        bank = plan.take(dve, (name, i))
                        dst = tables[name][:, i, :]
                        plan.took((name, i), dve.tensor_copy(dst, bank[:, :]) if name == "src" else
                                  dve.tensor_tensor(dst, bank[:, :], b1[:, :], ALU.add))


def edge_messages(nc, k):
    PT = 2
    EDGE = PT * P
    ctx = ExitStack()
    with ctx:
        sb, pb, sem = scope(ctx, nc, "edge")
        w1a, w2, b2 = sb("w1a", [EATTR, D]), sb("w2", [P, KF, D]), sb("b2", [P, D])
        iota_i, iota = sb("iota_i", [P, WIDE], I32), sb("iota", [P, WIDE])
        attrT = [sb(f"attrT{a}", [EATTR, EDGE]) for a in range(2)]
        index = [sb(f"index{a}", [P, 2 * PT], I32) for a in range(2)]
        from_rows = [sb(f"from_rows{a}", [P, PT, D]) for a in range(2)]
        to_rows = [sb(f"to_rows{a}", [P, PT, D]) for a in range(2)]
        z1, n1, h1 = ([sb(f"{n}{a}", [P, PT * D]) for a in range(2)] for n in ("z1", "n1", "h1"))
        z2, n2, h2 = ([sb(f"{n}{a}", [P, PT * D]) for a in range(2)] for n in ("z2", "n2", "h2"))
        e1, e2 = ([sb(f"{n}{a}", [P, PT * D]) for a in range(2)] for n in ("e1", "e2"))
        hT = [sb(f"hT{a}", [P, KF, EDGE]) for a in range(2)]
        onehot = [sb(f"onehot{a}", [P, PT, WIN]) for a in range(2)]
        ps_z1 = [pb(f"z1p{j}", [P, D]) for j in range(PT)]
        ps_hT = [pb(f"hTp{j}", [P, D]) for j in range(PT)]
        ps_z2 = [pb(f"z2p{j}", [P, D]) for j in range(PT)]
        ps_sum = pb("sump", [P, KF, WIN])
        loaded = {n: sem("loaded_" + n) for n in ("w1a", "w2", "b2")}
        attr_loaded, index_loaded, from_loaded, to_loaded = (
            [sem(f"{n}{a}") for a in range(2)] for n in ("attr_loaded", "index_loaded", "from_loaded", "to_loaded"))
        names = ("attr_product", "z1_ready", "e1_ready", "n1_ready", "log1_ready", "q1_ready",
                 "h1_ready", "turned", "hT_ready", "w2_product", "z2_ready", "e2_ready", "n2_ready", "log2_ready",
                 "q2_ready", "h2_ready", "onehot_ready", "sum_ready", "summed", "vec", "iota_made", "agg_zero",
                 "capped1", "capped2", "part_ready")
        S = {n: sem(n) for n in names}
        mish1 = [Mish(z1[a][:, :], e1[a][:, :], n1[a][:, :], h1[a][:, :]) for a in range(2)]
        mish2 = [Mish(z2[a][:, :], e2[a][:, :], n2[a][:, :], h2[a][:, :]) for a in range(2)]
        PAIRS = GROUPS * TPG // PT
        DEPTH = 4

        def sweeps(eng):
            return eng.value_load(k.sweeps[0:1, 0:1], min_val=0, max_val=MAXSWEEPS - 1)

        def run_steps(eng, step):
            n = sweeps(eng)
            for s in range(DEPTH):
                step(lambda add: s + add, s % 2, lambda lag: lag <= s)
            with eng.Fori(0, n * (PAIRS // 2) + (PAIRS - DEPTH) // 2) as t:
                for a in range(2):
                    step(lambda add: t * 2 + (a + DEPTH + add), a, lambda lag: True)
            for s in range(DEPTH):
                step(lambda add: n * PAIRS + (PAIRS + s + add), s % 2, lambda lag: lag > s)

        with nc.Block() as block:
            @block.sync
            def _(sp):
                sp.dma_start(w1a[:, :], k.dram["w1"][2 * D:2 * D + EATTR, :]).then_inc(loaded["w1a"], 16)
                sp.dma_start(w2[:, :, :], k.dram["w2"].rearrange("(c p) n -> p c n", p=P)).then_inc(loaded["w2"], 16)
                sp.dma_start(b2[:, :], k.dram["b2"][None, :].to_broadcast([P, D])).then_inc(loaded["b2"], 16)
                n = sweeps(sp)
                with sp.Fori(0, n * (PAIRS // 2) + PAIRS // 2) as t:
                    for a in range(2):
                        p = (t % (PAIRS // 2)) * 2 + a
                        sp.wait_ge(S["z1_ready"], t * 2 + (a + 1))
                        sp.dma_start(index[a][:, :], k.dram["pair_index"][bass.ds(p, 1)].rearrange("o p c -> (o p) c")
                                     ).then_inc(index_loaded[a], 16)
                        sp.wait_ge(S["part_ready"], t * 2 + (a + 1))
                        sp.dma_start(attrT[a][:, :], k.dram["attr_T"][:, bass.ds(p * EDGE, EDGE)]).then_inc(attr_loaded[a], 16)

            @block.gpsimd
            def _(pool):
                pool.iota(iota_i[:, :], pattern=[[1, WIDE]], base=0, channel_multiplier=0).then_inc(S["iota_made"], 1)
                pool.memset(k.aggT[:, :, :], 0.0).then_inc(S["agg_zero"], 1)
                n = sweeps(pool)
                with pool.Fori(0, n * (PAIRS // 2) + PAIRS // 2) as t:
                    for a in range(2):
                        pool.wait_ge(index_loaded[a], t * 16 + 16)
                        pool.wait_ge(S["z1_ready"], t * 2 + (a + 1))
                        settle(k, pool)
                        for c, (table, rows, done) in enumerate(((k.src_table, from_rows, from_loaded),
                                                                 (k.dst_table, to_rows, to_loaded))):
                            for j in range(PT):
                                pool.indirect_dma_start(
                                    out=rows[a][:, j, :], out_offset=None, in_=table,
                                    in_offset=bass.IndirectOffsetOnAxis(ap=index[a][:, c * PT + j:c * PT + j + 1], axis=0)
                                ).then_inc(done[a], 16)

            @block.tensor
            def _(pe):
                for n in loaded:
                    if n != "b2":
                        pe.wait_ge(loaded[n], 16)

                def step(s, a, on):
                    b = 1 - a
                    if on(0):
                        half = s(0) // 2
                        pe.wait_ge(attr_loaded[a], half * 16 + 16)
                        if on(1):
                            pe.wait_ge(S["part_ready"], s(2))
                        for j in range(PT):
                            mm = pe.matmul(ps_z1[j][:, :], attrT[a][:, j * P:(j + 1) * P], w1a[:, :], start=True, stop=True)
                        mm.then_inc(S["attr_product"], 1)
                    if on(2):
                        pe.wait_ge(S["hT_ready"], s(-1) * PT)
                        if on(3):
                            pe.wait_ge(S["z2_ready"], s(-2))
                        for j in range(PT):
                            mm = chain(pe, ps_z2[j][:, :], [(hT[a][:, c, j * P:(j + 1) * P], w2[:, c, :]) for c in range(KF)])
                        mm.then_inc(S["w2_product"], 1)
                    if on(4):
                        pe.wait_ge(S["h2_ready"], s(-3))
                        pe.wait_ge(S["onehot_ready"], s(-3) * PT)
                        pe.wait_ge(S["summed"], s(-3))
                        for c in range(KF):
                            mm = chain(pe, ps_sum[:, c, :], [(h2[a][:, j * D + c * P:j * D + (c + 1) * P], onehot[a][:, j, :])
                                                             for j in range(PT)])
                        mm.then_inc(S["sum_ready"], 1)
                    if on(1):
                        pe.wait_ge(S["h1_ready"], s(0))
                        for j in range(PT):
                            turn(pe, ps_hT[j], h1[b][:, j * D:(j + 1) * D], k.ident[:, :]).then_inc(S["turned"], 1)

                run_steps(pe, step)

            @block.scalar
            def _(act):
                act.preload_act_table_set(LOG_AND_EXP)
                def step(s, a, on):
                    b = 1 - a
                    if on(1):
                        act.wait_ge(S["capped1"], s(0))
                        mish1[b].exp(act).then_inc(S["e1_ready"], 1)
                    if on(3):
                        act.wait_ge(S["capped2"], s(-2))
                        mish2[b].exp(act).then_inc(S["e2_ready"], 1)
                    if on(1):
                        act.wait_ge(S["n1_ready"], s(0))
                        mish1[b].log(act).then_inc(S["log1_ready"], 1)
                        act.wait_ge(S["log1_ready"], s(0))
                        mish1[b].quotient(act).then_inc(S["q1_ready"], 1)
                    if on(3):
                        act.wait_ge(S["n2_ready"], s(-2))
                        mish2[b].log(act).then_inc(S["log2_ready"], 1)
                        act.wait_ge(S["log2_ready"], s(-2))
                        mish2[b].quotient(act).then_inc(S["q2_ready"], 1)
                    if on(1):
                        for j in range(PT):
                            act.wait_ge(S["turned"], s(-1) * PT + (j + 1))
                            act.activation(hT[b][:, :, j * P:(j + 1) * P], cols(ps_hT[j][:, :], P),
                                           ACT.Copy).then_inc(S["hT_ready"], 1)

                run_steps(act, step)

            @block.vector
            def _(dve):
                dve.wait_ge(S["iota_made"], 1)
                dve.tensor_copy(iota[:, :], iota_i[:, :]).then_inc(S["vec"], 1)
                dve.wait_ge(S["vec"], 1)
                dve.wait_ge(loaded["b2"], 16)
                dve.wait_ge(S["agg_zero"], 1)
                dve.sem_inc(S["part_ready"], 2)
                dve.sem_inc(S["z1_ready"], 2)
                dve.sem_inc(S["summed"], 1)

                def step(s, a, on):
                    b = 1 - a
                    if on(1):
                        half = s(-1) // 2
                        z = cols(z1[b][:, :], D)
                        dve.wait_ge(from_loaded[b], half * (16 * PT) + 16 * PT)
                        dve.wait_ge(to_loaded[b], half * (16 * PT) + 16 * PT)
                        dve.wait_ge(S["attr_product"], s(0))
                        for j in range(PT):
                            ins = dve.tensor_tensor(z[:, j, :], ps_z1[j][:, :], from_rows[b][:, j, :], ALU.add)
                        ins.then_inc(S["part_ready"], 1)
                        dve.wait_ge(S["part_ready"], s(2))
                        dve.tensor_tensor(z, z, to_rows[b][:, :, :], ALU.add).then_inc(S["z1_ready"], 1)
                        dve.wait_ge(S["z1_ready"], s(2))
                        mish1[b].cap(dve).then_inc(S["capped1"], 1)
                    if on(3):
                        dve.wait_ge(S["w2_product"], s(-2))
                        z = cols(z2[b][:, :], D)
                        for j in range(PT):
                            ins = dve.tensor_tensor(z[:, j, :], ps_z2[j][:, :], b2[:, :], ALU.add)
                        ins.then_inc(S["z2_ready"], 1)
                        dve.wait_ge(S["z2_ready"], s(-2))
                        mish2[b].cap(dve).then_inc(S["capped2"], 1)
                    if on(1):
                        dve.wait_ge(S["e1_ready"], s(0))
                        mish1[b].square(dve).then_inc(S["n1_ready"], 1)
                    if on(3):
                        dve.wait_ge(S["e2_ready"], s(-2))
                        mish2[b].square(dve).then_inc(S["n2_ready"], 1)
                    if on(1):
                        dve.wait_ge(S["q1_ready"], s(0))
                        mish1[b].product(dve).then_inc(S["h1_ready"], 1)
                    if on(3):
                        u = s(-3) // 2
                        start = dve.value_load(k.starts[0:1, bass.ds(u, 1)], min_val=0, max_val=NP)
                        tile0 = (s(-3) % PAIRS) * PT
                        for j in range(PT):
                            dve.tensor_scalar(onehot[b][:, j, :], iota[:, bass.ds(start, WIN)],
                                              k.dst_f[:, bass.ds(tile0 + j, 1)], None,
                                              ALU.is_equal).then_inc(S["onehot_ready"], 1)
                        dve.wait_ge(S["q2_ready"], s(-2))
                        mish2[b].product(dve).then_inc(S["h2_ready"], 1)
                    if on(4):
                        u = s(-4) // 2
                        start = dve.value_load(k.starts[0:1, bass.ds(u, 1)], min_val=0, max_val=NP)
                        dve.wait_ge(S["sum_ready"], s(-3))
                        dve.wait_ge(S["summed"], s(-3))
                        into = k.aggT[:, :, bass.ds(start, WIN)]
                        dve.tensor_tensor(into, into, ps_sum[:, :, :], ALU.add).then_inc(S["summed"], 1)

                run_steps(dve, step)


def edge_layer_nodes(nc, k):
    ctx = ExitStack()
    with ctx:
        sb, pb, sem = scope(ctx, nc, "node")
        w3, w4 = sb("w3", [P, 2 * KF, D]), sb("w4", [P, KF, D])
        b3 = sb("b3", [P, KF])
        rows = {n: sb("row_" + n, [P, D]) for n in ("b4", "gamma", "beta")}
        z, e, n_, uT = sb("z", [P, KF, NP]), sb("e", [P, KF, NP]), sb("n", [P, KF, NP]), sb("uT", [P, KF, NP])
        st, mv = sb("st", [P, NT, 6]), sb("mv", [P, NT, 2])
        ps = [pb(f"p{i}", [P, D]) for i in range(8)]
        loaded = {n: sem("loaded_" + n) for n in ("w3", "w4", "b3", "b4", "gamma", "beta")}
        vec, sca, var_ready, rstd_ready, e_ready, n_ready, q_ready, u_ready, stored, x_ready = (
            sem(n) for n in ("vec", "sca", "var_ready", "rstd_ready", "e_ready", "n_ready", "q_ready", "u_ready",
                             "stored", "x_ready"))
        capped = sem("capped")
        plan = Plan(sem("product_ready"), {"vec": sem("taken_vec"), "sca": sem("taken_sca")}, {"one": ps})
        for m in range(KF):
            for f in range(2):
                plan.add(("u", m, f), "sca")
        for i in range(NT):
            plan.add(("w4", i), "vec")
        parts = [Mish(z[:, m, :], e[:, m, :], n_[:, m, :], uT[:, m, :]) for m in range(KF)]

        with nc.Block() as block:
            @block.sync
            def _(sp):
                sp.dma_start(w3[:, :, :], k.dram["w3"].rearrange("(c p) n -> p c n", p=P)).then_inc(loaded["w3"], 16)
                sp.dma_start(b3[:, :], k.dram["b3_cols"]).then_inc(loaded["b3"], 16)
                sp.dma_start(w4[:, :, :], k.dram["w4"].rearrange("(c p) n -> p c n", p=P)).then_inc(loaded["w4"], 16)
                for n, src in (("b4", k.dram["b4"]), ("gamma", k.dram["gamma"]), ("beta", k.dram["beta"])):
                    sp.dma_start(rows[n][:, :], src[None, :].to_broadcast([P, D])).then_inc(loaded[n], 16)
                for i in range(NT):
                    sp.wait_ge(x_ready, i + 1)
                    sp.dma_start(k.dram["out"][i * P:(i + 1) * P, :], k.x[:, i, :]).then_inc(stored, 16)
                sp.wait_ge(stored, 16 * NT)

            @block.tensor
            def _(pe):
                pe.wait_ge(loaded["w3"], 16)
                for m in range(KF):
                    for f in range(2):
                        bank = plan.open(pe, ("u", m, f))
                        half = slice(f * HALF, (f + 1) * HALF)
                        plan.made(chain(pe, bank[:, 0:HALF],
                                        [(w3[:, c, m * P:(m + 1) * P], k.hT[:, c, half]) for c in range(KF)] +
                                        [(w3[:, KF + c, m * P:(m + 1) * P], k.aggT[:, c, half]) for c in range(KF)]))
                pe.wait_ge(loaded["w4"], 16)
                pe.wait_ge(u_ready, KF)
                for i in range(NT):
                    bank = plan.open(pe, ("w4", i))
                    plan.made(chain(pe, bank[:, :], [(uT[:, c, i * P:(i + 1) * P], w4[:, c, :]) for c in range(KF)]))

            @block.scalar
            def _(act):
                act.preload_act_table_set(LOG_AND_EXP)
                own = Count(act, sca)
                act.wait_ge(loaded["b3"], 16)
                for m in range(KF):
                    for f in range(2):
                        bank = plan.take(act, ("u", m, f))
                        plan.took(("u", m, f), act.activation(z[:, m, f * HALF:(f + 1) * HALF], bank[:, 0:HALF],
                                                              ACT.Identity, bias=b3[:, m:m + 1]))
                    act.wait_ge(capped, m + 1)
                    parts[m].exp(act).then_inc(e_ready, 1)
                for m in range(KF):
                    act.wait_ge(n_ready, m + 1)
                    own(parts[m].log(act))
                    own.wait()
                    parts[m].quotient(act).then_inc(q_ready, 1)
                act.wait_ge(var_ready, 1)
                inverse_root(act, k, own, rstd_ready)

            @block.vector
            def _(dve):
                own = Count(dve, vec)
                for m in range(KF):
                    plan.need(dve, ("u", m, 1))
                    parts[m].cap(dve).then_inc(capped, 1)
                for m in range(KF):
                    dve.wait_ge(e_ready, m + 1)
                    parts[m].square(dve).then_inc(n_ready, 1)
                for n in ("b4", "gamma", "beta"):
                    dve.wait_ge(loaded[n], 16)
                for i in range(NT):
                    own(dve.tensor_tensor(k.h[:, i, :], k.h[:, i, :], rows["b4"][:, :], ALU.add))
                for m in range(KF):
                    dve.wait_ge(q_ready, m + 1)
                    parts[m].product(dve).then_inc(u_ready, 1)
                own.wait()
                for i in range(NT):
                    bank = plan.take(dve, ("w4", i))
                    plan.took(("w4", i), dve.tensor_tensor(k.h[:, i, :], k.h[:, i, :], bank[:, :], ALU.add))
                    plan.need(dve, ("w4", i))
                    own(dve.bn_stats(st[:, i, :], k.h[:, i, :]))
                own.wait()
                for i in range(NT):
                    own(dve.bn_aggr(mv[:, i, :], st[:, i, :]))
                own.wait()
                dve.tensor_scalar(k.rstd[:, :], mv[:, :, 1], EPS, None, ALU.add).then_inc(var_ready, 1)
                for i in range(NT):
                    own(dve.tensor_tensor(k.x[:, i, :], k.x[:, i, :], rows["beta"][:, :], ALU.add))
                dve.wait_ge(rstd_ready, 1)
                for i in range(NT):
                    own(dve.tensor_scalar(k.h[:, i, :], k.h[:, i, :], mv[:, i, 0:1], k.rstd[:, i:i + 1],
                                          ALU.subtract, ALU.mult))
                own.wait()
                for i in range(NT):
                    own(dve.tensor_tensor(k.h[:, i, :], k.h[:, i, :], rows["gamma"][:, :], ALU.mult))
                own.wait()
                for i in range(NT):
                    dve.tensor_tensor(k.x[:, i, :], k.x[:, i, :], k.h[:, i, :], ALU.add).then_inc(x_ready, 1)


def write_rows(nc, k):
    with nc.semaphore("stored") as stored, nc.Block() as block:
        @block.sync
        def _(sp):
            sp.dma_start(k.dram["out"].rearrange("(i p) d -> p i d", p=P), k.x[:, :, :]).then_inc(stored, 16)
            sp.wait_ge(stored, 16)


STAGES = 5


def build(nc, a, out):
    k = Kernel(dict(a, out=out))
    ctx = ExitStack()
    with ctx:
        sb = lambda name, shape, dt=F32: ctx.enter_context(nc.sbuf_tensor(name, shape, dt))
        k.x, k.C, k.W, k.logc = sb("x", [P, NT, D]), sb("C", [P, NT, NP]), sb("W", [P, NT, NP]), sb("logc", [P, NT, NP])
        k.ident, k.ones, k.rstd = sb("ident", [P, P]), sb("ones", [P, P]), sb("rstd", [P, NT])
        k.has, k.dis, k.rdeg = sb("has", [P, NT]), sb("dis", [P, NT]), sb("rdeg", [P, NT])
        k.dst_f = sb("dst_f", [P, TILES])
        k.starts, k.sweeps = sb("starts", [1, (MAXSWEEPS + 1) * GROUPS], I32), sb("sweeps", [1, 1], I32)
        k.settled = ctx.enter_context(nc.semaphore("settled"))
        k.condT = sb("condT", [CROWS, NP])
        condition(nc, k)
        edge_windows_and_matrices(nc, k)
        sage_layer(nc, k)
        if STAGES > 2:
            transformer_layer(nc, k)
        if STAGES > 3:
            gcn_layer(nc, k)
        if STAGES < 5:
            write_rows(nc, k)
            return
        k.h, k.hT, k.aggT = sb("h", [P, NT, D]), sb("hT", [P, KF, NP]), sb("aggT", [P, KF, WIDE])
        k.src_table = nc.dram_tensor("src_table", (NP, D), F32, kind="Internal").ap()
        k.dst_table = nc.dram_tensor("dst_table", (NP, D), F32, kind="Internal").ap()
        edge_layer_tables(nc, k)
        edge_messages(nc, k)
        edge_layer_nodes(nc, k)


def kernel(**inputs):
    import numpy as np
    import concourse.bacc as bacc
    from concourse.bass_utils import run_bass_kernel_spmd as run

    v = {n: np.asarray(a) for n, a in inputs.items()}
    pad, pad_nodes = TILES * P - EDGES, NP - NODES

    def edges(a, fill):
        a = np.concatenate([a, np.full((pad,) + a.shape[1:], fill, a.dtype)])
        return np.ascontiguousarray(np.moveaxis(a.reshape((GROUPS, P, TPG) + a.shape[1:]), 1, 0)).reshape(P, -1)

    dst = v["dst"]
    host = {
        "x_in": np.concatenate([v["x"], np.zeros((NP - NODES, D), np.float32)]),
        "dst_rows": np.concatenate([dst, np.broadcast_to(dst[-1:], (pad,))]).reshape(GROUPS, GROUP),
        "dst_mark": edges(dst, -1),
        "src_tiles": edges(v["src"], 0),
        "attr3_tiles": edges(v["edge_attr_3"], 0),
        "conf_rows": np.broadcast_to(np.concatenate([v["L2_gnn_conf_w"][0], v["L2_gnn_conf_b"]]), (P, 4)),
        "w_l": v["L0_gnn_W_l"].T, "w_r": v["L0_gnn_W_r"].T, "b_l": v["L0_gnn_b_l"],
    }
    noise = np.concatenate([v["node_vec1"][:, 0], np.zeros(pad_nodes, np.float32)])
    host["noise_rows"] = np.broadcast_to(noise, (EMB, NP))
    freqs = np.arange(1, EMB // 2 + 1, dtype=np.float32) * np.float32(2.0 * np.pi / 16)
    quarter = np.repeat(np.array([0.0, 0.25], np.float32), EMB // 2)
    host["angle_consts"] = np.stack([np.tile(freqs, 2), quarter, (quarter * np.float32(2 * np.pi)).astype(np.float32)], 1)
    t = {n[7:]: a for n, a in v.items() if n.startswith("L1_gnn_")}
    host.update(f_w1=t["f_w1"], f_w2=t["f_w2"], f_b=np.stack([t["f_b1"], t["f_b2"]], 1))
    host.update(wq=t["wq"], wk=t["wk"], wv=t["wv"], wo=t["wo"], m1=t["m_w1"], m2=t["m_w2"],
                bv=t["bv"], bo=t["bo"], mb2=t["m_b2"])
    cond_w = np.zeros((BLOCKS, CROWS, 4, D), np.float32)
    for n, (ws, bs) in enumerate((("s1_w", "s1_b"), ("b1_w", "b1_b"), ("s2_w", "s2_b"), ("b2_w", "b2_b"))):
        cond_w[:, 0:COND, n], cond_w[:, CROWS - 1, n] = t[ws], t[bs]
    host["cond_w"] = cond_w
    host["col_biases"] = np.stack([t["bq"], t["bk"], t["m_b1"]], 1).reshape(BLOCKS, 3, KF, P).transpose(3, 0, 1, 2).reshape(P, -1)
    t = {n[7:]: a for n, a in v.items() if n.startswith("L3_gnn_")}
    host.update(lin_w=v["L2_gnn_lin_w"].T, lin_b=v["L2_gnn_lin_b"], w1=t["W1"], w2=t["W2"], w3=t["W3"], w4=t["W4"],
                b1=t["b1"], b2=t["b2"], b4=t["b4"], gamma=t["gamma"], beta=t["beta"],
                b3_cols=t["b3"].reshape(KF, P).T)
    both = np.stack([host["src_tiles"], edges(dst, 0)]).reshape(2, P, TILES // 2, 2)
    host["pair_index"] = both.transpose(2, 1, 0, 3).reshape(TILES // 2, P, 4)
    attr = edges(v["edge_attr_64"], 0).reshape(P, TILES, EATTR)
    host["attr_T"] = attr.transpose(2, 1, 0).reshape(EATTR, TILES * P)
    nc = bacc.Bacc("TRN2", target_bir_lowering=False, num_devices=1)
    arrays, args = {}, {}
    for name, a in host.items():
        a = np.ascontiguousarray(a)
        arrays["in_" + name] = a
        args[name] = nc.dram_tensor("in_" + name, a.shape, mybir.dt.from_np(a.dtype), kind="ExternalInput").ap()
    out = nc.dram_tensor("out_0", (NP, D), F32, kind="ExternalOutput").ap()
    build(nc, args, out)
    r = run(nc, [arrays], core_ids=[0])
    return r.results[0]["out_0"][:NODES]
```

```python
from contextlib import ExitStack

import concourse.bass as bass
from concourse import mybir

F32, BF16, I32 = mybir.dt.float32, mybir.dt.bfloat16, mybir.dt.int32
F16, F32R = mybir.dt.float16, mybir.dt.float32r
ALU, ACT, AX = mybir.AluOpType, mybir.ActivationFunctionType, mybir.AxisListType

P = 128
NODES, D, EDGES = 625, 512, 20000
NT = -(-NODES // P)
NP = NT * P
HALF = NP // 2
KF = D // P
HEADS, DH = 4, 128
BLOCKS = 4
EMB, COND = 64, 16
CROWS = 33
TPG = 4
GROUP = TPG * P
GROUPS = -(-EDGES // GROUP)
TILES = GROUPS * TPG
WIN = 64
WIDE = NP + WIN
MAXSWEEPS = NP // WIN
EATTR = 64
EPS = 1e-5
NONE = -1.0e30
LOG_AND_EXP = "natural_log_exp_and_others"
CAP = 20.0


class Kernel:

    def __init__(self, dram):
        self.dram = dram


class Product:
    def __init__(self, n, by, c, before, bank):
        self.n, self.by, self.c, self.before, self.bank = n, by, c, before, bank


class Count:

    def __init__(self, eng, sem, start=0, it=None, per=0):
        self.eng, self.sem, self.n, self.it, self.per = eng, sem, start, it, per

    def at(self, n=None):
        n = self.n if n is None else n
        return n if self.it is None else self.it * self.per + n

    def __call__(self, ins):
        ins.then_inc(self.sem, 1)
        self.n += 1
        return self.n

    def wait(self, n=None):
        self.eng.wait_ge(self.sem, self.at(n))


class Plan:

    def __init__(self, product_ready, taken, rings):
        self.ready, self.taken, self.rings = product_ready, taken, rings
        self.at, self.used, self.count = {}, {r: [] for r in rings}, {e: 0 for e in taken}
        self.total = 0

    def add(self, key, by, ring="one"):
        self.total += 1
        self.count[by] += 1
        slots = self.rings[ring]
        used = self.used[ring]
        before = used[-len(slots)] if len(used) >= len(slots) else None
        used.append(key)
        self.at[key] = Product(n=self.total, by=by, c=self.count[by], before=before,
                                       bank=slots[(len(used) - 1) % len(slots)])

    def open(self, pe, key, it=None):
        g = self.at[key]
        if g.before is not None:
            self.need(pe, g.before, it)
        return g.bank

    def need(self, eng, key, it=None):
        g = self.at[key]
        eng.wait_ge(self.taken[g.by], g.c if it is None else it * self.count[g.by] + g.c)

    def made(self, ins):
        ins.then_inc(self.ready, 1)

    def take(self, eng, key, it=None):
        g = self.at[key]
        eng.wait_ge(self.ready, g.n if it is None else it * self.total + g.n)
        return g.bank

    def took(self, key, ins):
        ins.then_inc(self.taken[self.at[key].by], 1)


def scope(ctx, nc, tag):
    return (lambda name, shape, dt=F32: ctx.enter_context(nc.sbuf_tensor(f"{tag}_{name}", shape, dt)),
            lambda name, shape: ctx.enter_context(nc.psum_tensor(f"{tag}_{name}", shape, F32)),
            lambda name: ctx.enter_context(nc.semaphore(f"{tag}_{name}")))


def settle(k, eng):
    eng.sem_inc(k.settled, 1)


def cols(ap, n):
    return ap.rearrange("p (a b) -> p a b", b=n)


def edge_windows_and_matrices(nc, k):
    ctx = ExitStack()
    with ctx:
        sb, pb, sem = scope(ctx, nc, "mat")
        sums = sb("sums", [P, NT, 4, WIDE])
        dst_i = sb("dst_i", [P, TILES], I32)
        src_f = sb("src_f", [P, TILES])
        rows_i, rows_f = sb("rows_i", [GROUPS, GROUP], I32), sb("rows_f", [GROUPS, GROUP])
        lo_span = sb("lo_span", [GROUPS, 3])
        wtab = sb("wtab", [1, (MAXSWEEPS + 1) * GROUPS])
        span1 = sb("span1", [1, 2])
        iota_i = sb("iota_i", [P, WIDE], I32)
        attr3, confb = sb("attr3", [P, TILES, 3]), sb("confb", [P, 4])
        wz, wr = sb("wz", [P, TILES]), sb("wr", [P, TILES])
        wb = sb("wb", [P, 3, TILES], BF16)
        wf = sb("wf", [P, 3, TILES])
        group_src = [sb(f"group_src{a}", [P, TPG]) for a in range(2)]
        from_onehot = [sb(f"from_onehot{a}", [P, TPG, NP], BF16) for a in range(2)]
        to_onehot = [sb(f"to_onehot{a}", [P, TPG, 4, WIN], BF16) for a in range(2)]
        iota16 = sb("iota16", [P, WIDE], F16)
        ps = [pb(f"sum_ps{i}", [P, 4, WIN]) for i in range(NT)]
        ps_row = pb("row_ps", [1, 2, GROUPS])
        ps_deg = pb("deg_ps", [P, NT])

        loaded_rows, loaded_dst, loaded_src = sem("loaded_rows"), sem("loaded_dst"), sem("loaded_src")
        loaded_attr, loaded_conf, loaded_x = sem("loaded_attr"), sem("loaded_conf"), sem("loaded_x")
        iota_made, ident_zero, ident_made, sums_zero = sem("iota_made"), sem("ident_zero"), sem("ident_made"), sem("sums_zero")
        vec, spans_ready, rows_ready, windows_known = sem("vec"), sem("spans_ready"), sem("rows_ready"), sem("windows_known")
        z_ready, exp_ready, act_ready = sem("z_ready"), sem("exp_ready"), sem("act_ready")
        iota_ready, src_copied = sem("iota_ready"), sem("src_copied")
        from_ready, to_ready, tile_ready, tile_free = (
            sem("from_ready"), sem("to_ready"), sem("tile_ready"), sem("tile_free"))
        counts_ready, degree_ready, logs_ready = sem("counts_ready"), sem("degree_ready"), sem("logs_ready")

        def sweeps(eng):
            eng.wait_ge(windows_known, 2)
            return eng.value_load(k.sweeps[0:1, 0:1], min_val=0, max_val=MAXSWEEPS - 1)

        with nc.Block() as block:
            @block.sync
            def _(sp):
                sp.dma_start(rows_i[:, :], k.dram["dst_rows"]).then_inc(loaded_rows, 16)
                sp.dma_start(dst_i[:, :], k.dram["dst_mark"]).then_inc(loaded_dst, 16)
                sp.dma_start(k.src_i[:, :], k.dram["src_tiles"]).then_inc(loaded_src, 16)
                sp.dma_start(attr3[:, :, :], k.dram["attr3_tiles"].rearrange("p (t c) -> p t c", c=3)).then_inc(loaded_attr, 16)
                sp.dma_start(confb[:, :], k.dram["conf_rows"]).then_inc(loaded_conf, 16)
                sp.dma_start(k.x[:, :, :], k.dram["x_in"].rearrange("(i p) d -> p i d", p=P)).then_inc(loaded_x, 16)
                sp.wait_ge(loaded_x, 16)

            @block.gpsimd
            def _(pool):
                pool.iota(iota_i[:, :], pattern=[[1, WIDE]], base=0, channel_multiplier=0).then_inc(iota_made, 1)
                pool.memset(k.ident[:, :], 0.0).then_inc(ident_zero, 1)
                pool.wait_ge(ident_zero, 1)
                pool.affine_select(out=k.ident[:, :], in_=k.ident[:, :], compare_op=ALU.not_equal, fill=1.0,
                                   base=0, pattern=[[-1, P]], channel_multiplier=1).then_inc(ident_made, 1)
                for i in range(NT):
                    pool.memset(sums[:, i, :, :], 0.0).then_inc(sums_zero, 1)
                n = sweeps(pool)
                pool.wait_ge(iota_ready, 2)
                with pool.Fori(0, n * (GROUPS // 2) + GROUPS // 2) as t:
                    for a in range(2):
                        g = (t * 2 + a) % GROUPS
                        pool.wait_ge(tile_ready, t * (2 * NT) + NT * (a + 1))
                        settle(k, pool)
                        pool.tensor_copy(group_src[a][:, :], src_f[:, bass.ds(g * TPG, TPG)]).then_inc(src_copied, 1)
                        pool.wait_ge(src_copied, t * 2 + (a + 1))
                        settle(k, pool)
                        for j in range(TPG):
                            pool.tensor_scalar(from_onehot[a][:, j, :], iota16[:, 0:NP], group_src[a][:, j:j + 1],
                                               None, ALU.is_equal).then_inc(from_ready, 1)

            @block.scalar
            def _(act):
                act.preload_act_table_set(LOG_AND_EXP)
                act.wait_ge(z_ready, 1)
                act.activation(wz[:, :], wz[:, :], ACT.Exp, scale=-1.0).then_inc(exp_ready, 1)
                act.wait_ge(counts_ready, NT + 1)
                for i in range(NT):
                    act.activation(k.logc[:, i, :], k.logc[:, i, :], ACT.Ln).then_inc(logs_ready, 1)
                act.activation(k.dis[:, :], k.dis[:, :], ACT.Ln).then_inc(act_ready, 1)
                act.wait_ge(act_ready, 1)
                act.activation(k.dis[:, :], k.dis[:, :], ACT.Exp, scale=-0.5).then_inc(logs_ready, 1)

            @block.tensor
            def _(pe):
                pe.wait_ge(ident_made, 1)
                pe.wait_ge(spans_ready, 1)
                pe.matmul(ps_row[:, 0, :], lo_span[:, 0:1], k.ident[0:GROUPS, 0:GROUPS], start=True, stop=True)
                pe.matmul(ps_row[:, 1, :], lo_span[:, 2:3], k.ident[0:GROUPS, 0:GROUPS], start=True,
                          stop=True).then_inc(rows_ready, 1)
                n = sweeps(pe)
                pe.sem_inc(tile_ready, 2 * NT)
                pe.sem_inc(tile_free, NT)
                with pe.Fori(0, n * (GROUPS // 2) + GROUPS // 2) as t:
                    for a in range(2):
                        pe.wait_ge(from_ready, t * (2 * TPG) + TPG * (a + 1))
                        pe.wait_ge(to_ready, t * (8 * TPG) + 4 * TPG * (a + 1))
                        for i in range(NT):
                            pe.wait_ge(tile_free, t * (2 * NT) + (NT * a + i + 1))
                            for j in range(TPG):
                                mm = pe.matmul(ps[i][:, :, :].rearrange("p a b -> p (a b)"),
                                               from_onehot[a][:, j, i * P:(i + 1) * P],
                                               to_onehot[a][:, j, :, :].rearrange("p a b -> p (a b)"),
                                               start=(j == 0), stop=(j == TPG - 1))
                            mm.then_inc(tile_ready, 1)
                pe.wait_ge(counts_ready, NT + 1)
                for j in range(NT):
                    for i in range(NT):
                        mm = pe.matmul(ps_deg[:, j:j + 1], k.C[:, i, j * P:(j + 1) * P], k.ones[:, 0:1],
                                       start=(i == 0), stop=(i == NT - 1))
                mm.then_inc(degree_ready, 1)

            @block.vector
            def _(dve):
                own = Count(dve, vec)

                def step(ins):
                    own(ins)
                    own.wait()

                own(dve.memset(k.ones[:, :], 1.0))
                own(dve.memset(wtab[:, :], 0.0))
                dve.wait_ge(loaded_rows, 16)
                step(dve.tensor_copy(rows_f[:, :], rows_i[:, :]))
                own(dve.tensor_reduce(lo_span[:, 0:1], rows_f[:, :], AX.X, ALU.min))
                step(dve.tensor_reduce(lo_span[:, 1:2], rows_f[:, :], AX.X, ALU.max))
                dve.tensor_tensor(lo_span[:, 2:3], lo_span[:, 1:2], lo_span[:, 0:1], ALU.subtract).then_inc(spans_ready, 1)
                dve.wait_ge(iota_made, 1)
                dve.tensor_copy(iota16[:, :], iota_i[:, :]).then_inc(iota_ready, 1)
                dve.wait_ge(loaded_src, 16)
                dve.tensor_copy(src_f[:, :], k.src_i[:, :]).then_inc(iota_ready, 1)
                dve.wait_ge(loaded_dst, 16)
                step(dve.tensor_copy(k.dst_f[:, :], dst_i[:, :]))
                dve.wait_ge(rows_ready, 1)
                for w in range(MAXSWEEPS):
                    own(dve.tensor_scalar(wtab[:, w * GROUPS:(w + 1) * GROUPS], ps_row[:, 0, :], float(WIN * w),
                                          float(NP), ALU.add, ALU.min))
                own(dve.tensor_reduce(span1[:, 0:1], ps_row[:, 1, :], AX.X, ALU.max))
                step(dve.memset(span1[:, 1:2], 0.0))
                for w in range(1, MAXSWEEPS):
                    step(dve.scalar_tensor_tensor(span1[:, 1:2], span1[:, 0:1], float(WIN * w), span1[:, 1:2],
                                                  ALU.is_ge, ALU.add))
                dve.tensor_copy(k.starts[:, :], wtab[:, :]).then_inc(windows_known, 1)
                dve.tensor_copy(k.sweeps[:, :], span1[:, 1:2]).then_inc(windows_known, 1)
                dve.wait_ge(loaded_attr, 16)
                dve.wait_ge(loaded_conf, 16)
                step(dve.tensor_scalar(wz[:, :], attr3[:, :, 0], confb[:, 0:1], confb[:, 3:4], ALU.mult, ALU.add))
                step(dve.scalar_tensor_tensor(wz[:, :], attr3[:, :, 1], confb[:, 1:2], wz[:, :], ALU.mult, ALU.add))
                dve.scalar_tensor_tensor(wz[:, :], attr3[:, :, 2], confb[:, 2:3], wz[:, :],
                                         ALU.mult, ALU.add).then_inc(z_ready, 1)
                dve.wait_ge(exp_ready, 1)
                step(dve.tensor_scalar(wz[:, :], wz[:, :], 1.0, None, ALU.add))
                step(dve.reciprocal(wr[:, :], wz[:, :]))
                step(dve.tensor_scalar(wr[:, :], wr[:, :], 0.0, None, ALU.max))
                for n in range(3):
                    step(dve.tensor_copy(wb[:, n, :], wr[:, :]))
                    step(dve.tensor_copy(wf[:, n, :], wb[:, n, :]))
                    if n < 2:
                        step(dve.tensor_tensor(wr[:, :], wr[:, :], wf[:, n, :], ALU.subtract))

                def start_of(u):
                    return dve.value_load(k.starts[0:1, bass.ds(u, 1)], min_val=0, max_val=NP)

                def compare(u, a, start):
                    g = u % GROUPS
                    for j in range(TPG):
                        col = bass.ds(g * TPG + j, 1)
                        dve.tensor_scalar(to_onehot[a][:, j, 0, :], iota16[:, bass.ds(start, WIN)], k.dst_f[:, col],
                                          None, ALU.is_equal).then_inc(to_ready, 1)
                        for n in range(3):
                            dve.tensor_scalar(to_onehot[a][:, j, n + 1, :], iota16[:, bass.ds(start, WIN)],
                                              k.dst_f[:, col], wf[:, n, col], ALU.is_equal, ALU.mult).then_inc(to_ready, 1)

                n = sweeps(dve)
                dve.wait_ge(sums_zero, NT)
                dve.wait_ge(iota_ready, 2)
                compare(0, 0, start_of(0))
                with dve.Fori(0, n * (GROUPS // 2) + GROUPS // 2) as t:
                    for a in range(2):
                        u = t * 2 + a
                        dve.wait_ge(tile_ready, u * NT + 2 * NT)
                        compare(u + 1, 1 - a, start_of(u + 1))
                        start = start_of(u)
                        dve.wait_ge(tile_free, u * NT + NT)
                        for i in range(NT):
                            dve.wait_ge(tile_ready, u * NT + (i + 1 + 2 * NT))
                            into = sums[:, i, :, bass.ds(start, WIN)]
                            dve.tensor_tensor(into, into, ps[i][:, :, :], ALU.add).then_inc(tile_free, 1)
                dve.wait_ge(tile_free, n * (GROUPS * NT) + (GROUPS + 1) * NT)
                done = Count(dve, counts_ready)
                for i in range(NT):
                    done(dve.tensor_copy(k.C[:, i, :], sums[:, i, 0, 0:NP]))
                    own(dve.tensor_tensor(k.W[:, i, :], sums[:, i, 1, 0:NP], sums[:, i, 2, 0:NP], ALU.add))
                done.wait()
                step(dve.tensor_reduce(k.has[:, :], k.C[:, :, :], AX.X, ALU.add))
                step(dve.tensor_scalar(k.dis[:, :], k.has[:, :], 1.0, None, ALU.max))
                step(dve.tensor_scalar(k.has[:, :], k.has[:, :], 1.0, None, ALU.min))
                for i in range(NT):
                    own(dve.tensor_tensor(k.W[:, i, :], k.W[:, i, :], sums[:, i, 3, 0:NP], ALU.add))
                    own(dve.tensor_scalar(k.logc[:, i, :], k.C[:, i, :], 1.0, None, ALU.max))
                own.wait()
                done(dve.memset(sums[:, 0, 0, 0:1], 0.0))
                dve.wait_ge(logs_ready, NT + 1)
                own(dve.tensor_tensor(k.dis[:, :], k.dis[:, :], k.has[:, :], ALU.mult))
                for i in range(NT):
                    none = sums[:, i, 0, 0:NP]
                    step(dve.tensor_scalar(none, k.C[:, i, :], 0.0, NONE, ALU.is_equal, ALU.mult))
                    own(dve.tensor_tensor(k.logc[:, i, :], k.logc[:, i, :], none, ALU.add))
                dve.wait_ge(degree_ready, 1)
                step(dve.tensor_scalar(k.rdeg[:, :], ps_deg[:, :], 1.0, None, ALU.max))
                step(dve.reciprocal(k.rdeg[:, :], k.rdeg[:, :]))



def layernorm_relu(nc, k, x, h, st, mv, var_ready, rstd_ready, h_ready, own, dve):
    for i in range(NT):
        own(dve.bn_stats(st[:, i, :], x[:, i, :]))
    own.wait()
    for i in range(NT):
        own(dve.bn_aggr(mv[:, i, :], st[:, i, :]))
    own.wait()
    dve.tensor_scalar(k.rstd[:, :], mv[:, :, 1], EPS, None, ALU.add).then_inc(var_ready, 1)
    dve.wait_ge(rstd_ready, 1)
    for i in range(NT):
        own(dve.tensor_scalar(h[:, i, :], x[:, i, :], mv[:, i, 0:1], k.rstd[:, i:i + 1], ALU.subtract, ALU.mult))
    own.wait()
    for i in range(NT):
        dve.tensor_scalar(h[:, i, :], h[:, i, :], 0.0, None, ALU.max).then_inc(h_ready, 1)


def inverse_root(act, k, own, rstd_ready):
    own(act.activation(k.rstd[:, :], k.rstd[:, :], ACT.Ln))
    own.wait()
    act.activation(k.rstd[:, :], k.rstd[:, :], ACT.Exp, scale=-0.5).then_inc(rstd_ready, 1)


def turn(pe, bank, src, ident):
    for m in range(KF):
        mm = pe.transpose(bank[:, m * P:(m + 1) * P], src[:, m * P:(m + 1) * P], ident)
    return mm


def chain(pe, out, pairs):
    last = len(pairs) - 1
    for n, (a, b) in enumerate(pairs):
        mm = pe.matmul(out, a, b, start=(n == 0), stop=(n == last))
    return mm


def sage_layer(nc, k):
    ctx = ExitStack()
    with ctx:
        sb, pb, sem = scope(ctx, nc, "sage")
        wl, wr = sb("wl", [P, KF, D]), sb("wr_", [P, KF, D])
        bl = sb("bl", [P, D])
        h, hT, aggT = sb("h", [P, NT, D]), sb("hT", [P, KF, NP]), sb("aggT0", [P, KF, NP])
        own_part = sb("own_part", [P, NT, D])
        st, mv = sb("st", [P, NT, 6]), sb("mv", [P, NT, 2])
        ps = [pb(f"p{i}", [P, D]) for i in range(8)]
        loaded_wl, loaded_wr, loaded_bl = sem("loaded_wl"), sem("loaded_wr"), sem("loaded_bl")
        vec, sca, var_ready, rstd_ready, h_ready = (sem(n) for n in ("vec", "sca", "var_ready", "rstd_ready", "h_ready"))
        plan = Plan(sem("product_ready"), {"vec": sem("taken_vec"), "sca": sem("taken_sca")}, {"one": ps})
        for i in range(NT):
            plan.add(("hT", i), "sca")
        for m in range(KF):
            for f in range(2):
                plan.add(("agg", m, f), "vec")
        for i in range(NT):
            plan.add(("left", i), "sca")
            plan.add(("right", i), "vec")

        with nc.Block() as block:
            @block.sync
            def _(sp):
                sp.dma_start(wl[:, :, :], k.dram["w_l"].rearrange("(c p) n -> p c n", p=P)).then_inc(loaded_wl, 16)
                sp.dma_start(wr[:, :, :], k.dram["w_r"].rearrange("(c p) n -> p c n", p=P)).then_inc(loaded_wr, 16)
                sp.dma_start(bl[:, :], k.dram["b_l"][None, :].to_broadcast([P, D])).then_inc(loaded_bl, 16)

            @block.tensor
            def _(pe):
                for i in range(NT):
                    bank = plan.open(pe, ("hT", i))
                    pe.wait_ge(h_ready, i + 1)
                    plan.made(turn(pe, bank, h[:, i, :], k.ident[:, :]))
                for m in range(KF):
                    for f in range(2):
                        bank = plan.open(pe, ("agg", m, f))
                        plan.made(chain(pe, bank[:, 0:HALF], [(h[:, i, m * P:(m + 1) * P],
                                  k.C[:, i, f * HALF:(f + 1) * HALF]) for i in range(NT)]))
                pe.wait_ge(loaded_wl, 16)
                pe.wait_ge(loaded_wr, 16)
                for i in range(NT):
                    for key, wts, src, before in (("left", wl, aggT, ("agg", KF - 1, 1)), ("right", wr, hT, ("hT", NT - 1))):
                        bank = plan.open(pe, (key, i))
                        if i == 0:
                            plan.need(pe, before)
                        plan.made(chain(pe, bank[:, :], [(src[:, c, i * P:(i + 1) * P], wts[:, c, :]) for c in range(KF)]))

            @block.scalar
            def _(act):
                act.preload_act_table_set(LOG_AND_EXP)
                own = Count(act, sca)
                act.wait_ge(var_ready, 1)
                inverse_root(act, k, own, rstd_ready)
                for i in range(NT):
                    bank = plan.take(act, ("hT", i))
                    plan.took(("hT", i), act.activation(hT[:, :, i * P:(i + 1) * P], cols(bank[:, :], P), ACT.Copy))
                for i in range(NT):
                    bank = plan.take(act, ("left", i))
                    plan.took(("left", i), act.activation(own_part[:, i, :], bank[:, :], ACT.Copy,
                                                          scale=k.rdeg[:, i:i + 1]))

            @block.vector
            def _(dve):
                own = Count(dve, vec)
                layernorm_relu(nc, k, k.x, h, st, mv, var_ready, rstd_ready, h_ready, own, dve)
                for m in range(KF):
                    for f in range(2):
                        bank = plan.take(dve, ("agg", m, f))
                        plan.took(("agg", m, f), dve.tensor_copy(aggT[:, m, f * HALF:(f + 1) * HALF], bank[:, 0:HALF]))
                dve.wait_ge(loaded_bl, 16)
                for i in range(NT):
                    plan.need(dve, ("left", i))
                    own(dve.tensor_tensor(own_part[:, i, :], own_part[:, i, :], bl[:, :], ALU.add))
                    own.wait()
                    bank = plan.take(dve, ("right", i))
                    plan.took(("right", i), dve.tensor_tensor(own_part[:, i, :], own_part[:, i, :], bank[:, :], ALU.add))
                    plan.need(dve, ("right", i))
                    own(dve.scalar_tensor_tensor(k.x[:, i, :], own_part[:, i, :], 0.0, k.x[:, i, :], ALU.max, ALU.add))


TWO_PI_PARTS = (6.28125, 0.0019353071795864769 - 3.0199159819567e-07, 3.0199159819567e-07)
ROUND = 1.5 * 2.0 ** 23


def condition(nc, k):
    ctx = ExitStack()
    with ctx:
        sb, pb, sem = scope(ctx, nc, "cond")
        noise, ph, turns = sb("noise", [EMB, NP]), sb("ph", [EMB, NP]), sb("turns", [EMB, NP])
        emb = sb("emb", [EMB, NP])
        consts = sb("consts", [EMB, 3])
        f1, f2, fb = sb("f1", [EMB, COND]), sb("f2", [COND, COND]), sb("fb", [COND, 2])
        z, e = sb("z", [COND, NP]), sb("e", [COND, NP])
        ps = [pb(f"cp{i}", [COND, HALF]) for i in range(4)]
        loaded = sem("loaded")
        vec, angle_ready, emb_ready, hidden_ready, z_ready, e_ready, silu_ready, out_ready = (
            sem(n) for n in ("vec", "angle_ready", "emb_ready", "hidden_ready", "z_ready", "e_ready", "silu_ready", "out_ready"))
        with nc.Block() as block:
            @block.sync
            def _(sp):
                sp.dma_start(noise[:, :], k.dram["noise_rows"]).then_inc(loaded, 16)
                for dst, src in zip((consts, f1, f2, fb), (k.dram["angle_consts"], k.dram["f_w1"], k.dram["f_w2"], k.dram["f_b"])):
                    sp.dma_start(dst[:, :], src).then_inc(loaded, 16)

            @block.vector
            def _(dve):
                own = Count(dve, vec)

                def step(ins):
                    own(ins)
                    own.wait()

                step(dve.memset(k.condT[:, :], 0.0))
                own(dve.memset(k.condT[32:33, :], 1.0))
                dve.wait_ge(loaded, 16 * 5)
                step(dve.tensor_scalar(ph[:, :], noise[:, :], consts[:, 0:1], None, ALU.mult))
                step(dve.tensor_scalar(turns[:, :], ph[:, :], 0.15915494309189535, consts[:, 1:2], ALU.mult, ALU.add))
                step(dve.tensor_scalar(turns[:, :], turns[:, :], ROUND, None, ALU.add))
                step(dve.tensor_scalar(turns[:, :], turns[:, :], ROUND, None, ALU.subtract))
                for part in TWO_PI_PARTS:
                    step(dve.scalar_tensor_tensor(ph[:, :], turns[:, :], -part, ph[:, :], ALU.mult, ALU.add))
                step(dve.tensor_scalar(ph[:, :], ph[:, :], consts[:, 2:3], None, ALU.add))
                dve.tensor_scalar(ph[:, :], ph[:, :], 3.1415925, -3.1415925, ALU.min, ALU.max).then_inc(angle_ready, 1)
                for f in range(2):
                    dve.wait_ge(hidden_ready, f + 1)
                    dve.tensor_scalar(z[:, f * HALF:(f + 1) * HALF], ps[f][:, :], fb[:, 0:1], None,
                                      ALU.add).then_inc(z_ready, 1)
                dve.wait_ge(z_ready, 2)
                dve.wait_ge(e_ready, 1)
                step(dve.tensor_scalar(e[:, :], e[:, :], 1.0, None, ALU.add))
                step(dve.reciprocal(e[:, :], e[:, :]))
                dve.tensor_tensor(z[:, :], z[:, :], e[:, :], ALU.mult).then_inc(silu_ready, 1)
                for f in range(2):
                    dve.wait_ge(out_ready, f + 1)
                    own(dve.tensor_scalar(k.condT[0:COND, f * HALF:(f + 1) * HALF], ps[2 + f][:, :], fb[:, 1:2], None,
                                          ALU.add))

            @block.scalar
            def _(act):
                act.wait_ge(angle_ready, 1)
                act.activation(emb[:, :], ph[:, :], ACT.Sin).then_inc(emb_ready, 1)
                act.preload_act_table_set(LOG_AND_EXP)
                act.wait_ge(z_ready, 2)
                act.activation(e[:, :], z[:, :], ACT.Exp, scale=-1.0).then_inc(e_ready, 1)

            @block.tensor
            def _(pe):
                pe.wait_ge(emb_ready, 1)
                pe.wait_ge(loaded, 16 * 5)
                for f in range(2):
                    pe.matmul(ps[f][:, :], f1[:, :], emb[:, f * HALF:(f + 1) * HALF], start=True,
                              stop=True).then_inc(hidden_ready, 1)
                pe.wait_ge(silu_ready, 1)
                for f in range(2):
                    pe.matmul(ps[2 + f][:, :], f2[:, :], z[:, f * HALF:(f + 1) * HALF], start=True,
                              stop=True).then_inc(out_ready, 1)


def transformer_layer(nc, k):
    ctx = ExitStack()
    with ctx:
        sb, pb, sem = scope(ctx, nc, "tr")
        names = ("wq", "wk", "wv", "wo", "m1", "m2")
        w = {n: sb("w_" + n, [P, KF, D]) for n in names}
        cw = sb("cw", [CROWS, 4, D])
        rows = {n: sb("row_" + n, [P, D]) for n in ("bv", "bo", "mb2")}
        cb = sb("cb", [P, BLOCKS, 3, KF])
        r, y = sb("r", [P, NT, D]), sb("y", [P, NT, D])
        yT, qT, kT, v = sb("yT", [P, KF, NP]), sb("qT", [P, KF, NP]), sb("kT", [P, KF, NP]), sb("v", [P, NT, D])
        scores, probs = sb("scores", [P, 3, NP]), sb("probs", [P, 3, NP])
        probsT = [sb("probsT", [P, NT, NP]), k.C]
        hidT = qT
        oT = yT
        nmax, den = sb("nmax", [P, HEADS * NT]), sb("den", [P, HEADS * NT])
        st, mv = sb("st", [P, NT, 6]), sb("mv", [P, NT, 2])
        one = [pb(f"one{i}", [P, D]) for i in range(2)]
        two = [pb(f"two{i}", [P, 2, D]) for i in range(3)]
        loaded = {n: sem("loaded_" + n) for n in names + ("cw", "bv", "bo", "mb2", "cb")}
        vec, sca, var_ready, rstd_ready, h_ready, exp_ready, probs_ready, read1, bias_added, block_done = (
            sem(n) for n in ("vec", "sca", "var_ready", "rstd_ready", "h_ready", "exp_ready", "probs_ready",
                             "read1", "bias_added", "block_done"))
        cb_scaled = sem("cb_scaled")
        plan = Plan(sem("product_ready"), {"vec": sem("taken_vec"), "sca": sem("taken_sca")}, {"one": one, "two": two})
        N = HEADS * NT

        def norm_products(s):
            for i in range(NT):
                plan.add(("scale", s, i), "vec")
                plan.add(("shift", s, i), "vec")
            for i in range(NT):
                plan.add(("yT", s, i), "sca")

        norm_products(0)
        for name, by in (("q", "sca"), ("k", "vec")):
            for m in range(KF):
                for f in range(2):
                    plan.add((name, m, f), by)
        for i in range(NT):
            plan.add(("v", i), "vec")
        for n in range(N + 4):
            if n < N:
                plan.add(("S", n), "vec", "two")
            if 2 <= n < N + 2:
                plan.add(("T", n - 2), "sca", "two")
            if n >= 8 and (n - 8) % NT == 0:
                for f in range(2):
                    plan.add(("o", (n - 8) // NT, f), "sca")
        for i in range(NT):
            plan.add(("wo", i), "vec")
        norm_products(1)
        for m in range(KF):
            for f in range(2):
                plan.add(("m1", m, f), "sca")
        for i in range(NT):
            plan.add(("m2", i), "vec")

        with nc.Block() as block:
            @block.sync
            def _(sp):
                def load(name, b):
                    if name == "cw":
                        dst, src = cw[:, :, :], k.dram["cond_w"][bass.ds(b, 1)].rearrange("o p a n -> p (o a) n")
                    elif name in rows:
                        dst = rows[name][:, :]
                        src = row_biases[name][bass.ds(b, 1), :].to_broadcast([P, D])
                    else:
                        dst = w[name][:, :, :]
                        src = mats[name].rearrange("b (c p) n -> b p c n", p=P)[bass.ds(b, 1)].rearrange("o p c n -> p (o c) n")
                    sp.dma_start(dst, src).then_inc(loaded[name], 16)

                mats = {"wq": k.dram["wq"], "wk": k.dram["wk"], "wv": k.dram["wv"], "wo": k.dram["wo"], "m1": k.dram["m1"], "m2": k.dram["m2"]}
                row_biases = {"bv": k.dram["bv"], "bo": k.dram["bo"], "mb2": k.dram["mb2"]}
                sp.dma_start(cb[:, :, :, :], k.dram["col_biases"].rearrange("p (b n c) -> p b n c", n=3, c=KF)).then_inc(loaded["cb"], 16)
                for name in ("cw", "wq", "wk", "wv", "bv", "bo", "wo", "m1", "m2", "mb2"):
                    load(name, 0)
                with sp.Fori(0, BLOCKS - 1) as b:
                    for name, key in (("wq", ("q", KF - 1, 1)), ("wk", ("k", KF - 1, 1)), ("wv", ("v", NT - 1)),
                                      ("bv", None), ("bo", None), ("wo", ("wo", NT - 1)), ("cw", ("shift", 1, NT - 1)),
                                      ("m1", ("m1", KF - 1, 1)), ("m2", ("m2", NT - 1)), ("mb2", None)):
                        if key:
                            plan.take(sp, key, b)
                        elif name == "bv":
                            plan.need(sp, ("v", NT - 1), b)
                        elif name == "bo":
                            sp.wait_ge(bias_added, b * 2 * NT + NT)
                        else:
                            sp.wait_ge(bias_added, b * 2 * NT + 2 * NT)
                        load(name, b + 1)

            @block.gpsimd
            def _(pool):
                with pool.Fori(0, BLOCKS) as b:
                    for s, name in enumerate(("bo", "mb2")):
                        pool.wait_ge(loaded[name], b * 16 + 16)
                        for i in range(NT):
                            pool.wait_ge(read1, b * (2 * NT) + (s * NT + i + 1))
                            pool.tensor_tensor(r[:, i, :], r[:, i, :], rows[name][:, :], ALU.add).then_inc(bias_added, 1)

            @block.tensor
            def _(pe):
                def norm(s, b):
                    if s == 0:
                        pe.wait_ge(loaded["cw"], b * 16 + 16)
                    for i in range(NT):
                        for key, c in (("scale", 0), ("shift", 1)):
                            bank = plan.open(pe, (key, s, i), b)
                            plan.made(pe.matmul(bank[:, :], k.condT[:, i * P:(i + 1) * P], cw[:, 2 * s + c, :],
                                                start=True, stop=True))
                    for i in range(NT):
                        bank = plan.open(pe, ("yT", s, i), b)
                        plan.need(pe, ("shift", s, i), b)
                        plan.made(turn(pe, bank, y[:, i, :], k.ident[:, :]))

                def by_feature(name, wts, src, b):
                    for m in range(KF):
                        for f in range(2):
                            bank = plan.open(pe, (name, m, f), b)
                            plan.made(chain(pe, bank[:, 0:HALF], [(wts[:, c, m * P:(m + 1) * P],
                                      src[:, c, f * HALF:(f + 1) * HALF]) for c in range(KF)]))

                def by_node(name, wts, src, b):
                    for i in range(NT):
                        bank = plan.open(pe, (name, i), b)
                        plan.made(chain(pe, bank[:, :], [(src[:, c, i * P:(i + 1) * P], wts[:, c, :]) for c in range(KF)]))

                pe.sem_inc(block_done, 1)
                with pe.Fori(0, BLOCKS) as b:
                    pe.wait_ge(block_done, b + 1)
                    norm(0, b)
                    plan.need(pe, ("yT", 0, NT - 1), b)
                    pe.wait_ge(loaded["wq"], b * 16 + 16)
                    by_feature("q", w["wq"], yT, b)
                    pe.wait_ge(loaded["wk"], b * 16 + 16)
                    by_feature("k", w["wk"], yT, b)
                    pe.wait_ge(loaded["wv"], b * 16 + 16)
                    by_node("v", w["wv"], yT, b)
                    for n in range(N + 4):
                        if n < N:
                            h, i = divmod(n, NT)
                            bank = plan.open(pe, ("S", n), b)
                            if i == 0:
                                plan.need(pe, ("q", h, 1), b)
                                plan.need(pe, ("k", h, 1), b)
                            for f in range(2):
                                mm = pe.matmul(bank[:, f, 0:HALF], qT[:, h, i * P:(i + 1) * P],
                                               kT[:, h, f * HALF:(f + 1) * HALF], start=True, stop=True)
                            plan.made(mm)
                        if 2 <= n < N + 2:
                            bank = plan.open(pe, ("T", n - 2), b)
                            pe.wait_ge(probs_ready, b * N + (n - 1))
                            flat = bank[:, :, :].rearrange("p a b -> p (a b)")
                            for j in range(NT):
                                mm = pe.transpose(flat[:, j * P:(j + 1) * P], probs[:, (n - 2) % 3, j * P:(j + 1) * P],
                                                  k.ident[:, :])
                            plan.made(mm)
                        if n >= 8 and (n - 8) % NT == 0:
                            h = (n - 8) // NT
                            plan.need(pe, ("T", h * NT + NT - 1), b)
                            if h == 0:
                                plan.need(pe, ("v", NT - 1), b)
                            for f in range(2):
                                bank = plan.open(pe, ("o", h, f), b)
                                plan.made(chain(pe, bank[:, 0:HALF], [(v[:, j, h * DH:(h + 1) * DH],
                                          probsT[h % 2][:, j, f * HALF:(f + 1) * HALF]) for j in range(NT)]))
                    plan.need(pe, ("o", HEADS - 1, 1), b)
                    pe.wait_ge(loaded["wo"], b * 16 + 16)
                    by_node("wo", w["wo"], oT, b)
                    norm(1, b)
                    plan.need(pe, ("yT", 1, NT - 1), b)
                    pe.wait_ge(loaded["m1"], b * 16 + 16)
                    by_feature("m1", w["m1"], yT, b)
                    plan.need(pe, ("m1", KF - 1, 1), b)
                    pe.wait_ge(loaded["m2"], b * 16 + 16)
                    by_node("m2", w["m2"], hidT, b)

            @block.scalar
            def _(act):
                act.preload_act_table_set(LOG_AND_EXP)
                first = Count(act, sca)
                act.wait_ge(var_ready, 1)
                inverse_root(act, k, first, rstd_ready)
                act.wait_ge(cb_scaled, 1)

                with act.Fori(0, BLOCKS) as b:
                    own = Count(act, sca, 1, b, 2)

                    def norm(s):
                        act.wait_ge(var_ready, b * 2 + (s + 2))
                        inverse_root(act, k, own, rstd_ready)
                        for i in range(NT):
                            bank = plan.take(act, ("yT", s, i), b)
                            plan.took(("yT", s, i), act.activation(yT[:, :, i * P:(i + 1) * P], cols(bank[:, :], P), ACT.Copy))

                    def bias_of(which, m):
                        return cb[:, bass.ds(b, 1), which, m]

                    norm(0)
                    for m in range(KF):
                        for f in range(2):
                            bank = plan.take(act, ("q", m, f), b)
                            settle(k, act)
                            plan.took(("q", m, f), act.activation(qT[:, m, f * HALF:(f + 1) * HALF], bank[:, 0:HALF],
                                                                  ACT.Identity, bias=bias_of(0, m), scale=DH ** -0.5))
                    for n in range(N + 4):
                        if n < N:
                            plan.need(act, ("S", n), b)
                            act.activation(probs[:, n % 3, :], scores[:, n % 3, :], ACT.Exp, bias=nmax[:, n:n + 1],
                                           scale=-1.0, accum_out=den[:, n:n + 1]).then_inc(exp_ready, 1)
                        if 2 <= n < N + 2:
                            h, i = divmod(n - 2, NT)
                            bank = plan.take(act, ("T", n - 2), b)
                            flat = bank[:, :, :].rearrange("p a b -> p (a b)")
                            plan.took(("T", n - 2), act.activation(probsT[h % 2][:, :, i * P:(i + 1) * P],
                                                                   cols(flat[:, 0:NP], P), ACT.Copy))
                        if n >= 8 and (n - 8) % NT == 0:
                            h = (n - 8) // NT
                            for f in range(2):
                                bank = plan.take(act, ("o", h, f), b)
                                plan.took(("o", h, f), act.activation(oT[:, h, f * HALF:(f + 1) * HALF],
                                                                      bank[:, 0:HALF], ACT.Copy))
                    norm(1)
                    for m in range(KF):
                        for f in range(2):
                            bank = plan.take(act, ("m1", m, f), b)
                            settle(k, act)
                            plan.took(("m1", m, f), act.activation(hidT[:, m, f * HALF:(f + 1) * HALF], bank[:, 0:HALF],
                                                                   ACT.Relu, bias=bias_of(2, m)))

            @block.vector
            def _(dve):
                first = Count(dve, vec)
                layernorm_relu(nc, k, k.x, r, st, mv, var_ready, rstd_ready, h_ready, first, dve)
                dve.wait_ge(loaded["cb"], 16)
                dve.tensor_scalar(cb[:, :, 0, :], cb[:, :, 0, :], DH ** -0.5, None, ALU.mult).then_inc(cb_scaled, 1)
                dve.wait_ge(cb_scaled, 1)
                dve.wait_ge(h_ready, NT)

                with dve.Fori(0, BLOCKS) as b:
                    own = Count(dve, vec, first.n, b, 4 * NT + N)

                    def norm(s):
                        for i in range(NT):
                            own(dve.bn_stats(st[:, i, :], r[:, i, :]))
                        own.wait()
                        settle(k, dve)
                        for i in range(NT):
                            own(dve.bn_aggr(mv[:, i, :], st[:, i, :]))
                        own.wait()
                        dve.tensor_scalar(k.rstd[:, :], mv[:, :, 1], EPS, None, ALU.add).then_inc(var_ready, 1)
                        dve.wait_ge(rstd_ready, b * 2 + (s + 2))
                        for i in range(NT):
                            dve.tensor_scalar(y[:, i, :], r[:, i, :], mv[:, i, 0:1], k.rstd[:, i:i + 1],
                                              ALU.subtract, ALU.mult).then_inc(read1, 1)
                        dve.wait_ge(read1, b * (2 * NT) + (s + 1) * NT)
                        for i in range(NT):
                            bank = plan.take(dve, ("scale", s, i), b)
                            plan.took(("scale", s, i), dve.scalar_tensor_tensor(y[:, i, :], bank[:, :], 1.0, y[:, i, :],
                                                                                ALU.add, ALU.mult))
                            bank = plan.take(dve, ("shift", s, i), b)
                            plan.need(dve, ("scale", s, i), b)
                            plan.took(("shift", s, i), dve.tensor_tensor(y[:, i, :], y[:, i, :], bank[:, :], ALU.add))

                    def residual(name, s):
                        for i in range(NT):
                            dve.wait_ge(bias_added, b * (2 * NT) + (s * NT + i + 1))
                            bank = plan.take(dve, (name, i), b)
                            plan.took((name, i), dve.tensor_tensor(r[:, i, :], r[:, i, :], bank[:, :], ALU.add))
                        plan.need(dve, (name, NT - 1), b)

                    norm(0)
                    for m in range(KF):
                        for f in range(2):
                            bank = plan.take(dve, ("k", m, f), b)
                            plan.took(("k", m, f), dve.tensor_scalar(kT[:, m, f * HALF:(f + 1) * HALF], bank[:, 0:HALF],
                                                                     cb[:, bass.ds(b, 1), 1, m], None, ALU.add))
                    dve.wait_ge(loaded["bv"], b * 16 + 16)
                    for i in range(NT):
                        bank = plan.take(dve, ("v", i), b)
                        plan.took(("v", i), dve.tensor_tensor(v[:, i, :], bank[:, :], rows["bv"][:, :], ALU.add))
                    for n in range(N + 1):
                        if n < N:
                            i = n % NT
                            bank = plan.take(dve, ("S", n), b)
                            settle(k, dve)
                            ins = dve.tensor_tensor_reduce(out=cols(scores[:, n % 3, :], HALF), in0=bank[:, :, 0:HALF],
                                                           in1=cols(k.logc[:, i, :], HALF), scale=-1.0, scalar=3.0e38,
                                                           op0=ALU.add, op1=ALU.min, accum_out=nmax[:, n:n + 1])
                            plan.took(("S", n), ins)
                        if n >= 1:
                            m = n - 1
                            dve.wait_ge(exp_ready, b * N + (m + 1))
                            own(dve.reciprocal(den[:, m:m + 1], den[:, m:m + 1]))
                            own.wait()
                            dve.tensor_scalar(probs[:, m % 3, :], probs[:, m % 3, :], den[:, m:m + 1],
                                              k.has[:, m % NT:m % NT + 1], ALU.mult, ALU.mult).then_inc(probs_ready, 1)
                    residual("wo", 0)
                    norm(1)
                    residual("m2", 1)
                    dve.sem_inc(block_done, 1)
                for i in range(NT):
                    dve.tensor_tensor(k.x[:, i, :], k.x[:, i, :], r[:, i, :], ALU.add).then_inc(h_ready, 1)


def gcn_layer(nc, k):
    ctx = ExitStack()
    with ctx:
        sb, pb, sem = scope(ctx, nc, "gcn")
        wt, lb = sb("wt", [P, KF, D]), sb("lb", [P, D])
        h, aggT = sb("h", [P, NT, D]), sb("aggT", [P, KF, NP])
        st, mv = sb("st", [P, NT, 6]), sb("mv", [P, NT, 2])
        ps = [pb(f"p{i}", [P, D]) for i in range(8)]
        loaded_wt, loaded_lb = sem("loaded_wt"), sem("loaded_lb")
        vec, sca, var_ready, rstd_ready, h_ready, scaled = (
            sem(n) for n in ("vec", "sca", "var_ready", "rstd_ready", "h_ready", "scaled"))
        plan = Plan(sem("product_ready"), {"vec": sem("taken_vec"), "sca": sem("taken_sca")}, {"one": ps})
        for m in range(KF):
            for f in range(2):
                plan.add(("agg", m, f), "sca")
        for i in range(NT):
            plan.add(("lin", i), "vec")

        with nc.Block() as block:
            @block.sync
            def _(sp):
                sp.dma_start(wt[:, :, :], k.dram["lin_w"].rearrange("(c p) n -> p c n", p=P)).then_inc(loaded_wt, 16)
                sp.dma_start(lb[:, :], k.dram["lin_b"][None, :].to_broadcast([P, D])).then_inc(loaded_lb, 16)

            @block.scalar
            def _(act):
                act.preload_act_table_set(LOG_AND_EXP)
                own = Count(act, sca)
                act.wait_ge(var_ready, 1)
                inverse_root(act, k, own, rstd_ready)
                for m in range(KF):
                    for f in range(2):
                        bank = plan.take(act, ("agg", m, f))
                        plan.took(("agg", m, f), act.activation(aggT[:, m, f * HALF:(f + 1) * HALF], bank[:, 0:HALF], ACT.Copy))

            @block.tensor
            def _(pe):
                pe.wait_ge(scaled, NT)
                for m in range(KF):
                    for f in range(2):
                        bank = plan.open(pe, ("agg", m, f))
                        plan.made(chain(pe, bank[:, 0:HALF], [(h[:, i, m * P:(m + 1) * P],
                                  k.W[:, i, f * HALF:(f + 1) * HALF]) for i in range(NT)]))
                pe.wait_ge(loaded_wt, 16)
                for i in range(NT):
                    bank = plan.open(pe, ("lin", i))
                    if i == 0:
                        plan.need(pe, ("agg", KF - 1, 1))
                    plan.made(chain(pe, bank[:, :], [(aggT[:, c, i * P:(i + 1) * P], wt[:, c, :]) for c in range(KF)]))

            @block.vector
            def _(dve):
                own = Count(dve, vec)
                layernorm_relu(nc, k, k.x, h, st, mv, var_ready, rstd_ready, h_ready, own, dve)
                dve.wait_ge(h_ready, NT)
                for i in range(NT):
                    dve.tensor_scalar(h[:, i, :], h[:, i, :], k.dis[:, i:i + 1], None, ALU.mult).then_inc(scaled, 1)
                dve.wait_ge(loaded_lb, 16)
                for i in range(NT):
                    own(dve.tensor_tensor(k.x[:, i, :], k.x[:, i, :], lb[:, :], ALU.add))
                own.wait()
                for i in range(NT):
                    bank = plan.take(dve, ("lin", i))
                    plan.took(("lin", i), dve.scalar_tensor_tensor(k.x[:, i, :], bank[:, :], k.dis[:, i:i + 1],
                                                                   k.x[:, i, :], ALU.mult, ALU.add))


class Mish:

    def __init__(self, z, e, n, out):
        self.z, self.e, self.n, self.out = z, e, n, out

    def cap(self, dve):
        return dve.tensor_scalar(self.e, self.z, CAP, None, ALU.min)

    def exp(self, act):
        return act.activation(self.e, self.e, ACT.Exp)

    def square(self, dve):
        return dve.scalar_tensor_tensor(self.n, self.e, 2.0, self.e, ALU.add, ALU.mult)

    def log(self, act):
        return act.activation(self.n, self.n, ACT.Ln, bias=1.0, scale=0.5)

    def quotient(self, act):
        return act.activation(self.n, self.n, ACT.Exp, scale=-1.0)

    def product(self, dve):
        return dve.scalar_tensor_tensor(self.out, self.n, 1.0, self.z, ALU.subtract, ALU.mult, reverse0=True)


def edge_layer_tables(nc, k):
    ctx = ExitStack()
    with ctx:
        sb, pb, sem = scope(ctx, nc, "tab")
        ws, wd, b1 = sb("ws", [P, KF, D]), sb("wd", [P, KF, D]), sb("b1", [P, D])
        tables = {"src": sb("ts", [P, NT, D]), "dst": sb("td", [P, NT, D])}
        zero = sb("zero", [WIN, D])
        st, mv = sb("st", [P, NT, 6]), sb("mv", [P, NT, 2])
        ps = [pb(f"p{i}", [P, D]) for i in range(8)]
        loaded = {n: sem("loaded_" + n) for n in ("src", "dst", "b1")}
        stored = sem("stored")
        zeroed = sem("zeroed")
        vec, sca, var_ready, rstd_ready, h_ready = (
            sem(n) for n in ("vec", "sca", "var_ready", "rstd_ready", "h_ready"))
        plan = Plan(sem("product_ready"), {"vec": sem("taken_vec"), "sca": sem("taken_sca")}, {"one": ps})
        for i in range(NT):
            plan.add(("hT", i), "sca")
        for name in ("src", "dst"):
            for i in range(NT):
                plan.add((name, i), "vec")

        with nc.Block() as block:
            @block.sync
            def _(sp):
                w1 = k.dram["w1"][0:2 * D, :].rearrange("(c p) n -> p c n", p=P)
                sp.dma_start(ws[:, :, :], w1[:, 0:KF, :]).then_inc(loaded["src"], 16)
                sp.dma_start(wd[:, :, :], w1[:, KF:2 * KF, :]).then_inc(loaded["dst"], 16)
                sp.dma_start(b1[:, :], k.dram["b1"][None, :].to_broadcast([P, D])).then_inc(loaded["b1"], 16)
                sp.wait_ge(zeroed, 1)
                sp.dma_start(k.dst_table[NP:NP + WIN, :], zero[:, :]).then_inc(stored, 16)
                for name, out in (("src", k.src_table), ("dst", k.dst_table[0:NP, :])):
                    plan.need(sp, (name, NT - 1))
                    sp.dma_start(out.rearrange("(i p) d -> p i d", p=P), tables[name][:, :, :]).then_inc(stored, 16)
                sp.wait_ge(stored, 16 * 3)

            @block.scalar
            def _(act):
                act.preload_act_table_set(LOG_AND_EXP)
                own = Count(act, sca)
                act.wait_ge(var_ready, 1)
                inverse_root(act, k, own, rstd_ready)
                for i in range(NT):
                    bank = plan.take(act, ("hT", i))
                    plan.took(("hT", i), act.activation(k.hT[:, :, i * P:(i + 1) * P], cols(bank[:, :], P), ACT.Copy))

            @block.tensor
            def _(pe):
                for i in range(NT):
                    bank = plan.open(pe, ("hT", i))
                    pe.wait_ge(h_ready, i + 1)
                    plan.made(turn(pe, bank, k.h[:, i, :], k.ident[:, :]))
                for name, w in (("src", ws), ("dst", wd)):
                    pe.wait_ge(loaded[name], 16)
                    for i in range(NT):
                        bank = plan.open(pe, (name, i))
                        plan.need(pe, ("hT", i))
                        plan.made(chain(pe, bank[:, :], [(k.hT[:, c, i * P:(i + 1) * P], w[:, c, :]) for c in range(KF)]))

            @block.vector
            def _(dve):
                own = Count(dve, vec)
                dve.memset(zero[:, :], 0.0).then_inc(zeroed, 1)
                layernorm_relu(nc, k, k.x, k.h, st, mv, var_ready, rstd_ready, h_ready, own, dve)
                dve.wait_ge(loaded["b1"], 16)
                for name in ("src", "dst"):
                    for i in range(NT):
                        bank = plan.take(dve, (name, i))
                        dst = tables[name][:, i, :]
                        plan.took((name, i), dve.tensor_copy(dst, bank[:, :]) if name == "src" else
                                  dve.tensor_tensor(dst, bank[:, :], b1[:, :], ALU.add))


def edge_messages(nc, k):
    PT = 2
    EDGE = PT * P
    RING = 4
    PARTS = 3
    LASTROW = 32 * (PARTS - 1) + 1
    ctx = ExitStack()
    with ctx:
        sb, pb, sem = scope(ctx, nc, "edge")
        w2, b2, rest = sb("w2", [P, KF, D]), sb("b2", [P, D]), sb("rest", [P, D])
        w2_hi, w2_lo = sb("w2_hi", [P, KF, D], F32R), sb("w2_lo", [P, KF, D], F32R)
        bias = sb("bias", [P, D], BF16)
        part = [sb(f"part{n}", [P, D], BF16) for n in range(PARTS)]
        ones16 = sb("ones16", [P, P], BF16)
        iota_i, iota = sb("iota_i", [P, WIDE], I32), sb("iota", [P, WIDE])
        row_i, row = sb("row_i", [P, 1], I32), sb("row", [P, 1])
        USES = (MAXSWEEPS + 1) * GROUPS
        starts_f, window_node = sb("starts_f", [1, USES]), sb("window_node", [P, USES])
        terms_w = [sb(f"terms_w{a}", [P, D]) for a in range(2)]
        terms = [sb(f"terms{a}", [P, GROUP]) for a in range(2)]
        dst_row = [sb(f"dst_row{a}", [P, GROUP], I32) for a in range(2)]
        index = [sb(f"index{a}", [P, PT], I32) for a in range(RING)]
        from_rows = [sb(f"from_rows{a}", [P, PT, D]) for a in range(RING)]
        m1, z2, m2, h2 = ([sb(f"{n}{a}", [P, PT * D]) for a in range(2)] for n in ("m1", "z2", "m2", "h2"))
        h1_hi, h1_lo = ([sb(f"{n}{a}", [P, KF, EDGE], F32R) for a in range(2)] for n in ("h1_hi", "h1_lo"))
        onehot = [sb(f"onehot{a}", [P, PT, WIN]) for a in range(2)]
        ps_z1 = [pb(f"z1p{a}", [P, KF * EDGE]) for a in range(2)]
        ps_z2 = pb("z2p", [P, PT * D])
        ps_sum = [pb(f"sump{a}", [P, D]) for a in range(2)]
        S = {n: sem(n) for n in (
            "loaded_w2", "loaded_b2", "loaded_w1a", "vec", "made", "starts_ready", "starts_spread", "weights_cut",
            "index_ready", "turned", "z1_made", "terms_ready", "capped1", "e1_ready", "n1_ready", "log1_ready", "q1_ready",
            "h1_ready", "hi_ready", "lo_ready", "z2_made", "z2_ready", "capped2", "e2_ready", "n2_ready", "log2_ready",
            "q2_ready", "h2_ready", "onehot_ready", "pair_summed", "added")}
        from_loaded = [sem(f"from_loaded{a}") for a in range(RING)]
        attr_loaded, window_loaded, dst_row_loaded = (
            [sem(f"{n}{a}") for a in range(2)] for n in ("attr_loaded", "window_loaded", "dst_row_loaded"))
        mish1 = [Mish(ps_z1[a][:, :], m1[a][:, :], m1[a][:, :], m1[a][:, :]) for a in range(2)]
        mish2 = [Mish(z2[a][:, :], m2[a][:, :], m2[a][:, :], h2[a][:, :]) for a in range(2)]
        PAIRS = GROUPS * TPG // PT
        DEPTH = 4
        low, high = slice(0, EATTR), slice(EATTR, P)

        def sweeps(eng):
            return eng.value_load(k.sweeps[0:1, 0:1], min_val=0, max_val=MAXSWEEPS - 1)

        def run_steps(eng, step):
            n = sweeps(eng)
            for a in range(DEPTH):
                step(lambda add: a + add, lambda lag: (a - lag) // 2, a, lambda lag: lag <= a)
            with eng.Fori(0, n * (PAIRS // 4) + (PAIRS - DEPTH) // 4) as t:
                for a in range(4):
                    step(lambda add: t * 4 + (a + DEPTH + add), lambda lag: t * 2 + (a + DEPTH - lag) // 2, a,
                         lambda lag: True)
            for a in range(DEPTH):
                step(lambda add: n * PAIRS + (PAIRS + a + add), lambda lag: n * GROUPS + (GROUPS + (a - lag) // 2), a,
                     lambda lag: lag > a)

        with nc.Block() as block:
            @block.sync
            def _(sp):
                sp.dma_start(w2[:, :, :], k.dram["w2"].rearrange("(c p) n -> p c n", p=P)).then_inc(S["loaded_w2"], 16)
                sp.dma_start(b2[:, :], k.dram["b2"][None, :].to_broadcast([P, D])).then_inc(S["loaded_b2"], 16)
                for a in range(2):
                    sp.dma_start(terms_w[a][low, :], k.dram["w1"][2 * D:2 * D + EATTR, :]).then_inc(S["loaded_w1a"], 16)

                def step(s, g, a, on):
                    if a % 2 == 0 and on(0):
                        slot, u = a // 2, g(0)
                        o = u % GROUPS
                        if on(4):
                            sp.wait_ge(S["terms_ready"], g(2))
                        sp.dma_start(dst_row[slot][high, :], k.dram["dst_rows"][bass.ds(o, 1)].to_broadcast([WIN, GROUP])
                                     ).then_inc(dst_row_loaded[slot], 16)
                        if on(4):
                            sp.wait_ge(S["z1_made"], s(-2))
                        start = sp.value_load(k.starts[0:1, bass.ds(u, 1)], min_val=0, max_val=NP)
                        sp.dma_start(terms_w[slot][high, :], k.dst_table[bass.ds(start, WIN), :]).then_inc(window_loaded[slot], 16)
                        sp.dma_start(terms[slot][low, :], k.dram["attr_T"][:, bass.ds(o * GROUP, GROUP)]
                                     ).then_inc(attr_loaded[slot], 16)

                run_steps(sp, step)

            @block.gpsimd
            def _(pool):
                pool.iota(iota_i[:, :], pattern=[[1, WIDE]], base=0, channel_multiplier=0).then_inc(S["made"], 1)
                pool.iota(row_i[:, :], pattern=[[0, 1]], base=-EATTR, channel_multiplier=1).then_inc(S["made"], 1)
                pool.memset(k.aggT[:, :, :], 0.0).then_inc(S["made"], 1)

                def step(s, g, a, on):
                    if on(0):
                        if on(4):
                            pool.wait_ge(S["turned"], s(-3))
                            settle(k, pool)
                        tile0 = (s(0) % PAIRS) * PT
                        pool.tensor_copy(index[a][:, :], k.src_i[:, bass.ds(tile0, PT)]).then_inc(S["index_ready"], 1)
                        pool.wait_ge(S["index_ready"], s(1))
                        settle(k, pool)
                        for j in range(PT):
                            pool.indirect_dma_start(
                                out=from_rows[a][:, j, :], out_offset=None, in_=k.src_table,
                                in_offset=bass.IndirectOffsetOnAxis(ap=index[a][:, j:j + 1], axis=0)
                            ).then_inc(from_loaded[a], 16)
                    if on(3):
                        b = (a - 3) % 2
                        pool.wait_ge(S["hi_ready"], s(-2))
                        pool.tensor_tensor(h1_lo[b][:, :, :], cols(m1[b][:, :], EDGE), h1_hi[b][:, :, :].bitcast(F32),
                                           ALU.subtract).then_inc(S["lo_ready"], 1)

                run_steps(pool, step)

            @block.tensor
            def _(pe):
                pe.wait_ge(S["starts_ready"], 1)
                pe.matmul(ps_z2[:, 0:USES], k.ones[0:1, :], starts_f[:, :], start=True, stop=True).then_inc(S["starts_spread"], 1)
                pe.wait_ge(S["weights_cut"], 1)
                pe.wait_ge(S["loaded_w1a"], 32)

                def step(s, g, a, on):
                    b = a % 2
                    if on(2):
                        pe.wait_ge(S["hi_ready"], s(-1))
                        pe.wait_ge(S["lo_ready"], s(-1))
                        if on(3):
                            pe.wait_ge(S["z2_ready"], s(-2))
                        for j in range(PT):
                            out, tile = ps_z2[:, j * D:(j + 1) * D], slice(j * P, (j + 1) * P)
                            terms2 = [(ones16[0:LASTROW, :], bias[0:LASTROW, :])]
                            for c in range(KF):
                                hi, lo = h1_hi[b][:, c, tile], h1_lo[b][:, c, tile]
                                terms2 += [(hi, w2_hi[:, c, :]), (hi, w2_lo[:, c, :]), (lo, w2_hi[:, c, :])]
                            mm = chain(pe, out, terms2)
                        mm.then_inc(S["z2_made"], 1)
                    if on(4):
                        slot = a // 2
                        pe.wait_ge(S["h2_ready"], s(-1))
                        pe.wait_ge(S["onehot_ready"], s(-3) * PT)
                        if b == 0:
                            pe.wait_ge(S["added"], g(2))
                        for c in range(KF):
                            for j in range(PT):
                                mm = pe.matmul(ps_sum[slot][:, c * WIN:(c + 1) * WIN], h2[b][:, j * D + c * P:j * D + (c + 1) * P],
                                               onehot[b][:, j, :], start=(b == 0 and c == 0 and j == 0),
                                               stop=(b == 1 and c == KF - 1 and j == PT - 1))
                        mm.then_inc(S["pair_summed"], 1)
                    if on(0):
                        pe.wait_ge(from_loaded[a], s(0) // RING * (16 * PT) + 16 * PT)
                        if on(2):
                            pe.wait_ge(S["h1_ready"], s(-1))
                        z1 = cols(ps_z1[b][:, :], EDGE)
                        for c in range(KF):
                            for j in range(PT):
                                mm = pe.matmul(z1[:, c, j * P:(j + 1) * P], from_rows[a][:, j, c * P:(c + 1) * P],
                                               k.ident[:, :], is_transpose=True, start=(c % 2 == 0 and j == 0), stop=False)
                        mm.then_inc(S["turned"], 1)
                        slot = a // 2
                        if b == 0:
                            pe.wait_ge(attr_loaded[slot], g(0) // 2 * 16 + 16)
                            pe.wait_ge(window_loaded[slot], g(0) // 2 * 16 + 16)
                            pe.wait_ge(S["terms_ready"], g(-2))
                        for c in range(KF):
                            mm = pe.matmul(z1[:, c, :], terms_w[slot][:, c * P:(c + 1) * P],
                                           terms[slot][:, b * EDGE:(b + 1) * EDGE], start=False, stop=(c % 2 == 1))
                        mm.then_inc(S["z1_made"], 1)

                run_steps(pe, step)

            @block.scalar
            def _(act):
                act.preload_act_table_set(LOG_AND_EXP)

                def step(s, g, a, on):
                    b = (a - 1) % 2
                    if on(3):
                        act.wait_ge(S["z2_made"], s(-2))
                        act.wait_ge(S["h2_ready"], s(-2))
                        act.activation(z2[b][:, :], ps_z2[:, :], ACT.Copy).then_inc(S["z2_ready"], 1)
                    if on(1):
                        act.wait_ge(S["capped1"], s(0))
                        mish1[b].exp(act).then_inc(S["e1_ready"], 1)
                    if on(3):
                        act.wait_ge(S["capped2"], s(-2))
                        mish2[b].exp(act).then_inc(S["e2_ready"], 1)
                    if on(1):
                        act.wait_ge(S["n1_ready"], s(0))
                        mish1[b].log(act).then_inc(S["log1_ready"], 1)
                        act.wait_ge(S["log1_ready"], s(0))
                        mish1[b].quotient(act).then_inc(S["q1_ready"], 1)
                    if on(3):
                        act.wait_ge(S["n2_ready"], s(-2))
                        mish2[b].log(act).then_inc(S["log2_ready"], 1)
                        act.wait_ge(S["log2_ready"], s(-2))
                        mish2[b].quotient(act).then_inc(S["q2_ready"], 1)

                run_steps(act, step)

            @block.vector
            def _(dve):
                own = Count(dve, S["vec"])
                dve.sem_inc(S["h2_ready"], 2)
                dve.sem_inc(S["pair_summed"], 2)
                dve.sem_inc(S["added"], 2)
                dve.tensor_copy(starts_f[:, :], k.starts[:, :]).then_inc(S["starts_ready"], 1)
                dve.wait_ge(S["made"], 3)
                own(dve.tensor_copy(iota[:, :], iota_i[:, :]))
                own(dve.tensor_copy(row[:, :], row_i[:, :]))
                own(dve.memset(ones16[:, :], 1.0))
                own(dve.memset(bias[:, :], 0.0))
                own.wait()
                dve.wait_ge(S["starts_spread"], 1)
                own(dve.tensor_scalar(window_node[:, :], ps_z2[:, 0:USES], row[:, 0:1], None, ALU.add))
                dve.wait_ge(S["loaded_b2"], 16)
                for n in range(PARTS):
                    source = b2 if n == 0 else rest
                    own(dve.tensor_copy(part[n][:, :], source[:, :]))
                    own.wait()
                    own(dve.tensor_tensor(rest[:, :], source[:, :], part[n][:, :], ALU.subtract))
                    own(dve.tensor_copy(bias[32 * n:32 * n + 1, :], part[n][32 * n:32 * n + 1, :]))
                    own.wait()
                dve.wait_ge(S["loaded_w2"], 16)
                own(dve.tensor_copy(w2_hi[:, :, :], w2[:, :, :]))
                own.wait()
                dve.tensor_tensor(w2_lo[:, :, :], w2[:, :, :], w2_hi[:, :, :].bitcast(F32),
                                  ALU.subtract).then_inc(S["weights_cut"], 1)

                def step(s, g, a, on):
                    b = (a - 1) % 2
                    if a % 2 == 0 and on(0):
                        slot = a // 2
                        dve.wait_ge(dst_row_loaded[slot], g(0) // 2 * 16 + 16)
                        if on(4):
                            dve.wait_ge(S["z1_made"], s(-2))
                        dve.tensor_scalar(terms[slot][high, :], dst_row[slot][high, :], window_node[high, bass.ds(g(0), 1)],
                                          None, ALU.is_equal).then_inc(S["terms_ready"], 1)
                    if on(1):
                        dve.wait_ge(S["z1_made"], s(0))
                        mish1[b].cap(dve).then_inc(S["capped1"], 1)
                    if on(3):
                        dve.wait_ge(S["z2_ready"], s(-2))
                        mish2[b].cap(dve).then_inc(S["capped2"], 1)
                        start = dve.value_load(k.starts[0:1, bass.ds(g(3), 1)], min_val=0, max_val=NP)
                        tile0 = (s(-3) % PAIRS) * PT
                        dve.wait_ge(S["pair_summed"], s(-2))
                        for j in range(PT):
                            dve.tensor_scalar(onehot[b][:, j, :], iota[:, bass.ds(start, WIN)],
                                              k.dst_f[:, bass.ds(tile0 + j, 1)], None,
                                              ALU.is_equal).then_inc(S["onehot_ready"], 1)
                    if on(1):
                        dve.wait_ge(S["e1_ready"], s(0))
                        mish1[b].square(dve).then_inc(S["n1_ready"], 1)
                    if on(3):
                        dve.wait_ge(S["e2_ready"], s(-2))
                        mish2[b].square(dve).then_inc(S["n2_ready"], 1)
                    if on(1):
                        dve.wait_ge(S["q1_ready"], s(0))
                        mish1[b].product(dve).then_inc(S["h1_ready"], 1)
                        dve.wait_ge(S["h1_ready"], s(0))
                        if on(3):
                            dve.wait_ge(S["z2_made"], s(-2))
                        dve.tensor_copy(h1_hi[b][:, :, :], cols(m1[b][:, :], EDGE)).then_inc(S["hi_ready"], 1)
                    if on(3):
                        dve.wait_ge(S["q2_ready"], s(-2))
                        mish2[b].product(dve).then_inc(S["h2_ready"], 1)
                    if on(4) and a % 2 == 1:
                        start = dve.value_load(k.starts[0:1, bass.ds(g(4), 1)], min_val=0, max_val=NP)
                        dve.wait_ge(S["pair_summed"], s(-1))
                        dve.wait_ge(S["added"], g(0))
                        into = k.aggT[:, :, bass.ds(start, WIN)]
                        dve.tensor_tensor(into, into, cols(ps_sum[a // 2][:, 0:KF * WIN], WIN), ALU.add).then_inc(S["added"], 1)

                run_steps(dve, step)


def edge_layer_nodes(nc, k):
    ctx = ExitStack()
    with ctx:
        sb, pb, sem = scope(ctx, nc, "node")
        w3, w4 = sb("w3", [P, 2 * KF, D]), sb("w4", [P, KF, D])
        b3 = sb("b3", [P, KF])
        rows = {n: sb("row_" + n, [P, D]) for n in ("b4", "gamma", "beta")}
        z, e, n_, uT = sb("z", [P, KF, NP]), sb("e", [P, KF, NP]), sb("n", [P, KF, NP]), sb("uT", [P, KF, NP])
        st, mv = sb("st", [P, NT, 6]), sb("mv", [P, NT, 2])
        ps = [pb(f"p{i}", [P, D]) for i in range(8)]
        loaded = {n: sem("loaded_" + n) for n in ("w3", "w4", "b3", "rows")}
        vec, sca, var_ready, rstd_ready, e_ready, n_ready, q_ready, u_ready, stored, x_ready = (
            sem(n) for n in ("vec", "sca", "var_ready", "rstd_ready", "e_ready", "n_ready", "q_ready", "u_ready",
                             "stored", "x_ready"))
        capped = sem("capped")
        plan = Plan(sem("product_ready"), {"vec": sem("taken_vec"), "sca": sem("taken_sca")}, {"one": ps})
        for m in range(KF):
            for f in range(2):
                plan.add(("u", m, f), "sca")
        for i in range(NT):
            plan.add(("w4", i), "vec")
        parts = [Mish(z[:, m, :], e[:, m, :], n_[:, m, :], uT[:, m, :]) for m in range(KF)]

        with nc.Block() as block:
            @block.sync
            def _(sp):
                sp.dma_start(w3[:, :, :], k.dram["w3"].rearrange("(c p) n -> p c n", p=P)).then_inc(loaded["w3"], 16)
                sp.dma_start(b3[:, :], k.dram["b3_cols"]).then_inc(loaded["b3"], 16)
                sp.dma_start(w4[:, :, :], k.dram["w4"].rearrange("(c p) n -> p c n", p=P)).then_inc(loaded["w4"], 16)
                for n, src in (("b4", k.dram["b4"]), ("gamma", k.dram["gamma"]), ("beta", k.dram["beta"])):
                    sp.dma_start(rows[n][:, :], src[None, :].to_broadcast([P, D])).then_inc(loaded["rows"], 16)
                for i in range(NT):
                    sp.wait_ge(x_ready, i + 1)
                    sp.dma_start(k.dram["out"][i * P:(i + 1) * P, :], k.x[:, i, :]).then_inc(stored, 16)
                sp.wait_ge(stored, 16 * NT)

            @block.tensor
            def _(pe):
                pe.wait_ge(loaded["w3"], 16)
                for m in range(KF):
                    for f in range(2):
                        bank = plan.open(pe, ("u", m, f))
                        half = slice(f * HALF, (f + 1) * HALF)
                        plan.made(chain(pe, bank[:, 0:HALF],
                                        [(w3[:, c, m * P:(m + 1) * P], k.hT[:, c, half]) for c in range(KF)] +
                                        [(w3[:, KF + c, m * P:(m + 1) * P], k.aggT[:, c, half]) for c in range(KF)]))
                pe.wait_ge(loaded["w4"], 16)
                pe.wait_ge(u_ready, KF)
                for i in range(NT):
                    bank = plan.open(pe, ("w4", i))
                    plan.made(chain(pe, bank[:, :], [(uT[:, c, i * P:(i + 1) * P], w4[:, c, :]) for c in range(KF)]))

            @block.scalar
            def _(act):
                act.preload_act_table_set(LOG_AND_EXP)
                own = Count(act, sca)
                act.wait_ge(loaded["b3"], 16)
                for m in range(KF):
                    for f in range(2):
                        bank = plan.take(act, ("u", m, f))
                        plan.took(("u", m, f), act.activation(z[:, m, f * HALF:(f + 1) * HALF], bank[:, 0:HALF],
                                                              ACT.Identity, bias=b3[:, m:m + 1]))
                    act.wait_ge(capped, m + 1)
                    parts[m].exp(act).then_inc(e_ready, 1)
                for m in range(KF):
                    act.wait_ge(n_ready, m + 1)
                    own(parts[m].log(act))
                    own.wait()
                    parts[m].quotient(act).then_inc(q_ready, 1)
                act.wait_ge(var_ready, 1)
                inverse_root(act, k, own, rstd_ready)

            @block.vector
            def _(dve):
                own = Count(dve, vec)
                for m in range(KF):
                    plan.need(dve, ("u", m, 1))
                    parts[m].cap(dve).then_inc(capped, 1)
                for m in range(KF):
                    dve.wait_ge(e_ready, m + 1)
                    parts[m].square(dve).then_inc(n_ready, 1)
                dve.wait_ge(loaded["rows"], 16 * 3)
                for i in range(NT):
                    own(dve.tensor_tensor(k.h[:, i, :], k.h[:, i, :], rows["b4"][:, :], ALU.add))
                for m in range(KF):
                    dve.wait_ge(q_ready, m + 1)
                    parts[m].product(dve).then_inc(u_ready, 1)
                own.wait()
                for i in range(NT):
                    bank = plan.take(dve, ("w4", i))
                    plan.took(("w4", i), dve.tensor_tensor(k.h[:, i, :], k.h[:, i, :], bank[:, :], ALU.add))
                    plan.need(dve, ("w4", i))
                    own(dve.bn_stats(st[:, i, :], k.h[:, i, :]))
                own.wait()
                for i in range(NT):
                    own(dve.bn_aggr(mv[:, i, :], st[:, i, :]))
                own.wait()
                dve.tensor_scalar(k.rstd[:, :], mv[:, :, 1], EPS, None, ALU.add).then_inc(var_ready, 1)
                for i in range(NT):
                    own(dve.tensor_tensor(k.x[:, i, :], k.x[:, i, :], rows["beta"][:, :], ALU.add))
                dve.wait_ge(rstd_ready, 1)
                for i in range(NT):
                    own(dve.tensor_scalar(k.h[:, i, :], k.h[:, i, :], mv[:, i, 0:1], k.rstd[:, i:i + 1],
                                          ALU.subtract, ALU.mult))
                own.wait()
                for i in range(NT):
                    own(dve.tensor_tensor(k.h[:, i, :], k.h[:, i, :], rows["gamma"][:, :], ALU.mult))
                own.wait()
                for i in range(NT):
                    dve.tensor_tensor(k.x[:, i, :], k.x[:, i, :], k.h[:, i, :], ALU.add).then_inc(x_ready, 1)


def write_rows(nc, k):
    with nc.semaphore("stored") as stored, nc.Block() as block:
        @block.sync
        def _(sp):
            sp.dma_start(k.dram["out"].rearrange("(i p) d -> p i d", p=P), k.x[:, :, :]).then_inc(stored, 16)
            sp.wait_ge(stored, 16)


STAGES = 5


def build(nc, a, out):
    k = Kernel(dict(a, out=out))
    ctx = ExitStack()
    with ctx:
        sb = lambda name, shape, dt=F32: ctx.enter_context(nc.sbuf_tensor(name, shape, dt))
        k.x, k.C, k.W, k.logc = sb("x", [P, NT, D]), sb("C", [P, NT, NP]), sb("W", [P, NT, NP]), sb("logc", [P, NT, NP])
        k.ident, k.ones, k.rstd = sb("ident", [P, P]), sb("ones", [P, P]), sb("rstd", [P, NT])
        k.has, k.dis, k.rdeg = sb("has", [P, NT]), sb("dis", [P, NT]), sb("rdeg", [P, NT])
        k.dst_f, k.src_i = sb("dst_f", [P, TILES]), sb("src_i", [P, TILES], I32)
        k.starts, k.sweeps = sb("starts", [1, (MAXSWEEPS + 1) * GROUPS], I32), sb("sweeps", [1, 1], I32)
        k.settled = ctx.enter_context(nc.semaphore("settled"))
        k.condT = sb("condT", [CROWS, NP])
        condition(nc, k)
        edge_windows_and_matrices(nc, k)
        sage_layer(nc, k)
        if STAGES > 2:
            transformer_layer(nc, k)
        if STAGES > 3:
            gcn_layer(nc, k)
        if STAGES < 5:
            write_rows(nc, k)
            return
        k.h, k.hT, k.aggT = sb("h", [P, NT, D]), sb("hT", [P, KF, NP]), sb("aggT", [P, KF, WIDE])
        k.src_table = nc.dram_tensor("src_table", (NP, D), F32, kind="Internal").ap()
        k.dst_table = nc.dram_tensor("dst_table", (NP + WIN, D), F32, kind="Internal").ap()
        edge_layer_tables(nc, k)
        edge_messages(nc, k)
        edge_layer_nodes(nc, k)


def kernel(**inputs):
    import numpy as np
    import concourse.bacc as bacc
    from concourse.bass_utils import run_bass_kernel_spmd as run

    v = {n: np.asarray(a) for n, a in inputs.items()}
    pad, pad_nodes = TILES * P - EDGES, NP - NODES

    def edges(a, fill):
        a = np.concatenate([a, np.full((pad,) + a.shape[1:], fill, a.dtype)])
        return np.ascontiguousarray(np.moveaxis(a.reshape((GROUPS, P, TPG) + a.shape[1:]), 1, 0)).reshape(P, -1)

    dst = v["dst"]
    host = {
        "x_in": np.concatenate([v["x"], np.zeros((NP - NODES, D), np.float32)]),
        "dst_rows": np.concatenate([dst, np.broadcast_to(dst[-1:], (pad,))]).reshape(
            GROUPS, P, TPG).transpose(0, 2, 1).reshape(GROUPS, GROUP),
        "dst_mark": edges(dst, -1),
        "src_tiles": edges(v["src"], 0),
        "attr3_tiles": edges(v["edge_attr_3"], 0),
        "conf_rows": np.broadcast_to(np.concatenate([v["L2_gnn_conf_w"][0], v["L2_gnn_conf_b"]]), (P, 4)),
        "w_l": v["L0_gnn_W_l"].T, "w_r": v["L0_gnn_W_r"].T, "b_l": v["L0_gnn_b_l"],
    }
    noise = np.concatenate([v["node_vec1"][:, 0], np.zeros(pad_nodes, np.float32)])
    host["noise_rows"] = np.broadcast_to(noise, (EMB, NP))
    freqs = np.arange(1, EMB // 2 + 1, dtype=np.float32) * np.float32(2.0 * np.pi / 16)
    quarter = np.repeat(np.array([0.0, 0.25], np.float32), EMB // 2)
    host["angle_consts"] = np.stack([np.tile(freqs, 2), quarter, (quarter * np.float32(2 * np.pi)).astype(np.float32)], 1)
    t = {n[7:]: a for n, a in v.items() if n.startswith("L1_gnn_")}
    host.update(f_w1=t["f_w1"], f_w2=t["f_w2"], f_b=np.stack([t["f_b1"], t["f_b2"]], 1))
    host.update(wq=t["wq"], wk=t["wk"], wv=t["wv"], wo=t["wo"], m1=t["m_w1"], m2=t["m_w2"],
                bv=t["bv"], bo=t["bo"], mb2=t["m_b2"])
    cond_w = np.zeros((BLOCKS, CROWS, 4, D), np.float32)
    for n, (ws, bs) in enumerate((("s1_w", "s1_b"), ("b1_w", "b1_b"), ("s2_w", "s2_b"), ("b2_w", "b2_b"))):
        cond_w[:, 0:COND, n], cond_w[:, CROWS - 1, n] = t[ws], t[bs]
    host["cond_w"] = cond_w
    host["col_biases"] = np.stack([t["bq"], t["bk"], t["m_b1"]], 1).reshape(BLOCKS, 3, KF, P).transpose(3, 0, 1, 2).reshape(P, -1)
    t = {n[7:]: a for n, a in v.items() if n.startswith("L3_gnn_")}
    host.update(lin_w=v["L2_gnn_lin_w"].T, lin_b=v["L2_gnn_lin_b"], w1=t["W1"], w2=t["W2"], w3=t["W3"], w4=t["W4"],
                b1=t["b1"], b2=t["b2"], b4=t["b4"], gamma=t["gamma"], beta=t["beta"],
                b3_cols=t["b3"].reshape(KF, P).T)
    attr = edges(v["edge_attr_64"], 0).reshape(P, TILES, EATTR)
    host["attr_T"] = attr.transpose(2, 1, 0).reshape(EATTR, TILES * P)
    nc = bacc.Bacc("TRN2", target_bir_lowering=False, num_devices=1)
    arrays, args = {}, {}
    for name, a in host.items():
        a = np.ascontiguousarray(a)
        arrays["in_" + name] = a
        args[name] = nc.dram_tensor("in_" + name, a.shape, mybir.dt.from_np(a.dtype), kind="ExternalInput").ap()
    out = nc.dram_tensor("out_0", (NP, D), F32, kind="ExternalOutput").ap()
    build(nc, args, out)
    r = run(nc, [arrays], core_ids=[0])
    return r.results[0]["out_0"][:NODES]
```

```python
from contextlib import ExitStack

import concourse.bass as bass
from concourse import mybir

F32, BF16, I32 = mybir.dt.float32, mybir.dt.bfloat16, mybir.dt.int32
F16, F32R = mybir.dt.float16, mybir.dt.float32r
ALU, ACT, AX = mybir.AluOpType, mybir.ActivationFunctionType, mybir.AxisListType

P = 128
NODES, D, EDGES = 625, 512, 20000
NT = -(-NODES // P)
NP = NT * P
HALF = NP // 2
KF = D // P
HEADS, DH = 4, 128
BLOCKS = 4
EMB, COND = 64, 16
PART = 32
CROWS = 3 * PART
TPG = 4
GROUP = TPG * P
GROUPS = -(-EDGES // GROUP)
TILES = GROUPS * TPG
WIN = 64
WIDE = NP + WIN
MAXSWEEPS = NP // WIN
EATTR = 64
EPS = 1e-5
NONE = -1.0e30
LOG_AND_EXP = "natural_log_exp_and_others"
CAP = 20.0


class Kernel:

    def __init__(self, dram):
        self.dram = dram


class Product:
    def __init__(self, n, by, c, before, bank):
        self.n, self.by, self.c, self.before, self.bank = n, by, c, before, bank


class Count:

    def __init__(self, eng, sem, start=0, it=None, per=0):
        self.eng, self.sem, self.n, self.it, self.per = eng, sem, start, it, per

    def at(self, n=None):
        n = self.n if n is None else n
        return n if self.it is None else self.it * self.per + n

    def __call__(self, ins):
        ins.then_inc(self.sem, 1)
        self.n += 1
        return self.n

    def wait(self, n=None):
        self.eng.wait_ge(self.sem, self.at(n))


class Plan:

    def __init__(self, product_ready, taken, rings):
        self.ready, self.taken, self.rings = product_ready, taken, rings
        self.at, self.used, self.count = {}, {r: [] for r in rings}, {e: 0 for e in taken}
        self.total = 0

    def add(self, key, by, ring="one"):
        self.total += 1
        self.count[by] += 1
        slots = self.rings[ring]
        used = self.used[ring]
        before = used[-len(slots)] if len(used) >= len(slots) else None
        used.append(key)
        self.at[key] = Product(n=self.total, by=by, c=self.count[by], before=before,
                                       bank=slots[(len(used) - 1) % len(slots)])

    def open(self, pe, key, it=None):
        g = self.at[key]
        if g.before is not None:
            self.need(pe, g.before, it)
        return g.bank

    def need(self, eng, key, it=None):
        g = self.at[key]
        eng.wait_ge(self.taken[g.by], g.c if it is None else it * self.count[g.by] + g.c)

    def made(self, ins):
        ins.then_inc(self.ready, 1)

    def take(self, eng, key, it=None):
        g = self.at[key]
        eng.wait_ge(self.ready, g.n if it is None else it * self.total + g.n)
        return g.bank

    def took(self, key, ins):
        ins.then_inc(self.taken[self.at[key].by], 1)


def scope(ctx, nc, tag):
    return (lambda name, shape, dt=F32: ctx.enter_context(nc.sbuf_tensor(f"{tag}_{name}", shape, dt)),
            lambda name, shape: ctx.enter_context(nc.psum_tensor(f"{tag}_{name}", shape, F32)),
            lambda name: ctx.enter_context(nc.semaphore(f"{tag}_{name}")))


def settle(k, eng):
    eng.sem_inc(k.settled, 1)


def rows_of(tensor, n):
    return tensor[:, :, :].rearrange("p a b -> p (a b)")[:, 0:n * D].rearrange("p (c n) -> p c n", n=D)


def cols(ap, n):
    return ap.rearrange("p (a b) -> p a b", b=n)


def edge_windows_and_matrices(nc, k):
    ctx = ExitStack()
    with ctx:
        sb, pb, sem = scope(ctx, nc, "mat")
        sums = sb("sums", [P, NT, 4, WIDE])
        dst_i = sb("dst_i", [P, TILES], I32)
        src_f = sb("src_f", [P, TILES])
        rows_i, rows_f = sb("rows_i", [GROUPS, GROUP], I32), sb("rows_f", [GROUPS, GROUP])
        lo_span = sb("lo_span", [GROUPS, 3])
        wtab = sb("wtab", [1, (MAXSWEEPS + 1) * GROUPS])
        span1 = sb("span1", [1, 2])
        iota_i = sb("iota_i", [P, WIDE], I32)
        attr3, confb = sb("attr3", [P, TILES, 3]), sb("confb", [P, 4])
        wz, wr = sb("wz", [P, TILES]), sb("wr", [P, TILES])
        wb = sb("wb", [P, TILES, 3], BF16)
        wf = sb("wf", [P, TILES])
        RING = 4
        from_onehot = [sb(f"from_onehot{a}", [P, TPG, NP], BF16) for a in range(RING)]
        to_onehot = [sb(f"to_onehot{a}", [P, TPG, 4, WIN], BF16) for a in range(RING)]
        iota16 = sb("iota16", [P, WIDE], F16)
        ps = [pb(f"sum_ps{a}", [P, 3 * D]) for a in range(2)]
        ps_row = pb("row_ps", [1, 2, GROUPS])
        ps_deg = pb("deg_ps", [P, NT])

        loaded_rows, loaded_dst, loaded_src = sem("loaded_rows"), sem("loaded_dst"), sem("loaded_src")
        loaded_attr, loaded_x = sem("loaded_attr"), sem("loaded_x")
        iota_made, ident_zero, ident_made, sums_zero = sem("iota_made"), sem("ident_zero"), sem("ident_made"), sem("sums_zero")
        vec, spans_ready, rows_ready, windows_known = sem("vec"), sem("spans_ready"), sem("rows_ready"), sem("windows_known")
        z_ready, exp_ready, act_ready = sem("z_ready"), sem("exp_ready"), sem("act_ready")
        iota_ready = sem("iota_ready")
        from_ready, to_ready, weighted, group_ready, added = (
            sem("from_ready"), sem("to_ready"), sem("weighted"), sem("group_ready"), sem("added"))
        W_summed = sem("W_summed")
        counts_ready, degree_ready, logs_ready = sem("counts_ready"), sem("degree_ready"), sem("logs_ready")

        def sweeps(eng):
            eng.wait_ge(windows_known, 2)
            return eng.value_load(k.sweeps[0:1, 0:1], min_val=0, max_val=MAXSWEEPS - 1)

        with nc.Block() as block:
            @block.sync
            def _(sp):
                sp.dma_start(rows_i[:, :], k.dram["dst_rows"]).then_inc(loaded_rows, 16)
                sp.dma_start(dst_i[:, :], k.dram["dst_mark"]).then_inc(loaded_dst, 16)
                sp.dma_start(k.src_i[:, :], k.dram["src_tiles"]).then_inc(loaded_src, 16)
                sp.dma_start(attr3[:, :, :], k.dram["attr3_tiles"].rearrange("p (t c) -> p t c", c=3)).then_inc(loaded_attr, 16)
                sp.dma_start(confb[:, :], k.dram["conf_rows"]).then_inc(loaded_attr, 16)
                sp.dma_start(k.x[:, :, :], k.dram["x_in"].rearrange("(i p) d -> p i d", p=P)).then_inc(loaded_x, 16)
                sp.wait_ge(loaded_x, 16)

            @block.gpsimd
            def _(pool):
                pool.iota(iota_i[:, :], pattern=[[1, WIDE]], base=0, channel_multiplier=0).then_inc(iota_made, 1)
                pool.memset(k.ident[:, :], 0.0).then_inc(ident_zero, 1)
                pool.wait_ge(ident_zero, 1)
                pool.affine_select(out=k.ident[:, :], in_=k.ident[:, :], compare_op=ALU.not_equal, fill=1.0,
                                   base=0, pattern=[[-1, P]], channel_multiplier=1).then_inc(ident_made, 1)
                for i in range(NT):
                    pool.memset(sums[:, i, :, :], 0.0).then_inc(sums_zero, 1)
                n = sweeps(pool)
                with pool.Fori(0, n * (GROUPS // RING) + GROUPS // RING) as t:
                    for a in range(RING):
                        pool.wait_ge(to_ready, t * RING + (a + 1))
                        settle(k, pool)
                        parts = [P, TPG, 3, WIN]
                        weights = wb[:, bass.ds((t * RING + a) % GROUPS * TPG, TPG), :]
                        pool.tensor_tensor(to_onehot[a][:, :, 1:4, :], to_onehot[a][:, :, 0:1, :].to_broadcast(parts),
                                           weights[:, :, :, None].to_broadcast(parts), ALU.mult).then_inc(weighted, 1)
                pool.wait_ge(added, n * GROUPS + (GROUPS + 2))
                settle(k, pool)
                for i in range(NT):
                    pool.tensor_tensor(k.W[:, i, :], sums[:, i, 1, 0:NP], sums[:, i, 2, 0:NP], ALU.add).then_inc(W_summed, 1)
                pool.wait_ge(W_summed, NT)
                for i in range(NT):
                    pool.tensor_tensor(k.W[:, i, :], k.W[:, i, :], sums[:, i, 3, 0:NP], ALU.add).then_inc(W_summed, 1)

            @block.scalar
            def _(act):
                act.preload_act_table_set(LOG_AND_EXP)
                act.wait_ge(z_ready, 1)
                act.activation(wz[:, :], wz[:, :], ACT.Exp, scale=-1.0).then_inc(exp_ready, 1)
                for i in range(NT):
                    act.wait_ge(counts_ready, 2 * (i + 1))
                    act.activation(k.logc[:, i, :], k.logc[:, i, :], ACT.Ln).then_inc(logs_ready, 1)
                act.wait_ge(counts_ready, 2 * NT + 1)
                act.activation(k.dis[:, :], k.dis[:, :], ACT.Ln).then_inc(act_ready, 1)
                act.wait_ge(act_ready, 1)
                act.activation(k.dis[:, :], k.dis[:, :], ACT.Exp, scale=-0.5).then_inc(logs_ready, 1)

            @block.tensor
            def _(pe):
                pe.wait_ge(ident_made, 1)
                pe.wait_ge(spans_ready, 1)
                pe.matmul(ps_row[:, 0, :], lo_span[:, 0:1], k.ident[0:GROUPS, 0:GROUPS], start=True, stop=True)
                pe.matmul(ps_row[:, 1, :], lo_span[:, 2:3], k.ident[0:GROUPS, 0:GROUPS], start=True,
                          stop=True).then_inc(rows_ready, 1)
                n = sweeps(pe)
                pe.sem_inc(group_ready, RING)
                pe.sem_inc(added, 2)
                with pe.Fori(0, n * (GROUPS // RING) + GROUPS // RING) as t:
                    for a in range(RING):
                        u = t * RING + a
                        pe.wait_ge(from_ready, u + 1)
                        pe.wait_ge(weighted, u + 1)
                        pe.wait_ge(added, u + 1)
                        for i in range(NT):
                            mm = chain(pe, ps[a % 2][:, i * 4 * WIN:(i + 1) * 4 * WIN],
                                       [(from_onehot[a][:, j, i * P:(i + 1) * P],
                                         to_onehot[a][:, j, :, :].rearrange("p a b -> p (a b)")) for j in range(TPG)])
                        mm.then_inc(group_ready, 1)
                pe.wait_ge(counts_ready, 2 * NT)
                for j in range(NT):
                    for i in range(NT):
                        mm = pe.matmul(ps_deg[:, j:j + 1], k.C[:, i, j * P:(j + 1) * P], k.ones[:, 0:1],
                                       start=(i == 0), stop=(i == NT - 1))
                mm.then_inc(degree_ready, 1)

            @block.vector
            def _(dve):
                own = Count(dve, vec)

                def step(ins):
                    own(ins)
                    own.wait()

                own(dve.memset(k.ones[:, :], 1.0))
                own(dve.memset(wtab[:, :], 0.0))
                dve.wait_ge(loaded_rows, 16)
                step(dve.tensor_copy(rows_f[:, :], rows_i[:, :]))
                own(dve.tensor_reduce(lo_span[:, 0:1], rows_f[:, :], AX.X, ALU.min))
                step(dve.tensor_reduce(lo_span[:, 1:2], rows_f[:, :], AX.X, ALU.max))
                dve.tensor_tensor(lo_span[:, 2:3], lo_span[:, 1:2], lo_span[:, 0:1], ALU.subtract).then_inc(spans_ready, 1)
                dve.wait_ge(iota_made, 1)
                dve.tensor_copy(iota16[:, :], iota_i[:, :]).then_inc(iota_ready, 1)
                dve.wait_ge(loaded_src, 16)
                dve.tensor_copy(src_f[:, :], k.src_i[:, :]).then_inc(iota_ready, 1)
                dve.wait_ge(loaded_dst, 16)
                step(dve.tensor_copy(k.dst_f[:, :], dst_i[:, :]))
                dve.wait_ge(rows_ready, 1)
                for w in range(MAXSWEEPS):
                    own(dve.tensor_scalar(wtab[:, w * GROUPS:(w + 1) * GROUPS], ps_row[:, 0, :], float(WIN * w),
                                          float(NP), ALU.add, ALU.min))
                own(dve.tensor_reduce(span1[:, 0:1], ps_row[:, 1, :], AX.X, ALU.max))
                step(dve.memset(span1[:, 1:2], 0.0))
                for w in range(1, MAXSWEEPS):
                    step(dve.scalar_tensor_tensor(span1[:, 1:2], span1[:, 0:1], float(WIN * w), span1[:, 1:2],
                                                  ALU.is_ge, ALU.add))
                dve.tensor_copy(k.starts[:, :], wtab[:, :]).then_inc(windows_known, 1)
                dve.tensor_copy(k.sweeps[:, :], span1[:, 1:2]).then_inc(windows_known, 1)
                dve.wait_ge(loaded_attr, 16 * 2)
                step(dve.tensor_scalar(wz[:, :], attr3[:, :, 0], confb[:, 0:1], confb[:, 3:4], ALU.mult, ALU.add))
                step(dve.scalar_tensor_tensor(wz[:, :], attr3[:, :, 1], confb[:, 1:2], wz[:, :], ALU.mult, ALU.add))
                dve.scalar_tensor_tensor(wz[:, :], attr3[:, :, 2], confb[:, 2:3], wz[:, :],
                                         ALU.mult, ALU.add).then_inc(z_ready, 1)
                dve.wait_ge(exp_ready, 1)
                step(dve.tensor_scalar(wz[:, :], wz[:, :], 1.0, None, ALU.add))
                step(dve.reciprocal(wr[:, :], wz[:, :]))
                step(dve.tensor_scalar(wr[:, :], wr[:, :], 0.0, None, ALU.max))
                for n in range(3):
                    step(dve.tensor_copy(wb[:, :, n], wr[:, :]))
                    if n < 2:
                        step(dve.tensor_copy(wf[:, :], wb[:, :, n]))
                        step(dve.tensor_tensor(wr[:, :], wr[:, :], wf[:, :], ALU.subtract))

                def start_of(u):
                    return dve.value_load(k.starts[0:1, bass.ds(u, 1)], min_val=0, max_val=NP)

                def compare(u, a, start):
                    tile0 = u % GROUPS * TPG
                    for j in range(TPG):
                        ins = dve.tensor_scalar(to_onehot[a][:, j, 0, :], iota16[:, bass.ds(start, WIN)],
                                                k.dst_f[:, bass.ds(tile0 + j, 1)], None, ALU.is_equal)
                    ins.then_inc(to_ready, 1)
                    for j in range(TPG):
                        ins = dve.tensor_scalar(from_onehot[a][:, j, :], iota16[:, 0:NP],
                                                src_f[:, bass.ds(tile0 + j, 1)], None, ALU.is_equal)
                    ins.then_inc(from_ready, 1)

                n = sweeps(dve)
                dve.wait_ge(sums_zero, NT)
                dve.wait_ge(iota_ready, 2)
                for a in range(2):
                    compare(a, a, start_of(a))
                with dve.Fori(0, n * (GROUPS // RING) + GROUPS // RING) as t:
                    for a in range(RING):
                        u = t * RING + a
                        dve.wait_ge(group_ready, u + 3)
                        compare(u + 2, (a + 2) % RING, start_of(u + 2))
                        start = start_of(u)
                        dve.wait_ge(group_ready, u + (1 + RING))
                        dve.wait_ge(added, u + 2)
                        into = sums[:, :, :, bass.ds(start, WIN)]
                        dve.tensor_tensor(into, into, ps[a % 2][:, 0:NT * 4 * WIN].rearrange(
                            "p (i n w) -> p i n w", i=NT, n=4), ALU.add).then_inc(added, 1)
                dve.wait_ge(added, n * GROUPS + (GROUPS + 2))
                done = Count(dve, counts_ready)
                for i in range(NT):
                    count = sums[:, i, 0, 0:NP]
                    done(dve.tensor_copy(k.C[:, i, :], count))
                    done(dve.tensor_scalar(k.logc[:, i, :], count, 1.0, None, ALU.max))
                    own(dve.tensor_scalar(count, count, 0.0, NONE, ALU.is_equal, ALU.mult))
                done.wait()
                step(dve.tensor_reduce(k.has[:, :], k.C[:, :, :], AX.X, ALU.add))
                done(dve.tensor_scalar(k.dis[:, :], k.has[:, :], 1.0, None, ALU.max))
                step(dve.tensor_scalar(k.has[:, :], k.has[:, :], 1.0, None, ALU.min))
                for i in range(NT):
                    dve.wait_ge(logs_ready, i + 1)
                    own(dve.tensor_tensor(k.logc[:, i, :], k.logc[:, i, :], sums[:, i, 0, 0:NP], ALU.add))
                dve.wait_ge(logs_ready, NT + 1)
                own(dve.tensor_tensor(k.dis[:, :], k.dis[:, :], k.has[:, :], ALU.mult))
                dve.wait_ge(degree_ready, 1)
                step(dve.tensor_scalar(k.rdeg[:, :], ps_deg[:, :], 1.0, None, ALU.max))
                step(dve.reciprocal(k.rdeg[:, :], k.rdeg[:, :]))



def row_stats(k, own, dve, i):
    own(dve.bn_stats(k.st[:, i, :], k.x[:, i, :]))


def layernorm_relu(k, h, var_ready, rstd_ready, h_ready, own, dve, factor=None):
    own.wait()
    for i in range(NT):
        own(dve.bn_aggr(k.mv[:, i, :], k.st[:, i, :]))
    own.wait()
    dve.tensor_scalar(k.rstd[:, :], k.mv[:, :, 1], EPS, None, ALU.add).then_inc(var_ready, 1)
    dve.wait_ge(rstd_ready, 1)
    at = {}
    for i in range(NT + 1):
        if i < NT:
            at[i] = own(dve.tensor_scalar(h[:, i, :], k.x[:, i, :], k.mv[:, i, 0:1], k.rstd[:, i:i + 1],
                                          ALU.subtract, ALU.mult))
        if i >= 1:
            t = i - 1
            own.wait(at[t])
            if factor is None:
                dve.tensor_scalar(h[:, t, :], h[:, t, :], 0.0, None, ALU.max).then_inc(h_ready, 1)
            else:
                dve.tensor_scalar(h[:, t, :], h[:, t, :], 0.0, factor[:, t:t + 1], ALU.max, ALU.mult).then_inc(h_ready, 1)


def inverse_root(act, k, own, rstd_ready):
    own(act.activation(k.rstd[:, :], k.rstd[:, :], ACT.Ln))
    own.wait()
    act.activation(k.rstd[:, :], k.rstd[:, :], ACT.Exp, scale=-0.5).then_inc(rstd_ready, 1)


def turn(pe, bank, src, ident):
    for m in range(KF):
        mm = pe.transpose(bank[:, m * P:(m + 1) * P], src[:, m * P:(m + 1) * P], ident)
    return mm


def chain(pe, out, pairs):
    last = len(pairs) - 1
    for n, (a, b) in enumerate(pairs):
        mm = pe.matmul(out, a, b, start=(n == 0), stop=(n == last))
    return mm


def sage_layer(nc, k):
    ctx = ExitStack()
    with ctx:
        sb, pb, sem = scope(ctx, nc, "sage")
        wl, wr = sb("wl", [P, KF, D]), sb("wr_", [P, KF, D])
        bl = sb("bl", [P, D])
        h, hT, aggT = sb("h", [P, NT, D]), sb("hT", [P, KF, NP]), sb("aggT0", [P, KF, NP])
        own_part = sb("own_part", [P, NT, D])
        ps = [pb(f"p{i}", [P, D]) for i in range(8)]
        loaded_wl, loaded_wr, loaded_bl = sem("loaded_wl"), sem("loaded_wr"), sem("loaded_bl")
        vec, sca, var_ready, rstd_ready, h_ready = (sem(n) for n in ("vec", "sca", "var_ready", "rstd_ready", "h_ready"))
        plan = Plan(sem("product_ready"), {"vec": sem("taken_vec"), "sca": sem("taken_sca")}, {"one": ps})
        for i in range(NT):
            plan.add(("hT", i), "sca")
        for m in range(KF):
            for f in range(2):
                plan.add(("agg", m, f), "vec")
        for i in range(NT):
            plan.add(("left", i), "sca")
            plan.add(("right", i), "vec")

        with nc.Block() as block:
            @block.sync
            def _(sp):
                sp.dma_start(wl[:, :, :], k.dram["w_l"].rearrange("(c p) n -> p c n", p=P)).then_inc(loaded_wl, 16)
                sp.dma_start(wr[:, :, :], k.dram["w_r"].rearrange("(c p) n -> p c n", p=P)).then_inc(loaded_wr, 16)
                sp.dma_start(bl[:, :], k.dram["b_l"][None, :].to_broadcast([P, D])).then_inc(loaded_bl, 16)

            @block.tensor
            def _(pe):
                for i in range(NT):
                    bank = plan.open(pe, ("hT", i))
                    pe.wait_ge(h_ready, i + 1)
                    plan.made(turn(pe, bank, h[:, i, :], k.ident[:, :]))
                for m in range(KF):
                    for f in range(2):
                        bank = plan.open(pe, ("agg", m, f))
                        plan.made(chain(pe, bank[:, 0:HALF], [(h[:, i, m * P:(m + 1) * P],
                                  k.C[:, i, f * HALF:(f + 1) * HALF]) for i in range(NT)]))
                pe.wait_ge(loaded_wl, 16)
                pe.wait_ge(loaded_wr, 16)
                for i in range(NT):
                    for key, wts, src, before in (("left", wl, aggT, ("agg", KF - 1, 1)), ("right", wr, hT, ("hT", NT - 1))):
                        bank = plan.open(pe, (key, i))
                        if i == 0:
                            plan.need(pe, before)
                        plan.made(chain(pe, bank[:, :], [(src[:, c, i * P:(i + 1) * P], wts[:, c, :]) for c in range(KF)]))

            @block.scalar
            def _(act):
                act.preload_act_table_set(LOG_AND_EXP)
                own = Count(act, sca)
                act.wait_ge(var_ready, 1)
                inverse_root(act, k, own, rstd_ready)
                for i in range(NT):
                    bank = plan.take(act, ("hT", i))
                    plan.took(("hT", i), act.activation(hT[:, :, i * P:(i + 1) * P], cols(bank[:, :], P), ACT.Copy))
                for i in range(NT):
                    bank = plan.take(act, ("left", i))
                    plan.took(("left", i), act.activation(own_part[:, i, :], bank[:, :], ACT.Copy,
                                                          scale=k.rdeg[:, i:i + 1]))

            @block.vector
            def _(dve):
                own = Count(dve, vec)
                for i in range(NT):
                    row_stats(k, own, dve, i)
                layernorm_relu(k, h, var_ready, rstd_ready, h_ready, own, dve)
                for m in range(KF):
                    for f in range(2):
                        bank = plan.take(dve, ("agg", m, f))
                        plan.took(("agg", m, f), dve.tensor_copy(aggT[:, m, f * HALF:(f + 1) * HALF], bank[:, 0:HALF]))
                dve.wait_ge(loaded_bl, 16)
                for i in range(NT):
                    plan.need(dve, ("left", i))
                    own(dve.tensor_tensor(own_part[:, i, :], own_part[:, i, :], bl[:, :], ALU.add))
                    own.wait()
                    bank = plan.take(dve, ("right", i))
                    plan.took(("right", i), dve.tensor_tensor(own_part[:, i, :], own_part[:, i, :], bank[:, :], ALU.add))
                    plan.need(dve, ("right", i))
                    own(dve.scalar_tensor_tensor(k.x[:, i, :], own_part[:, i, :], 0.0, k.x[:, i, :], ALU.max, ALU.add))
                    own.wait()
                    row_stats(k, own, dve, i)


TWO_PI_PARTS = (6.28125, 0.0019353071795864769 - 3.0199159819567e-07, 3.0199159819567e-07)
ROUND = 1.5 * 2.0 ** 23


def condition(nc, k):
    ctx = ExitStack()
    with ctx:
        sb, pb, sem = scope(ctx, nc, "cond")
        noise, ph, turns = sb("noise", [EMB, NP]), sb("ph", [EMB, NP]), sb("turns", [EMB, NP])
        emb = sb("emb", [EMB, NP])
        consts = sb("consts", [EMB, 3])
        f1, f2 = sb("f1", [EMB, COND]), sb("f2", [COND, CROWS])
        fb1, fb2 = sb("fb1", [COND, 1]), sb("fb2", [CROWS, 1])
        parts = sb("parts", [CROWS, NP])
        z, e = sb("z", [COND, NP]), sb("e", [COND, NP])
        ps = [pb(f"cp{i}", [COND if i < 2 else CROWS, HALF]) for i in range(4)]
        loaded = sem("loaded")
        vec, angle_ready, emb_ready, hidden_ready, z_ready, e_ready, silu_ready, out_ready = (
            sem(n) for n in ("vec", "angle_ready", "emb_ready", "hidden_ready", "z_ready", "e_ready", "silu_ready", "out_ready"))
        with nc.Block() as block:
            @block.sync
            def _(sp):
                sp.dma_start(noise[:, :], k.dram["noise_rows"]).then_inc(loaded, 16)
                for dst, src in zip((consts, f1, f2, fb1, fb2), (k.dram[n] for n in ("angle_consts", "f_w1", "f_w2", "f_b1", "f_b2"))):
                    sp.dma_start(dst[:, :], src).then_inc(loaded, 16)

            @block.vector
            def _(dve):
                own = Count(dve, vec)

                def step(ins):
                    own(ins)
                    own.wait()

                dve.wait_ge(loaded, 16 * 6)
                step(dve.tensor_scalar(ph[:, :], noise[:, :], consts[:, 0:1], None, ALU.mult))
                step(dve.tensor_scalar(turns[:, :], ph[:, :], 0.15915494309189535, consts[:, 1:2], ALU.mult, ALU.add))
                step(dve.tensor_scalar(turns[:, :], turns[:, :], ROUND, None, ALU.add))
                step(dve.tensor_scalar(turns[:, :], turns[:, :], ROUND, None, ALU.subtract))
                for part in TWO_PI_PARTS:
                    step(dve.scalar_tensor_tensor(ph[:, :], turns[:, :], -part, ph[:, :], ALU.mult, ALU.add))
                step(dve.tensor_scalar(ph[:, :], ph[:, :], consts[:, 2:3], None, ALU.add))
                dve.tensor_scalar(ph[:, :], ph[:, :], 3.1415925, -3.1415925, ALU.min, ALU.max).then_inc(angle_ready, 1)
                for f in range(2):
                    dve.wait_ge(hidden_ready, f + 1)
                    dve.tensor_scalar(z[:, f * HALF:(f + 1) * HALF], ps[f][:, :], fb1[:, 0:1], None,
                                      ALU.add).then_inc(z_ready, 1)
                dve.wait_ge(z_ready, 2)
                dve.wait_ge(e_ready, 1)
                step(dve.tensor_scalar(e[:, :], e[:, :], 1.0, None, ALU.add))
                step(dve.reciprocal(e[:, :], e[:, :]))
                dve.tensor_tensor(z[:, :], z[:, :], e[:, :], ALU.mult).then_inc(silu_ready, 1)
                for f in range(2):
                    dve.wait_ge(out_ready, f + 1)
                    own(dve.tensor_scalar(parts[:, f * HALF:(f + 1) * HALF], ps[2 + f][:, :], fb2[:, 0:1], None,
                                          ALU.add))
                own.wait()
                step(dve.tensor_copy(k.condT[:, :], parts[:, :]))
                low = slice(2 * PART, CROWS)
                own(dve.tensor_tensor(k.condT[low, :], parts[low, :], k.condT[low, :].bitcast(F32), ALU.subtract))

            @block.scalar
            def _(act):
                act.wait_ge(angle_ready, 1)
                act.activation(emb[:, :], ph[:, :], ACT.Sin).then_inc(emb_ready, 1)
                act.preload_act_table_set(LOG_AND_EXP)
                act.wait_ge(z_ready, 2)
                act.activation(e[:, :], z[:, :], ACT.Exp, scale=-1.0).then_inc(e_ready, 1)

            @block.tensor
            def _(pe):
                pe.wait_ge(emb_ready, 1)
                pe.wait_ge(loaded, 16 * 6)
                for f in range(2):
                    pe.matmul(ps[f][:, :], f1[:, :], emb[:, f * HALF:(f + 1) * HALF], start=True,
                              stop=True).then_inc(hidden_ready, 1)
                pe.wait_ge(silu_ready, 1)
                for f in range(2):
                    pe.matmul(ps[2 + f][:, :], f2[:, :], z[:, f * HALF:(f + 1) * HALF], start=True,
                              stop=True).then_inc(out_ready, 1)


def transformer_layer(nc, k):
    ctx = ExitStack()
    with ctx:
        sb, pb, sem = scope(ctx, nc, "tr")
        names = ("wq", "wk", "wv", "wo", "m1", "m2")
        w = {n: sb("w_" + n, [P, KF, D]) for n in names}
        cw_raw, cw = sb("cw_raw", [CROWS, 4, D]), sb("cw", [CROWS, 4, D], F32R)
        rows = {n: sb("row_" + n, [P, D]) for n in ("bv", "bo", "mb2")}
        cb = sb("cb", [P, BLOCKS, 3, KF])
        r, y = sb("r", [P, NT, D]), k.C
        yT, qT, kT, v = sb("yT", [P, KF, NP]), sb("qT", [P, KF, NP]), sb("kT", [P, KF, NP]), sb("v", [P, NT, D])
        scores, probs = sb("scores", [P, 3, NP]), sb("probs", [P, 3, NP])
        probsT = [sb("probsT", [P, NT, NP]), k.C]
        hidT = qT
        oT = yT
        nmax, den = sb("nmax", [P, HEADS * NT]), sb("den", [P, HEADS * NT])
        st, mv = sb("st", [P, NT, 6]), sb("mv", [P, NT, 2])
        one = [pb(f"one{i}", [P, D]) for i in range(2)]
        two = [pb(f"two{i}", [P, 2, D]) for i in range(3)]
        loaded = {n: sem("loaded_" + n) for n in names + ("cw", "bv", "bo", "mb2", "cb")}
        vec, sca, var_ready, rstd_ready, h_ready, exp_ready, probs_ready, read1, bias_added, block_done = (
            sem(n) for n in ("vec", "sca", "var_ready", "rstd_ready", "h_ready", "exp_ready", "probs_ready",
                             "read1", "bias_added", "block_done"))
        cb_scaled, cw_high, cw_ready = sem("cb_scaled"), sem("cw_high"), sem("cw_ready")
        plan = Plan(sem("product_ready"), {"vec": sem("taken_vec"), "sca": sem("taken_sca")}, {"one": one, "two": two})
        N = HEADS * NT

        def norm_products(s):
            for i in range(NT + 2):
                if i >= 2:
                    plan.add(("yT", s, i - 2), "sca", "two")
                if i < NT:
                    plan.add(("scale", s, i), "vec")

        norm_products(0)
        for name, by in (("q", "sca"), ("k", "vec")):
            for m in range(KF):
                for f in range(2):
                    plan.add((name, m, f), by)
        for i in range(NT):
            plan.add(("v", i), "vec")
        for n in range(N + 4):
            if n < N:
                plan.add(("S", n), "vec", "two")
            if 2 <= n < N + 2:
                plan.add(("T", n - 2), "sca", "two")
            if n >= 8 and (n - 8) % NT == 0:
                for f in range(2):
                    plan.add(("o", (n - 8) // NT, f), "sca")
        for i in range(NT):
            plan.add(("wo", i), "vec")
        norm_products(1)
        for m in range(KF):
            for f in range(2):
                plan.add(("m1", m, f), "sca")
        for i in range(NT):
            plan.add(("m2", i), "vec")

        with nc.Block() as block:
            @block.sync
            def _(sp):
                def load(name, b):
                    if name == "cw":
                        dst, src = cw_raw[:, :, :], k.dram["cond_w"][bass.ds(b, 1)].rearrange("o p a n -> p (o a) n")
                    elif name in rows:
                        dst = rows[name][:, :]
                        src = row_biases[name][bass.ds(b, 1), :].to_broadcast([P, D])
                    else:
                        dst = w[name][:, :, :]
                        src = mats[name].rearrange("b (c p) n -> b p c n", p=P)[bass.ds(b, 1)].rearrange("o p c n -> p (o c) n")
                    sp.dma_start(dst, src).then_inc(loaded[name], 16)

                mats = {"wq": k.dram["wq"], "wk": k.dram["wk"], "wv": k.dram["wv"], "wo": k.dram["wo"], "m1": k.dram["m1"], "m2": k.dram["m2"]}
                row_biases = {"bv": k.dram["bv"], "bo": k.dram["bo"], "mb2": k.dram["mb2"]}
                sp.dma_start(cb[:, :, :, :], k.dram["col_biases"].rearrange("p (b n c) -> p b n c", n=3, c=KF)).then_inc(loaded["cb"], 16)
                for name in ("cw", "wq", "wk", "wv", "bv", "bo", "wo", "m1", "m2", "mb2"):
                    load(name, 0)
                with sp.Fori(0, BLOCKS - 1) as b:
                    for name, key in (("cw", None), ("wq", ("q", KF - 1, 1)), ("wk", ("k", KF - 1, 1)), ("wv", ("v", NT - 1)),
                                      ("bv", None), ("bo", None), ("wo", ("wo", NT - 1)),
                                      ("m1", ("m1", KF - 1, 1)), ("m2", ("m2", NT - 1)), ("mb2", None)):
                        if key:
                            plan.take(sp, key, b)
                        elif name == "cw":
                            sp.wait_ge(cw_ready, b * 2 + 2)
                        elif name == "bv":
                            plan.need(sp, ("v", NT - 1), b)
                        elif name == "bo":
                            sp.wait_ge(bias_added, b * 2 * NT + NT)
                        else:
                            sp.wait_ge(bias_added, b * 2 * NT + 2 * NT)
                        load(name, b + 1)
                sp.wait_ge(cw_ready, BLOCKS * 2)
                load("cw", 0)

            @block.gpsimd
            def _(pool):
                rest = slice(PART, 2 * PART)

                def cut(b):
                    for s in range(2):
                        pool.wait_ge(cw_high, b * 2 + (s + 1))
                        both = slice(2 * s, 2 * s + 2)
                        pool.tensor_tensor(cw[rest, both, :], cw_raw[rest, both, :], cw[rest, both, :].bitcast(F32),
                                           ALU.subtract).then_inc(cw_ready, 1)
                        pool.wait_ge(cw_ready, b * 2 + (s + 1))

                cut(0)
                with pool.Fori(0, BLOCKS) as b:
                    for s, name in enumerate(("bo", "mb2")):
                        pool.wait_ge(loaded[name], b * 16 + 16)
                        for i in range(NT):
                            pool.wait_ge(read1, b * (2 * NT) + (s * NT + i + 1))
                            pool.tensor_tensor(r[:, i, :], r[:, i, :], rows[name][:, :], ALU.add).then_inc(bias_added, 1)
                    pool.wait_ge(bias_added, b * (2 * NT) + 2 * NT)
                    cut(b + 1)

            @block.tensor
            def _(pe):
                def norm(s, b):
                    pe.wait_ge(cw_ready, b * 2 + (s + 1))
                    for i in range(NT + 2):
                        if i >= 2:
                            t = i - 2
                            bank = plan.open(pe, ("yT", s, t), b)[:, 0, :]
                            plan.need(pe, ("scale", s, t), b)
                            for m in range(KF):
                                pe.matmul(bank[:, m * P:(m + 1) * P], y[:, t, m * P:(m + 1) * P], k.ident[:, :],
                                          is_transpose=True, start=(m == 0), stop=False)
                            for m in range(KF):
                                mm = pe.matmul(bank[:, m * P:(m + 1) * P], cw[:, 2 * s + 1, m * P:(m + 1) * P],
                                               k.condT[:, t * P:(t + 1) * P], start=False, stop=(m == KF - 1))
                            plan.made(mm)
                        if i < NT:
                            bank = plan.open(pe, ("scale", s, i), b)
                            plan.made(pe.matmul(bank[:, :], k.condT[:, i * P:(i + 1) * P], cw[:, 2 * s, :],
                                                start=True, stop=True))

                def by_feature(name, wts, src, b):
                    for m in range(KF):
                        for f in range(2):
                            bank = plan.open(pe, (name, m, f), b)
                            plan.made(chain(pe, bank[:, 0:HALF], [(wts[:, c, m * P:(m + 1) * P],
                                      src[:, c, f * HALF:(f + 1) * HALF]) for c in range(KF)]))

                def by_node(name, wts, src, b):
                    for i in range(NT):
                        bank = plan.open(pe, (name, i), b)
                        plan.made(chain(pe, bank[:, :], [(src[:, c, i * P:(i + 1) * P], wts[:, c, :]) for c in range(KF)]))

                pe.sem_inc(block_done, 1)
                with pe.Fori(0, BLOCKS) as b:
                    pe.wait_ge(block_done, b + 1)
                    norm(0, b)
                    plan.need(pe, ("yT", 0, NT - 1), b)
                    pe.wait_ge(loaded["wq"], b * 16 + 16)
                    by_feature("q", w["wq"], yT, b)
                    pe.wait_ge(loaded["wk"], b * 16 + 16)
                    by_feature("k", w["wk"], yT, b)
                    pe.wait_ge(loaded["wv"], b * 16 + 16)
                    by_node("v", w["wv"], yT, b)
                    for n in range(N + 4):
                        if n < N:
                            h, i = divmod(n, NT)
                            bank = plan.open(pe, ("S", n), b)
                            if i == 0:
                                plan.need(pe, ("q", h, 1), b)
                                plan.need(pe, ("k", h, 1), b)
                            for f in range(2):
                                mm = pe.matmul(bank[:, f, 0:HALF], qT[:, h, i * P:(i + 1) * P],
                                               kT[:, h, f * HALF:(f + 1) * HALF], start=True, stop=True)
                            plan.made(mm)
                        if 2 <= n < N + 2:
                            bank = plan.open(pe, ("T", n - 2), b)
                            pe.wait_ge(probs_ready, b * N + (n - 1))
                            flat = bank[:, :, :].rearrange("p a b -> p (a b)")
                            for j in range(NT):
                                mm = pe.transpose(flat[:, j * P:(j + 1) * P], probs[:, (n - 2) % 3, j * P:(j + 1) * P],
                                                  k.ident[:, :])
                            plan.made(mm)
                        if n >= 8 and (n - 8) % NT == 0:
                            h = (n - 8) // NT
                            plan.need(pe, ("T", h * NT + NT - 1), b)
                            if h == 0:
                                plan.need(pe, ("v", NT - 1), b)
                            for f in range(2):
                                bank = plan.open(pe, ("o", h, f), b)
                                plan.made(chain(pe, bank[:, 0:HALF], [(v[:, j, h * DH:(h + 1) * DH],
                                          probsT[h % 2][:, j, f * HALF:(f + 1) * HALF]) for j in range(NT)]))
                    plan.need(pe, ("o", HEADS - 1, 1), b)
                    pe.wait_ge(loaded["wo"], b * 16 + 16)
                    by_node("wo", w["wo"], oT, b)
                    norm(1, b)
                    plan.need(pe, ("yT", 1, NT - 1), b)
                    pe.wait_ge(loaded["m1"], b * 16 + 16)
                    by_feature("m1", w["m1"], yT, b)
                    plan.need(pe, ("m1", KF - 1, 1), b)
                    pe.wait_ge(loaded["m2"], b * 16 + 16)
                    by_node("m2", w["m2"], hidT, b)

            @block.scalar
            def _(act):
                act.preload_act_table_set(LOG_AND_EXP)
                first = Count(act, sca)
                act.wait_ge(var_ready, 1)
                inverse_root(act, k, first, rstd_ready)
                act.wait_ge(cb_scaled, 1)

                def cut(b):
                    act.wait_ge(loaded["cw"], b * 16 + 16)
                    settle(k, act)
                    for s in range(2):
                        both = slice(2 * s, 2 * s + 2)
                        act.activation(cw[:, both, :], cw_raw[:, both, :], ACT.Copy).then_inc(cw_high, 1)

                cut(0)
                with act.Fori(0, BLOCKS) as b:
                    own = Count(act, sca, 1, b, 2)

                    def norm(s):
                        act.wait_ge(var_ready, b * 2 + (s + 2))
                        inverse_root(act, k, own, rstd_ready)
                        for i in range(NT):
                            bank = plan.take(act, ("yT", s, i), b)
                            plan.took(("yT", s, i), act.activation(yT[:, :, i * P:(i + 1) * P], cols(bank[:, 0, :], P), ACT.Copy))

                    def bias_of(which, m):
                        return cb[:, bass.ds(b, 1), which, m]

                    norm(0)
                    for m in range(KF):
                        for f in range(2):
                            bank = plan.take(act, ("q", m, f), b)
                            settle(k, act)
                            plan.took(("q", m, f), act.activation(qT[:, m, f * HALF:(f + 1) * HALF], bank[:, 0:HALF],
                                                                  ACT.Identity, bias=bias_of(0, m), scale=DH ** -0.5))
                    for n in range(N + 4):
                        if n < N:
                            plan.need(act, ("S", n), b)
                            act.activation(probs[:, n % 3, :], scores[:, n % 3, :], ACT.Exp, bias=nmax[:, n:n + 1],
                                           scale=-1.0, accum_out=den[:, n:n + 1]).then_inc(exp_ready, 1)
                        if 2 <= n < N + 2:
                            h, i = divmod(n - 2, NT)
                            bank = plan.take(act, ("T", n - 2), b)
                            flat = bank[:, :, :].rearrange("p a b -> p (a b)")
                            plan.took(("T", n - 2), act.activation(probsT[h % 2][:, :, i * P:(i + 1) * P],
                                                                   cols(flat[:, 0:NP], P), ACT.Copy))
                        if n >= 8 and (n - 8) % NT == 0:
                            h = (n - 8) // NT
                            for f in range(2):
                                bank = plan.take(act, ("o", h, f), b)
                                plan.took(("o", h, f), act.activation(oT[:, h, f * HALF:(f + 1) * HALF],
                                                                      bank[:, 0:HALF], ACT.Copy))
                    norm(1)
                    for m in range(KF):
                        for f in range(2):
                            bank = plan.take(act, ("m1", m, f), b)
                            settle(k, act)
                            plan.took(("m1", m, f), act.activation(hidT[:, m, f * HALF:(f + 1) * HALF], bank[:, 0:HALF],
                                                                   ACT.Relu, bias=bias_of(2, m)))
                    cut(b + 1)

            @block.vector
            def _(dve):
                first = Count(dve, vec)
                layernorm_relu(k, r, var_ready, rstd_ready, h_ready, first, dve)
                dve.wait_ge(loaded["cb"], 16)
                dve.tensor_scalar(cb[:, :, 0, :], cb[:, :, 0, :], DH ** -0.5, None, ALU.mult).then_inc(cb_scaled, 1)
                dve.wait_ge(cb_scaled, 1)
                dve.wait_ge(h_ready, NT)
                for i in range(NT):
                    first(dve.bn_stats(st[:, i, :], r[:, i, :]))

                with dve.Fori(0, BLOCKS) as b:
                    own = Count(dve, vec, first.n, b, 4 * NT + N)

                    def norm(s):
                        own.wait()
                        settle(k, dve)
                        for i in range(NT):
                            own(dve.bn_aggr(mv[:, i, :], st[:, i, :]))
                        own.wait()
                        dve.tensor_scalar(k.rstd[:, :], mv[:, :, 1], EPS, None, ALU.add).then_inc(var_ready, 1)
                        dve.wait_ge(rstd_ready, b * 2 + (s + 2))
                        for i in range(NT + 1):
                            if i < NT:
                                dve.tensor_scalar(y[:, i, 0:D], r[:, i, :], mv[:, i, 0:1], k.rstd[:, i:i + 1],
                                                  ALU.subtract, ALU.mult).then_inc(read1, 1)
                            if i >= 1:
                                t = i - 1
                                dve.wait_ge(read1, b * (2 * NT) + (s * NT + i))
                                bank = plan.take(dve, ("scale", s, t), b)
                                plan.took(("scale", s, t), dve.scalar_tensor_tensor(
                                    y[:, t, 0:D], bank[:, :], 1.0, y[:, t, 0:D], ALU.add, ALU.mult))

                    def residual(name, s):
                        for i in range(NT):
                            dve.wait_ge(bias_added, b * (2 * NT) + (s * NT + i + 1))
                            bank = plan.take(dve, (name, i), b)
                            plan.took((name, i), dve.tensor_tensor(r[:, i, :], r[:, i, :], bank[:, :], ALU.add))
                            plan.need(dve, (name, i), b)
                            own(dve.bn_stats(st[:, i, :], r[:, i, :]))

                    norm(0)
                    for m in range(KF):
                        for f in range(2):
                            bank = plan.take(dve, ("k", m, f), b)
                            plan.took(("k", m, f), dve.tensor_scalar(kT[:, m, f * HALF:(f + 1) * HALF], bank[:, 0:HALF],
                                                                     cb[:, bass.ds(b, 1), 1, m], None, ALU.add))
                    dve.wait_ge(loaded["bv"], b * 16 + 16)
                    for i in range(NT):
                        bank = plan.take(dve, ("v", i), b)
                        plan.took(("v", i), dve.tensor_tensor(v[:, i, :], bank[:, :], rows["bv"][:, :], ALU.add))
                    for n in range(N + 1):
                        if n < N:
                            i = n % NT
                            bank = plan.take(dve, ("S", n), b)
                            settle(k, dve)
                            ins = dve.tensor_tensor_reduce(out=cols(scores[:, n % 3, :], HALF), in0=bank[:, :, 0:HALF],
                                                           in1=cols(k.logc[:, i, :], HALF), scale=-1.0, scalar=3.0e38,
                                                           op0=ALU.add, op1=ALU.min, accum_out=nmax[:, n:n + 1])
                            plan.took(("S", n), ins)
                        if n >= 1:
                            m = n - 1
                            dve.wait_ge(exp_ready, b * N + (m + 1))
                            own(dve.reciprocal(den[:, m:m + 1], den[:, m:m + 1]))
                            own.wait()
                            dve.tensor_scalar(probs[:, m % 3, :], probs[:, m % 3, :], den[:, m:m + 1],
                                              k.has[:, m % NT:m % NT + 1], ALU.mult, ALU.mult).then_inc(probs_ready, 1)
                    residual("wo", 0)
                    norm(1)
                    residual("m2", 1)
                    dve.sem_inc(block_done, 1)
                for i in range(NT):
                    dve.tensor_tensor(k.x[:, i, :], k.x[:, i, :], r[:, i, :], ALU.add).then_inc(h_ready, 1)
                for i in range(NT):
                    dve.wait_ge(h_ready, NT + i + 1)
                    row_stats(k, first, dve, i)


def gcn_layer(nc, k):
    ctx = ExitStack()
    with ctx:
        sb, pb, sem = scope(ctx, nc, "gcn")
        wt, lb = sb("wt", [P, KF, D]), sb("lb", [P, D])
        h, aggT = sb("h", [P, NT, D]), sb("aggT", [P, KF, NP])
        ps = [pb(f"p{i}", [P, D]) for i in range(8)]
        loaded_wt, loaded_lb = sem("loaded_wt"), sem("loaded_lb")
        vec, sca, var_ready, rstd_ready, h_ready = (
            sem(n) for n in ("vec", "sca", "var_ready", "rstd_ready", "h_ready"))
        plan = Plan(sem("product_ready"), {"vec": sem("taken_vec"), "sca": sem("taken_sca")}, {"one": ps})
        for m in range(KF):
            for f in range(2):
                plan.add(("agg", m, f), "sca")
        for i in range(NT):
            plan.add(("lin", i), "vec")

        with nc.Block() as block:
            @block.sync
            def _(sp):
                sp.dma_start(wt[:, :, :], k.dram["lin_w"].rearrange("(c p) n -> p c n", p=P)).then_inc(loaded_wt, 16)
                sp.dma_start(lb[:, :], k.dram["lin_b"][None, :].to_broadcast([P, D])).then_inc(loaded_lb, 16)

            @block.scalar
            def _(act):
                act.preload_act_table_set(LOG_AND_EXP)
                own = Count(act, sca)
                act.wait_ge(var_ready, 1)
                inverse_root(act, k, own, rstd_ready)
                for m in range(KF):
                    for f in range(2):
                        bank = plan.take(act, ("agg", m, f))
                        plan.took(("agg", m, f), act.activation(aggT[:, m, f * HALF:(f + 1) * HALF], bank[:, 0:HALF], ACT.Copy))

            @block.tensor
            def _(pe):
                pe.wait_ge(h_ready, NT)
                for m in range(KF):
                    for f in range(2):
                        bank = plan.open(pe, ("agg", m, f))
                        plan.made(chain(pe, bank[:, 0:HALF], [(h[:, i, m * P:(m + 1) * P],
                                  k.W[:, i, f * HALF:(f + 1) * HALF]) for i in range(NT)]))
                pe.wait_ge(loaded_wt, 16)
                for i in range(NT):
                    bank = plan.open(pe, ("lin", i))
                    if i == 0:
                        plan.need(pe, ("agg", KF - 1, 1))
                    plan.made(chain(pe, bank[:, :], [(aggT[:, c, i * P:(i + 1) * P], wt[:, c, :]) for c in range(KF)]))

            @block.vector
            def _(dve):
                own = Count(dve, vec)
                layernorm_relu(k, h, var_ready, rstd_ready, h_ready, own, dve, factor=k.dis)
                dve.wait_ge(loaded_lb, 16)
                for i in range(NT):
                    own(dve.tensor_tensor(k.x[:, i, :], k.x[:, i, :], lb[:, :], ALU.add))
                own.wait()
                for i in range(NT):
                    bank = plan.take(dve, ("lin", i))
                    plan.took(("lin", i), dve.scalar_tensor_tensor(k.x[:, i, :], bank[:, :], k.dis[:, i:i + 1],
                                                                   k.x[:, i, :], ALU.mult, ALU.add))
                    plan.need(dve, ("lin", i))
                    row_stats(k, own, dve, i)


class Mish:

    def __init__(self, z, e, n, out):
        self.z, self.e, self.n, self.out = z, e, n, out

    def cap(self, dve):
        return dve.tensor_scalar(self.e, self.z, CAP, None, ALU.min)

    def exp(self, act):
        return act.activation(self.e, self.e, ACT.Exp)

    def square(self, dve):
        return dve.scalar_tensor_tensor(self.n, self.e, 2.0, self.e, ALU.add, ALU.mult)

    def log(self, act):
        return act.activation(self.n, self.n, ACT.Ln, bias=1.0, scale=0.5)

    def quotient(self, act):
        return act.activation(self.n, self.n, ACT.Exp, scale=-1.0)

    def product(self, dve):
        return dve.scalar_tensor_tensor(self.out, self.n, 1.0, self.z, ALU.subtract, ALU.mult, reverse0=True)


def edge_layer_tables(nc, k):
    ctx = ExitStack()
    with ctx:
        sb, pb, sem = scope(ctx, nc, "tab")
        ws, wd, b1 = sb("ws", [P, KF, D]), sb("wd", [P, KF, D]), sb("b1", [P, D])
        tables = {"src": sb("ts", [P, NT, D]), "dst": sb("td", [P, NT, D])}
        zero = sb("zero", [WIN, D])
        ps = [pb(f"p{i}", [P, D]) for i in range(8)]
        loaded = {n: sem("loaded_" + n) for n in ("src", "dst", "b1", "w2")}
        stored = sem("stored")
        zeroed = sem("zeroed")
        w2 = rows_of(k.C, KF)
        vec, sca, var_ready, rstd_ready, h_ready = (
            sem(n) for n in ("vec", "sca", "var_ready", "rstd_ready", "h_ready"))
        plan = Plan(sem("product_ready"), {"vec": sem("taken_vec"), "sca": sem("taken_sca")}, {"one": ps})
        for i in range(NT):
            plan.add(("hT", i), "sca")
        for name in ("src", "dst"):
            for i in range(NT):
                plan.add((name, i), "vec")

        with nc.Block() as block:
            @block.sync
            def _(sp):
                w1 = k.dram["w1"][0:2 * D, :].rearrange("(c p) n -> p c n", p=P)
                sp.dma_start(ws[:, :, :], w1[:, 0:KF, :]).then_inc(loaded["src"], 16)
                sp.dma_start(wd[:, :, :], w1[:, KF:2 * KF, :]).then_inc(loaded["dst"], 16)
                sp.dma_start(b1[:, :], k.dram["b1"][None, :].to_broadcast([P, D])).then_inc(loaded["b1"], 16)
                sp.dma_start(w2, k.dram["w2"].rearrange("(c p) n -> p c n", p=P)).then_inc(loaded["w2"], 16)
                sp.wait_ge(zeroed, 1)
                sp.dma_start(k.dst_table[NP:NP + WIN, :], zero[:, :]).then_inc(stored, 16)
                plan.need(sp, ("src", NT - 1))
                sp.dma_start(k.src_table.rearrange("(i p) d -> p i d", p=P), tables["src"][:, :, :]).then_inc(stored, 16)
                for i in range(NT):
                    plan.need(sp, ("dst", i))
                    sp.dma_start(k.dst_table[i * P:(i + 1) * P, :], tables["dst"][:, i, :]).then_inc(stored, 16)
                sp.wait_ge(stored, 16 * (2 + NT))

            @block.scalar
            def _(act):
                act.preload_act_table_set(LOG_AND_EXP)
                own = Count(act, sca)
                act.wait_ge(var_ready, 1)
                inverse_root(act, k, own, rstd_ready)
                for i in range(NT):
                    bank = plan.take(act, ("hT", i))
                    plan.took(("hT", i), act.activation(k.hT[:, :, i * P:(i + 1) * P], cols(bank[:, :], P), ACT.Copy))

            @block.tensor
            def _(pe):
                for i in range(NT):
                    bank = plan.open(pe, ("hT", i))
                    pe.wait_ge(h_ready, i + 1)
                    plan.made(turn(pe, bank, k.h[:, i, :], k.ident[:, :]))
                for name, w in (("src", ws), ("dst", wd)):
                    pe.wait_ge(loaded[name], 16)
                    for i in range(NT):
                        bank = plan.open(pe, (name, i))
                        plan.need(pe, ("hT", i))
                        plan.made(chain(pe, bank[:, :], [(k.hT[:, c, i * P:(i + 1) * P], w[:, c, :]) for c in range(KF)]))

            @block.vector
            def _(dve):
                own = Count(dve, vec)
                dve.memset(zero[:, :], 0.0).then_inc(zeroed, 1)
                layernorm_relu(k, k.h, var_ready, rstd_ready, h_ready, own, dve)
                dve.wait_ge(loaded["b1"], 16)
                for name in ("src", "dst"):
                    if name == "dst":
                        dve.wait_ge(loaded["w2"], 16)
                        own(dve.tensor_copy(k.w2_hi[:, :, :], w2))
                        own.wait()
                        own(dve.tensor_tensor(k.w2_lo[:, :, :], w2, k.w2_hi[:, :, :].bitcast(F32), ALU.subtract))
                    for i in range(NT):
                        bank = plan.take(dve, (name, i))
                        dst = tables[name][:, i, :]
                        plan.took((name, i), dve.tensor_copy(dst, bank[:, :]) if name == "src" else
                                  dve.tensor_tensor(dst, bank[:, :], b1[:, :], ALU.add))


def edge_messages(nc, k):
    PT = 2
    EDGE = PT * P
    RING = 4
    ctx = ExitStack()
    with ctx:
        sb, pb, sem = scope(ctx, nc, "edge")
        b2, w2_hi, w2_lo = sb("b2", [P, D]), k.w2_hi, k.w2_lo
        iota_i, iota = sb("iota_i", [P, WIDE], I32), sb("iota", [P, WIDE])
        row_i, row = sb("row_i", [P, 1], I32), sb("row", [P, 1])
        USES = (MAXSWEEPS + 1) * GROUPS
        starts_f, window_node = sb("starts_f", [1, USES]), sb("window_node", [P, USES])
        terms_w = [sb(f"terms_w{a}", [P, D]) for a in range(2)]
        terms = [sb(f"terms{a}", [P, GROUP]) for a in range(2)]
        dst_row = [sb(f"dst_row{a}", [P, GROUP], I32) for a in range(2)]
        index = [sb(f"index{a}", [P, PT], I32) for a in range(RING)]
        from_rows = [sb(f"from_rows{a}", [P, PT, D]) for a in range(RING)]
        m1, z2, m2, h2 = ([sb(f"{n}{a}", [P, PT * D]) for a in range(2)] for n in ("m1", "z2", "m2", "h2"))
        h1_hi, h1_lo = ([sb(f"{n}{a}", [P, KF, EDGE], F32R) for a in range(2)] for n in ("h1_hi", "h1_lo"))
        onehot = [sb(f"onehot{a}", [P, PT, WIN]) for a in range(2)]
        ps_z1 = [pb(f"z1p{a}", [P, KF * EDGE]) for a in range(2)]
        ps_z2 = pb("z2p", [P, PT * D])
        ps_sum = [pb(f"sump{a}", [P, D]) for a in range(2)]
        S = {n: sem(n) for n in (
            "loaded_b2", "loaded_w1a", "vec", "made", "starts_ready", "starts_spread", "spread_taken",
            "index_ready", "turned", "z1_made", "terms_ready", "capped1", "e1_ready", "n1_ready", "log1_ready", "q1_ready",
            "h1_ready", "hi_ready", "lo_ready", "z2_made", "z2_ready", "capped2", "e2_ready", "n2_ready", "log2_ready",
            "q2_ready", "h2_ready", "onehot_ready", "pair_summed", "added")}
        from_loaded = [sem(f"from_loaded{a}") for a in range(RING)]
        attr_loaded, window_loaded, dst_row_loaded = (
            [sem(f"{n}{a}") for a in range(2)] for n in ("attr_loaded", "window_loaded", "dst_row_loaded"))
        mish1 = [Mish(ps_z1[a][:, :], m1[a][:, :], m1[a][:, :], m1[a][:, :]) for a in range(2)]
        mish2 = [Mish(z2[a][:, :], m2[a][:, :], m2[a][:, :], h2[a][:, :]) for a in range(2)]
        PAIRS = GROUPS * TPG // PT
        DEPTH = 4
        low, high = slice(0, EATTR), slice(EATTR, P)

        def sweeps(eng):
            return eng.value_load(k.sweeps[0:1, 0:1], min_val=0, max_val=MAXSWEEPS - 1)

        def run_steps(eng, step):
            n = sweeps(eng)
            for a in range(DEPTH):
                step(lambda add: a + add, lambda lag: (a - lag) // 2, a, lambda lag: lag <= a)
            with eng.Fori(0, n * (PAIRS // 4) + (PAIRS - DEPTH) // 4) as t:
                for a in range(4):
                    step(lambda add: t * 4 + (a + DEPTH + add), lambda lag: t * 2 + (a + DEPTH - lag) // 2, a,
                         lambda lag: True)
            for a in range(DEPTH):
                step(lambda add: n * PAIRS + (PAIRS + a + add), lambda lag: n * GROUPS + (GROUPS + (a - lag) // 2), a,
                     lambda lag: lag > a)

        with nc.Block() as block:
            @block.sync
            def _(sp):
                sp.dma_start(b2[:, :], k.dram["b2"][None, :].to_broadcast([P, D])).then_inc(S["loaded_b2"], 16)
                for a in range(2):
                    sp.dma_start(terms_w[a][low, :], k.dram["w1"][2 * D:2 * D + EATTR, :]).then_inc(S["loaded_w1a"], 16)

                def step(s, g, a, on):
                    if a % 2 == 0 and on(0):
                        slot, u = a // 2, g(0)
                        o = u % GROUPS
                        if on(4):
                            sp.wait_ge(S["terms_ready"], g(2))
                        sp.dma_start(dst_row[slot][high, :], k.dram["dst_rows"][bass.ds(o, 1)].to_broadcast([WIN, GROUP])
                                     ).then_inc(dst_row_loaded[slot], 16)
                        if on(4):
                            sp.wait_ge(S["z1_made"], s(-2))
                        start = sp.value_load(k.starts[0:1, bass.ds(u, 1)], min_val=0, max_val=NP)
                        sp.dma_start(terms_w[slot][high, :], k.dst_table[bass.ds(start, WIN), :]).then_inc(window_loaded[slot], 16)
                        sp.dma_start(terms[slot][low, :], k.dram["attr_T"][:, bass.ds(o * GROUP, GROUP)]
                                     ).then_inc(attr_loaded[slot], 16)

                run_steps(sp, step)
                sp.dma_start(k.w3[0], k.dram["w3"].rearrange("(c p) n -> p c n", p=P)[:, 0:KF, :]).then_inc(k.loaded_w3, 16)
                sp.dma_start(k.w3[1], k.dram["w3"].rearrange("(c p) n -> p c n", p=P)[:, KF:2 * KF, :]).then_inc(k.loaded_w3, 16)
                sp.dma_start(k.w4, k.dram["w4"].rearrange("(c p) n -> p c n", p=P)).then_inc(k.loaded_w4, 16)

            @block.gpsimd
            def _(pool):
                pool.iota(iota_i[:, :], pattern=[[1, WIDE]], base=0, channel_multiplier=0).then_inc(S["made"], 1)
                pool.iota(row_i[:, :], pattern=[[0, 1]], base=-EATTR, channel_multiplier=1).then_inc(S["made"], 1)
                pool.memset(k.aggT[:, :, :], 0.0).then_inc(S["made"], 1)

                def step(s, g, a, on):
                    if on(0):
                        if on(4):
                            pool.wait_ge(S["turned"], s(-3))
                            settle(k, pool)
                        tile0 = (s(0) % PAIRS) * PT
                        pool.tensor_copy(index[a][:, :], k.src_i[:, bass.ds(tile0, PT)]).then_inc(S["index_ready"], 1)
                        pool.wait_ge(S["index_ready"], s(1))
                        settle(k, pool)
                        for j in range(PT):
                            pool.indirect_dma_start(
                                out=from_rows[a][:, j, :], out_offset=None, in_=k.src_table,
                                in_offset=bass.IndirectOffsetOnAxis(ap=index[a][:, j:j + 1], axis=0)
                            ).then_inc(from_loaded[a], 16)
                    if on(3):
                        b = (a - 3) % 2
                        pool.wait_ge(S["hi_ready"], s(-2))
                        pool.tensor_tensor(h1_lo[b][:, :, :], cols(m1[b][:, :], EDGE), h1_hi[b][:, :, :].bitcast(F32),
                                           ALU.subtract).then_inc(S["lo_ready"], 1)

                run_steps(pool, step)

            @block.tensor
            def _(pe):
                pe.wait_ge(S["starts_ready"], 1)
                pe.matmul(ps_z2[:, 0:USES], k.ones[0:1, :], starts_f[:, :], start=True, stop=True).then_inc(S["starts_spread"], 1)
                pe.wait_ge(S["spread_taken"], 1)
                pe.wait_ge(S["loaded_w1a"], 32)

                def step(s, g, a, on):
                    b = a % 2
                    if on(0):
                        pe.wait_ge(from_loaded[a], s(0) // RING * (16 * PT) + 16 * PT)
                        if on(2):
                            pe.wait_ge(S["h1_ready"], s(-1))
                        z1 = cols(ps_z1[b][:, :], EDGE)
                        for c in range(KF):
                            for j in range(PT):
                                mm = pe.matmul(z1[:, c, j * P:(j + 1) * P], from_rows[a][:, j, c * P:(c + 1) * P],
                                               k.ident[:, :], is_transpose=True, start=(c % 2 == 0 and j == 0), stop=False)
                        mm.then_inc(S["turned"], 1)
                        slot = a // 2
                        if b == 0:
                            pe.wait_ge(attr_loaded[slot], g(0) // 2 * 16 + 16)
                            pe.wait_ge(window_loaded[slot], g(0) // 2 * 16 + 16)
                            pe.wait_ge(S["terms_ready"], g(-2))
                        for c in range(KF):
                            mm = pe.matmul(z1[:, c, :], terms_w[slot][:, c * P:(c + 1) * P],
                                           terms[slot][:, b * EDGE:(b + 1) * EDGE], start=False, stop=(c % 2 == 1))
                        mm.then_inc(S["z1_made"], 1)
                    if on(4):
                        slot = a // 2
                        pe.wait_ge(S["h2_ready"], s(-1))
                        pe.wait_ge(S["onehot_ready"], s(-3) * PT)
                        if b == 0:
                            pe.wait_ge(S["added"], g(2))
                        for c in range(KF):
                            for j in range(PT):
                                mm = pe.matmul(ps_sum[slot][:, c * WIN:(c + 1) * WIN], h2[b][:, j * D + c * P:j * D + (c + 1) * P],
                                               onehot[b][:, j, :], start=(b == 0 and c == 0 and j == 0),
                                               stop=(b == 1 and c == KF - 1 and j == PT - 1))
                        mm.then_inc(S["pair_summed"], 1)
                    if on(2):
                        pe.wait_ge(S["hi_ready"], s(-1))
                        pe.wait_ge(S["lo_ready"], s(-1))
                        if on(3):
                            pe.wait_ge(S["z2_ready"], s(-2))
                        for j in range(PT):
                            out, tile = ps_z2[:, j * D:(j + 1) * D], slice(j * P, (j + 1) * P)
                            terms2 = []
                            for c in range(KF):
                                hi, lo = h1_hi[b][:, c, tile], h1_lo[b][:, c, tile]
                                terms2 += [(hi, w2_hi[:, c, :]), (hi, w2_lo[:, c, :]), (lo, w2_hi[:, c, :])]
                            mm = chain(pe, out, terms2)
                        mm.then_inc(S["z2_made"], 1)

                run_steps(pe, step)

            @block.scalar
            def _(act):
                act.preload_act_table_set(LOG_AND_EXP)

                def step(s, g, a, on):
                    b, c = (a - 1) % 2, a % 2
                    if on(1):
                        act.wait_ge(S["capped1"], s(0))
                        mish1[b].exp(act).then_inc(S["e1_ready"], 1)
                    if on(4):
                        act.wait_ge(S["n2_ready"], s(-3))
                        mish2[c].log(act).then_inc(S["log2_ready"], 1)
                        act.wait_ge(S["log2_ready"], s(-3))
                        mish2[c].quotient(act).then_inc(S["q2_ready"], 1)
                    if on(1):
                        act.wait_ge(S["n1_ready"], s(0))
                        mish1[b].log(act).then_inc(S["log1_ready"], 1)
                        act.wait_ge(S["log1_ready"], s(0))
                        mish1[b].quotient(act).then_inc(S["q1_ready"], 1)
                    if on(3):
                        act.wait_ge(S["capped2"], s(-2))
                        mish2[b].exp(act).then_inc(S["e2_ready"], 1)
                    if on(1):
                        act.wait_ge(S["h1_ready"], s(0))
                        if on(3):
                            act.wait_ge(S["z2_made"], s(-2))
                        act.activation(h1_hi[b][:, :, :], cols(m1[b][:, :], EDGE), ACT.Copy).then_inc(S["hi_ready"], 1)

                run_steps(act, step)

            @block.vector
            def _(dve):
                own = Count(dve, S["vec"])
                dve.sem_inc(S["h2_ready"], 2)
                dve.sem_inc(S["pair_summed"], 2)
                dve.sem_inc(S["added"], 2)
                dve.tensor_copy(starts_f[:, :], k.starts[:, :]).then_inc(S["starts_ready"], 1)
                dve.wait_ge(S["made"], 3)
                own(dve.tensor_copy(iota[:, :], iota_i[:, :]))
                own(dve.tensor_copy(row[:, :], row_i[:, :]))
                own.wait()
                dve.wait_ge(S["starts_spread"], 1)
                dve.tensor_scalar(window_node[:, :], ps_z2[:, 0:USES], row[:, 0:1], None,
                                  ALU.add).then_inc(S["spread_taken"], 1)
                dve.wait_ge(S["spread_taken"], 1)
                dve.wait_ge(S["loaded_b2"], 16)

                def step(s, g, a, on):
                    b, c = (a - 1) % 2, a % 2
                    if on(1):
                        dve.wait_ge(S["z1_made"], s(0))
                        if on(3):
                            dve.wait_ge(S["lo_ready"], s(-2))
                        mish1[b].cap(dve).then_inc(S["capped1"], 1)
                    if a % 2 == 0 and on(0):
                        slot = a // 2
                        dve.wait_ge(dst_row_loaded[slot], g(0) // 2 * 16 + 16)
                        if on(4):
                            dve.wait_ge(S["z1_made"], s(-2))
                        dve.tensor_scalar(terms[slot][high, :], dst_row[slot][high, :], window_node[high, bass.ds(g(0), 1)],
                                          None, ALU.is_equal).then_inc(S["terms_ready"], 1)
                    if on(4):
                        dve.wait_ge(S["e2_ready"], s(-3))
                        mish2[c].square(dve).then_inc(S["n2_ready"], 1)
                    if on(1):
                        dve.wait_ge(S["e1_ready"], s(0))
                        mish1[b].square(dve).then_inc(S["n1_ready"], 1)
                    if on(4):
                        start = dve.value_load(k.starts[0:1, bass.ds(g(4), 1)], min_val=0, max_val=NP)
                        tile0 = (s(-4) % PAIRS) * PT
                        dve.wait_ge(S["pair_summed"], s(-3))
                        for j in range(PT):
                            dve.tensor_scalar(onehot[c][:, j, :], iota[:, bass.ds(start, WIN)],
                                              k.dst_f[:, bass.ds(tile0 + j, 1)], None,
                                              ALU.is_equal).then_inc(S["onehot_ready"], 1)
                        dve.wait_ge(S["q2_ready"], s(-3))
                        mish2[c].product(dve).then_inc(S["h2_ready"], 1)
                    if on(3):
                        dve.wait_ge(S["z2_made"], s(-2))
                        dve.tensor_tensor(cols(z2[b][:, :], D), cols(ps_z2[:, :], D),
                                          b2[:, None, :].to_broadcast([P, PT, D]), ALU.add).then_inc(S["z2_ready"], 1)
                        dve.wait_ge(S["z2_ready"], s(-2))
                        mish2[b].cap(dve).then_inc(S["capped2"], 1)
                    if on(1):
                        dve.wait_ge(S["q1_ready"], s(0))
                        mish1[b].product(dve).then_inc(S["h1_ready"], 1)
                    if on(4) and a % 2 == 1:
                        dve.wait_ge(S["pair_summed"], s(-1))
                        dve.wait_ge(S["added"], g(0))
                        into = k.aggT[:, :, bass.ds(start, WIN)]
                        dve.tensor_tensor(into, into, cols(ps_sum[a // 2][:, 0:KF * WIN], WIN), ALU.add).then_inc(S["added"], 1)

                run_steps(dve, step)


def edge_layer_nodes(nc, k):
    ctx = ExitStack()
    with ctx:
        sb, pb, sem = scope(ctx, nc, "node")
        w3, w4 = k.w3, k.w4
        b3 = sb("b3", [P, KF])
        rows = {n: sb("row_" + n, [P, D]) for n in ("b4", "gamma", "beta")}
        z, e, n_, uT = sb("z", [P, KF, NP]), sb("e", [P, KF, NP]), sb("n", [P, KF, NP]), sb("uT", [P, KF, NP])
        st, mv = sb("st", [P, NT, 6]), sb("mv", [P, NT, 2])
        ps = [pb(f"p{i}", [P, D]) for i in range(8)]
        loaded = {n: sem("loaded_" + n) for n in ("b3", "rows")}
        vec, sca, var_ready, rstd_ready, e_ready, n_ready, q_ready, u_ready, stored, x_ready = (
            sem(n) for n in ("vec", "sca", "var_ready", "rstd_ready", "e_ready", "n_ready", "q_ready", "u_ready",
                             "stored", "x_ready"))
        capped = sem("capped")
        plan = Plan(sem("product_ready"), {"vec": sem("taken_vec"), "sca": sem("taken_sca")}, {"one": ps})
        for m in range(KF):
            for f in range(2):
                plan.add(("u", m, f), "sca")
        for i in range(NT):
            plan.add(("w4", i), "vec")
        parts = [Mish(z[:, m, :], e[:, m, :], n_[:, m, :], uT[:, m, :]) for m in range(KF)]

        with nc.Block() as block:
            @block.sync
            def _(sp):
                sp.dma_start(b3[:, :], k.dram["b3_cols"]).then_inc(loaded["b3"], 16)
                for n, src in (("b4", k.dram["b4"]), ("gamma", k.dram["gamma"]), ("beta", k.dram["beta"])):
                    sp.dma_start(rows[n][:, :], src[None, :].to_broadcast([P, D])).then_inc(loaded["rows"], 16)
                for i in range(NT):
                    sp.wait_ge(x_ready, i + 1)
                    sp.dma_start(k.dram["out"][i * P:(i + 1) * P, :], k.x[:, i, :]).then_inc(stored, 16)
                sp.wait_ge(stored, 16 * NT)

            @block.tensor
            def _(pe):
                pe.wait_ge(k.loaded_w3, 16 * 2)
                for m in range(KF):
                    for f in range(2):
                        bank = plan.open(pe, ("u", m, f))
                        half = slice(f * HALF, (f + 1) * HALF)
                        plan.made(chain(pe, bank[:, 0:HALF],
                                        [(w3[0][:, c, m * P:(m + 1) * P], k.hT[:, c, half]) for c in range(KF)] +
                                        [(w3[1][:, c, m * P:(m + 1) * P], k.aggT[:, c, half]) for c in range(KF)]))
                pe.wait_ge(k.loaded_w4, 16)
                pe.wait_ge(u_ready, KF)
                for i in range(NT):
                    bank = plan.open(pe, ("w4", i))
                    plan.made(chain(pe, bank[:, :], [(uT[:, c, i * P:(i + 1) * P], w4[:, c, :]) for c in range(KF)]))

            @block.scalar
            def _(act):
                act.preload_act_table_set(LOG_AND_EXP)
                own = Count(act, sca)
                act.wait_ge(loaded["b3"], 16)
                for m in range(KF):
                    for f in range(2):
                        bank = plan.take(act, ("u", m, f))
                        plan.took(("u", m, f), act.activation(z[:, m, f * HALF:(f + 1) * HALF], bank[:, 0:HALF],
                                                              ACT.Identity, bias=b3[:, m:m + 1]))
                    act.wait_ge(capped, m + 1)
                    parts[m].exp(act).then_inc(e_ready, 1)
                    act.wait_ge(n_ready, m + 1)
                    own(parts[m].log(act))
                    own.wait()
                    parts[m].quotient(act).then_inc(q_ready, 1)
                act.wait_ge(var_ready, 1)
                inverse_root(act, k, own, rstd_ready)

            @block.vector
            def _(dve):
                own = Count(dve, vec)
                dve.wait_ge(loaded["rows"], 16 * 3)
                for i in range(NT):
                    own(dve.tensor_tensor(k.h[:, i, :], k.h[:, i, :], rows["b4"][:, :], ALU.add))
                    own(dve.tensor_tensor(k.x[:, i, :], k.x[:, i, :], rows["beta"][:, :], ALU.add))
                for m in range(KF):
                    plan.need(dve, ("u", m, 1))
                    parts[m].cap(dve).then_inc(capped, 1)
                    dve.wait_ge(e_ready, m + 1)
                    parts[m].square(dve).then_inc(n_ready, 1)
                    dve.wait_ge(q_ready, m + 1)
                    parts[m].product(dve).then_inc(u_ready, 1)
                own.wait()
                for i in range(NT):
                    bank = plan.take(dve, ("w4", i))
                    plan.took(("w4", i), dve.tensor_tensor(k.h[:, i, :], k.h[:, i, :], bank[:, :], ALU.add))
                    plan.need(dve, ("w4", i))
                    own(dve.bn_stats(st[:, i, :], k.h[:, i, :]))
                own.wait()
                for i in range(NT):
                    own(dve.bn_aggr(mv[:, i, :], st[:, i, :]))
                own.wait()
                dve.tensor_scalar(k.rstd[:, :], mv[:, :, 1], EPS, None, ALU.add).then_inc(var_ready, 1)
                for i in range(NT):
                    own(dve.scalar_tensor_tensor(k.h[:, i, :], k.h[:, i, :], mv[:, i, 0:1], rows["gamma"][:, :],
                                                 ALU.subtract, ALU.mult))
                dve.wait_ge(rstd_ready, 1)
                own.wait()
                for i in range(NT):
                    dve.scalar_tensor_tensor(k.x[:, i, :], k.h[:, i, :], k.rstd[:, i:i + 1], k.x[:, i, :],
                                             ALU.mult, ALU.add).then_inc(x_ready, 1)


def write_rows(nc, k):
    with nc.semaphore("stored") as stored, nc.Block() as block:
        @block.sync
        def _(sp):
            sp.dma_start(k.dram["out"].rearrange("(i p) d -> p i d", p=P), k.x[:, :, :]).then_inc(stored, 16)
            sp.wait_ge(stored, 16)


STAGES = 5


def build(nc, a, out):
    k = Kernel(dict(a, out=out))
    ctx = ExitStack()
    with ctx:
        sb = lambda name, shape, dt=F32: ctx.enter_context(nc.sbuf_tensor(name, shape, dt))
        k.x, k.C, k.W, k.logc = sb("x", [P, NT, D]), sb("C", [P, NT, NP]), sb("W", [P, NT, NP]), sb("logc", [P, NT, NP])
        k.ident, k.ones, k.rstd = sb("ident", [P, P]), sb("ones", [P, P]), sb("rstd", [P, NT])
        k.st, k.mv = sb("st", [P, NT, 6]), sb("mv", [P, NT, 2])
        k.has, k.dis, k.rdeg = sb("has", [P, NT]), sb("dis", [P, NT]), sb("rdeg", [P, NT])
        k.dst_f, k.src_i = sb("dst_f", [P, TILES]), sb("src_i", [P, TILES], I32)
        k.starts, k.sweeps = sb("starts", [1, (MAXSWEEPS + 1) * GROUPS], I32), sb("sweeps", [1, 1], I32)
        k.settled = ctx.enter_context(nc.semaphore("settled"))
        k.condT = sb("condT", [CROWS, NP], F32R)
        condition(nc, k)
        edge_windows_and_matrices(nc, k)
        sage_layer(nc, k)
        if STAGES > 2:
            transformer_layer(nc, k)
        if STAGES > 3:
            gcn_layer(nc, k)
        if STAGES < 5:
            write_rows(nc, k)
            return
        k.h, k.hT, k.aggT = sb("h", [P, NT, D]), sb("hT", [P, KF, NP]), sb("aggT", [P, KF, WIDE])
        k.src_table = nc.dram_tensor("src_table", (NP, D), F32, kind="Internal").ap()
        k.dst_table = nc.dram_tensor("dst_table", (NP + WIN, D), F32, kind="Internal").ap()
        k.w2_hi, k.w2_lo = sb("w2_hi", [P, KF, D], F32R), sb("w2_lo", [P, KF, D], F32R)
        k.w3, k.w4 = (rows_of(k.W, KF), rows_of(k.logc, KF)), rows_of(k.C, KF)
        k.loaded_w3, k.loaded_w4 = (ctx.enter_context(nc.semaphore(n)) for n in ("loaded_w3", "loaded_w4"))
        edge_layer_tables(nc, k)
        edge_messages(nc, k)
        edge_layer_nodes(nc, k)


def kernel(**inputs):
    import numpy as np
    import concourse.bacc as bacc
    from concourse.bass_utils import run_bass_kernel_spmd as run

    v = {n: np.asarray(a) for n, a in inputs.items()}
    pad, pad_nodes = TILES * P - EDGES, NP - NODES

    def edges(a, fill):
        a = np.concatenate([a, np.full((pad,) + a.shape[1:], fill, a.dtype)])
        return np.ascontiguousarray(np.moveaxis(a.reshape((GROUPS, P, TPG) + a.shape[1:]), 1, 0)).reshape(P, -1)

    dst = v["dst"]
    host = {
        "x_in": np.concatenate([v["x"], np.zeros((NP - NODES, D), np.float32)]),
        "dst_rows": np.concatenate([dst, np.broadcast_to(dst[-1:], (pad,))]).reshape(
            GROUPS, P, TPG).transpose(0, 2, 1).reshape(GROUPS, GROUP),
        "dst_mark": edges(dst, -1),
        "src_tiles": edges(v["src"], 0),
        "attr3_tiles": edges(v["edge_attr_3"], 0),
        "conf_rows": np.broadcast_to(np.concatenate([v["L2_gnn_conf_w"][0], v["L2_gnn_conf_b"]]), (P, 4)),
        "w_l": v["L0_gnn_W_l"].T, "w_r": v["L0_gnn_W_r"].T, "b_l": v["L0_gnn_b_l"],
    }
    noise = np.concatenate([v["node_vec1"][:, 0], np.zeros(pad_nodes, np.float32)])
    host["noise_rows"] = np.broadcast_to(noise, (EMB, NP))
    freqs = np.arange(1, EMB // 2 + 1, dtype=np.float32) * np.float32(2.0 * np.pi / 16)
    quarter = np.repeat(np.array([0.0, 0.25], np.float32), EMB // 2)
    host["angle_consts"] = np.stack([np.tile(freqs, 2), quarter, (quarter * np.float32(2 * np.pi)).astype(np.float32)], 1)
    t = {n[7:]: a for n, a in v.items() if n.startswith("L1_gnn_")}
    f_w2, f_b2 = np.zeros((COND, 3, PART), np.float32), np.zeros((3, PART), np.float32)
    f_w2[:, :, 0:COND], f_b2[:, 0:COND], f_b2[:, COND] = t["f_w2"][:, None], t["f_b2"], 1.0
    host.update(f_w1=t["f_w1"], f_w2=f_w2.reshape(COND, CROWS), f_b1=t["f_b1"][:, None], f_b2=f_b2.reshape(CROWS, 1))
    host.update(wq=t["wq"], wk=t["wk"], wv=t["wv"], wo=t["wo"], m1=t["m_w1"], m2=t["m_w2"],
                bv=t["bv"], bo=t["bo"], mb2=t["m_b2"])
    cond_w = np.zeros((BLOCKS, 3, PART, 4, D), np.float32)
    for n, (ws, bs) in enumerate((("s1_w", "s1_b"), ("b1_w", "b1_b"), ("s2_w", "s2_b"), ("b2_w", "b2_b"))):
        cond_w[:, :, 0:COND, n], cond_w[:, :, COND, n] = t[ws][:, None], t[bs][:, None]
    host["cond_w"] = cond_w.reshape(BLOCKS, CROWS, 4, D)
    host["col_biases"] = np.stack([t["bq"], t["bk"], t["m_b1"]], 1).reshape(BLOCKS, 3, KF, P).transpose(3, 0, 1, 2).reshape(P, -1)
    t = {n[7:]: a for n, a in v.items() if n.startswith("L3_gnn_")}
    host.update(lin_w=v["L2_gnn_lin_w"].T, lin_b=v["L2_gnn_lin_b"], w1=t["W1"], w2=t["W2"], w3=t["W3"], w4=t["W4"],
                b1=t["b1"], b2=t["b2"], b4=t["b4"], gamma=t["gamma"], beta=t["beta"],
                b3_cols=t["b3"].reshape(KF, P).T)
    attr = edges(v["edge_attr_64"], 0).reshape(P, TILES, EATTR)
    host["attr_T"] = attr.transpose(2, 1, 0).reshape(EATTR, TILES * P)
    nc = bacc.Bacc("TRN2", target_bir_lowering=False, num_devices=1)
    arrays, args = {}, {}
    for name, a in host.items():
        a = np.ascontiguousarray(a)
        arrays["in_" + name] = a
        args[name] = nc.dram_tensor("in_" + name, a.shape, mybir.dt.from_np(a.dtype), kind="ExternalInput").ap()
    out = nc.dram_tensor("out_0", (NP, D), F32, kind="ExternalOutput").ap()
    build(nc, args, out)
    r = run(nc, [arrays], core_ids=[0])
    return r.results[0]["out_0"][:NODES]
```
